# Optimizing a Trainium2 kernel written in Bass

```python
import numpy as np
import jax
import jax.numpy as jnp

def _softmax(x, axis=-1):
    return jax.nn.softmax(x, axis=axis)

def _gelu(x):
    return jax.nn.gelu(x, approximate=True)

def _silu(x):
    return jax.nn.silu(x)

def _sigmoid(x):
    return jax.nn.sigmoid(x)

def _layernorm(x, axis=-1, eps=1e-05):
    m = jnp.mean(x, axis=axis, keepdims=True)
    v = jnp.var(x, axis=axis, keepdims=True)
    return (x - m) / jnp.sqrt(v + eps)

def _scatter_add(tgt, idx, src, axis=0):
    return tgt.at[idx].add(src)

def _segment_sum(src, seg, n):
    return jax.ops.segment_sum(src, seg, n)
kernel_name = 'mk_decoder_postln_d1_seqx_r8_f6d164'

def setup_inputs(seed: int=0):
    np.random.seed(seed)
    _w = jnp.asarray

    def _rec_inputs():
        import jax
        import jax.numpy as jnp
        _rk = jax.random.key(seed)
        x = 7.22e-05 + 1 * jax.random.normal(jax.random.fold_in(_rk, 1), (64, 64, 128), jnp.float32)
        _lenS = 64 - jax.random.randint(jax.random.fold_in(_rk, 7), (64,), 0, max(1, 64 // 4) + 1, jnp.int32)
        _lenS2 = 64 - jax.random.randint(jax.random.fold_in(_rk, 8), (64,), 0, max(1, 64 // 4) + 1, jnp.int32)
        _ctx_1024P = jax.random.normal(jax.random.fold_in(_rk, 11), (64, 16, 128), jnp.float32)
        _ctx_1024c = jax.random.dirichlet(jax.random.fold_in(_rk, 511), 0.3 * jnp.ones((16,), jnp.float32), (64, 64))
        _ctx_1024t = jnp.einsum('bsk,bkd->bsd', _ctx_1024c, _ctx_1024P)
        _ctx_1024t = _ctx_1024t * jax.lax.rsqrt(jnp.mean(jnp.square(_ctx_1024t)) + 1e-12) * 0.953939
        ctx_1024 = 4.13588e-05 + 0.999923 * (_ctx_1024t + 0.3 * jax.random.normal(jax.random.fold_in(_rk, 611), (64, 64, 128), jnp.float32))
        return (x, ctx_1024)
    x, ctx_1024 = _rec_inputs()

    def _L0_attn_setup():
        import math
        import jax, jax.numpy as jnp
        import numpy as np
        B, T, D_MODEL, N_HEADS = (2, 256, 128, 16)
        HEAD_DIM = D_MODEL // N_HEADS

        def _alibi_slopes(n_heads: int) -> np.ndarray:

            def pow2(n):
                start = 2.0 ** (-(8.0 / n))
                return [start * start ** i for i in range(n)]
            if math.log2(n_heads).is_integer():
                s = pow2(n_heads)
            else:
                cp = 2 ** math.floor(math.log2(n_heads))
                base = pow2(cp)
                extra = pow2(2 * cp)[1::2]
                s = base + extra[:n_heads - cp]
            return np.asarray(s, dtype=np.float32)
        SLOPES = jnp.asarray(_alibi_slopes(N_HEADS))
        key = jax.random.key(seed)
        k1, k2, k3 = jax.random.split(key, 3)
        x = jax.random.normal(k1, (B, T, D_MODEL), dtype=jnp.float32)
        Wqkv = jax.random.normal(k2, (D_MODEL, 3 * D_MODEL), dtype=jnp.float32) * 0.02
        Wout = jax.random.normal(k3, (D_MODEL, D_MODEL), dtype=jnp.float32) * 0.02
        return {'x': x, 'Wqkv': Wqkv, 'Wout': Wout}
    _L0_attn_all = _L0_attn_setup()
    _L0_attn_in = {k: v for k, v in _L0_attn_all.items() if k in ('Wqkv', 'Wout')}
    del _L0_attn_all

    def _L0_xattn_setup():
        import jax, jax.numpy as jnp
        import numpy as np
        D_K = 128
        HEADS = 16
        HK = 64
        HV = 64
        key = jax.random.key(seed)
        ks = jax.random.split(key, 12)
        B, S = (4, 256)
        sc_in = 1.0 / np.sqrt(D_K)
        sc_u = 1.0 / np.sqrt(HV * HEADS)
        return {'q': jax.random.normal(ks[0], (B, S, D_K), jnp.float32), 'k': jax.random.normal(ks[1], (B, S, D_K), jnp.float32), 'v': jax.random.normal(ks[2], (B, S, D_K), jnp.float32), 'Wq': jax.random.normal(ks[3], (D_K, HK * HEADS), jnp.float32) * sc_in, 'bq': jax.random.normal(ks[4], (HK * HEADS,), jnp.float32) * sc_in, 'Wk': jax.random.normal(ks[5], (D_K, HK * HEADS), jnp.float32) * sc_in, 'bk': jax.random.normal(ks[6], (HK * HEADS,), jnp.float32) * sc_in, 'Wv': jax.random.normal(ks[7], (D_K, HV * HEADS), jnp.float32) * sc_in, 'bv': jax.random.normal(ks[8], (HV * HEADS,), jnp.float32) * sc_in, 'Wu': jax.random.normal(ks[9], (HV * HEADS, D_K), jnp.float32) * sc_u, 'bu': jax.random.normal(ks[10], (D_K,), jnp.float32) * sc_u}
    _L0_xattn_all = _L0_xattn_setup()
    _L0_xattn_in = {k: v for k, v in _L0_xattn_all.items() if k in ('Wq', 'bq', 'Wk', 'bk', 'Wv', 'bv', 'Wu', 'bu')}
    del _L0_xattn_all

    def _L0_ffn_setup():
        import jax, jax.numpy as jnp
        import numpy as np
        D_MODEL, FF_DIM = (128, 256)
        N_SHARED, N_ROUTED, TOP_K = (1, 8, 2)
        BATCH, SEQ = (2, 256)
        key = jax.random.key(seed)
        ks = jax.random.split(key, 8)
        init = lambda k, shape: jax.random.normal(k, shape, jnp.float32) * 0.02
        x = jax.random.normal(ks[0], (BATCH, SEQ, D_MODEL), jnp.float32)
        Wg = init(ks[1], (D_MODEL, N_ROUTED))
        Ws1 = init(ks[2], (D_MODEL, FF_DIM))
        Ws3 = init(ks[3], (D_MODEL, FF_DIM))
        Ws2 = init(ks[4], (FF_DIM, D_MODEL))
        We1 = init(ks[5], (N_ROUTED, D_MODEL, FF_DIM))
        We3 = init(ks[6], (N_ROUTED, D_MODEL, FF_DIM))
        We2 = init(ks[7], (N_ROUTED, FF_DIM, D_MODEL))
        return {'x': x, 'Wg': Wg, 'Ws1': Ws1, 'Ws3': Ws3, 'Ws2': Ws2, 'We1': We1, 'We3': We3, 'We2': We2}
    _L0_ffn_all = _L0_ffn_setup()
    _L0_ffn_in = {k: v for k, v in _L0_ffn_all.items() if k in ('Wg', 'Ws1', 'Ws3', 'Ws2', 'We1', 'We3', 'We2')}
    del _L0_ffn_all
    return {'x': x, 'ctx_1024': ctx_1024, 'L0_attn_Wqkv': _L0_attn_in['Wqkv'], 'L0_attn_Wout': _L0_attn_in['Wout'], 'L0_xattn_Wq': _L0_xattn_in['Wq'], 'L0_xattn_bq': _L0_xattn_in['bq'], 'L0_xattn_Wk': _L0_xattn_in['Wk'], 'L0_xattn_bk': _L0_xattn_in['bk'], 'L0_xattn_Wv': _L0_xattn_in['Wv'], 'L0_xattn_bv': _L0_xattn_in['bv'], 'L0_xattn_Wu': _L0_xattn_in['Wu'], 'L0_xattn_bu': _L0_xattn_in['bu'], 'L0_ffn_Wg': _L0_ffn_in['Wg'], 'L0_ffn_Ws1': _L0_ffn_in['Ws1'], 'L0_ffn_Ws3': _L0_ffn_in['Ws3'], 'L0_ffn_Ws2': _L0_ffn_in['Ws2'], 'L0_ffn_We1': _L0_ffn_in['We1'], 'L0_ffn_We3': _L0_ffn_in['We3'], 'L0_ffn_We2': _L0_ffn_in['We2']}

def reference(x, ctx_1024, L0_attn_Wqkv, L0_attn_Wout, L0_xattn_Wq, L0_xattn_bq, L0_xattn_Wk, L0_xattn_bk, L0_xattn_Wv, L0_xattn_bv, L0_xattn_Wu, L0_xattn_bu, L0_ffn_Wg, L0_ffn_Ws1, L0_ffn_Ws3, L0_ffn_Ws2, L0_ffn_We1, L0_ffn_We3, L0_ffn_We2):
    import jax
    import jax.numpy as jnp

    def _L0_attn_ref(x, Wqkv, Wout):
        import math
        import jax, jax.numpy as jnp
        import numpy as np
        B, T, D_MODEL, N_HEADS = (2, 256, 128, 16)
        HEAD_DIM = D_MODEL // N_HEADS

        def _alibi_slopes(n_heads: int) -> np.ndarray:

            def pow2(n):
                start = 2.0 ** (-(8.0 / n))
                return [start * start ** i for i in range(n)]
            if math.log2(n_heads).is_integer():
                s = pow2(n_heads)
            else:
                cp = 2 ** math.floor(math.log2(n_heads))
                base = pow2(cp)
                extra = pow2(2 * cp)[1::2]
                s = base + extra[:n_heads - cp]
            return np.asarray(s, dtype=np.float32)
        SLOPES = jnp.asarray(_alibi_slopes(N_HEADS))
        Bc, Tc, Dc = x.shape
        qkv = x @ Wqkv
        q, k, v = jnp.split(qkv, 3, axis=-1)
        q = q.reshape(Bc, Tc, N_HEADS, HEAD_DIM)
        k = k.reshape(Bc, Tc, N_HEADS, HEAD_DIM)
        v = v.reshape(Bc, Tc, N_HEADS, HEAD_DIM)
        scale = 1.0 / math.sqrt(HEAD_DIM)
        logits = jnp.einsum('bihd,bjhd->bhij', q, k) * scale
        pos = jnp.arange(Tc, dtype=jnp.float32)
        rel = pos[None, :] - pos[:, None]
        logits = logits + SLOPES[None, :, None, None] * rel[None, None, :, :]
        causal = pos[:, None] >= pos[None, :]
        logits = jnp.where(causal[None, None, :, :], logits, -jnp.inf)
        attn = jax.nn.softmax(logits, axis=-1)
        out = jnp.einsum('bhij,bjhd->bihd', attn, v).reshape(Bc, Tc, Dc)
        return out @ Wout

    def _L0_xattn_ref(q, k, v, Wq, bq, Wk, bk, Wv, bv, Wu, bu):
        import jax, jax.numpy as jnp
        import numpy as np
        D_K = 128
        HEADS = 16
        HK = 64
        HV = 64
        B, S, _ = q.shape
        qh = (q @ Wq + bq).reshape(B, S, HEADS, HK).transpose(0, 2, 1, 3)
        kh = (k @ Wk + bk).reshape(B, S, HEADS, HK).transpose(0, 2, 1, 3)
        vh = (v @ Wv + bv).reshape(B, S, HEADS, HV).transpose(0, 2, 1, 3)
        scores = jnp.einsum('bhqd,bhkd->bhqk', qh, kh) / jnp.sqrt(jnp.asarray(HK, qh.dtype))
        attn = jax.nn.softmax(scores, axis=-1)
        out = jnp.einsum('bhqk,bhkd->bhqd', attn, vh)
        merged = out.transpose(0, 2, 1, 3).reshape(B, S, HEADS * HV)
        return merged @ Wu + bu

    def _L0_ffn_ref(x, Wg, Ws1, Ws3, Ws2, We1, We3, We2):
        import jax, jax.numpy as jnp
        import numpy as np
        D_MODEL, FF_DIM = (128, 256)
        N_SHARED, N_ROUTED, TOP_K = (1, 8, 2)
        BATCH, SEQ = (2, 256)
        B, S, d = x.shape
        E = Wg.shape[1]
        xf = x.reshape(-1, d)
        T = xf.shape[0]
        gates = jax.nn.sigmoid(xf @ Wg)
        vals, idx = jax.lax.top_k(gates, TOP_K)
        vals = vals / vals.sum(axis=-1, keepdims=True)
        w = jnp.zeros((T, E), x.dtype).at[jnp.arange(T)[:, None], idx].add(vals)
        shared = jax.nn.silu(xf @ Ws1) * (xf @ Ws3) @ Ws2
        h = jax.nn.silu(jnp.einsum('td,edf->tef', xf, We1)) * jnp.einsum('td,edf->tef', xf, We3)
        routed = jnp.einsum('tef,efd,te->td', h, We2, w)
        out = (shared + routed) / (N_SHARED + TOP_K)
        return out.reshape(B, S, d)
    x = _layernorm(x + _L0_attn_ref(x, L0_attn_Wqkv, L0_attn_Wout), axis=-1)
    x = _layernorm(x + _L0_xattn_ref(x, ctx_1024, ctx_1024, L0_xattn_Wq, L0_xattn_bq, L0_xattn_Wk, L0_xattn_bk, L0_xattn_Wv, L0_xattn_bv, L0_xattn_Wu, L0_xattn_bu), axis=-1)
    x = _layernorm(x + _L0_ffn_ref(x, L0_ffn_Wg, L0_ffn_Ws1, L0_ffn_Ws3, L0_ffn_Ws2, L0_ffn_We1, L0_ffn_We3, L0_ffn_We2), axis=-1)
    return x

_drawn_inputs = setup_inputs


def setup_inputs(seed=0):
    import zlib

    import numpy as np

    out = dict(_drawn_inputs(seed))
    spreads = {}
    factors = {'L0_attn_Wqkv': 3.498,
     'L0_attn_Wout': 3.474,
     'L0_xattn_bq': 3.03,
     'L0_xattn_bk': 8.0,
     'L0_ffn_Wg': 8.0,
     'L0_ffn_Ws1': 8.0,
     'L0_ffn_Ws3': 8.0,
     'L0_ffn_Ws2': 8.0,
     'L0_ffn_We1': 8.0,
     'L0_ffn_We3': 8.0,
     'L0_ffn_We2': 8.0}
    for name, (base, spread) in spreads.items():
        noise = np.random.default_rng([zlib.crc32(name.encode()), seed]).standard_normal(out[name].shape)
        drawn = base * np.exp(spread * noise) if base else spread * noise
        out[name] = jnp.asarray(drawn.astype(out[name].dtype))
    for name, factor in factors.items():
        out[name] = (out[name] * factor).astype(out[name].dtype)
    return out
```

```python
import math
from contextlib import ExitStack

import numpy as np

import concourse.bass as bass
from concourse import mybir

F32 = mybir.dt.float32
F32R = mybir.dt.float32r
I32 = mybir.dt.int32
ALU = mybir.AluOpType
ACT = mybir.ActivationFunctionType
AX = mybir.AxisListType
ds = bass.ds

P = 128
B, T, D = 64, 64, 128
PAIRS = B // 2
H = 16
HD = D // H
HK = 64
E, FF = 8, 256
EPS = 1e-5
MASKED = -1e30
SA_SCALE = 1.0 / math.sqrt(HD)
CA_SCALE = 1.0 / math.sqrt(HK)
SLOPES = [float(np.float32(2.0 ** (-8.0 * (h + 1) / H))) for h in range(H)]


def heads(ap):
    return ap.rearrange("p (h k) -> p h k", k=T)


def over_keys(ap, n=T):
    return ap.unsqueeze(2).broadcast_to((ap.shape[0], ap.shape[1], n))


def constants(nc, sem, ident, table, quad_scale, head_mask, vx, rel_i, rel, mask16):
    set_v, set_g = sem("const_dve"), sem("const_pool")
    with nc.Block() as block:

        @block.vector
        def _(dve):
            nc.vector.memset(ident[:, :], 0.0).then_inc(set_v, 1)
            nc.vector.memset(mask16[:, :], 1.0).then_inc(set_v, 1)
            nc.vector.memset(quad_scale[:, :], 0.0).then_inc(set_v, 1)
            dve.wait_ge(set_v, 3)
            for g in range(4):
                nc.vector.memset(quad_scale[32 * g:32 * g + 32, g:g + 1], SA_SCALE).then_inc(set_v, 1)
            dve.wait_ge(set_g, 2)
            nc.vector.tensor_copy(rel[:, :], rel_i[:, :]).then_inc(set_v, 1)
            dve.wait_ge(set_v, 8)
            for h in range(H):
                nc.vector.tensor_scalar(table[:, h, :], rel[:, :], SLOPES[h], None, ALU.mult).then_inc(set_v, 1)
            dve.wait_ge(set_g, 6)
            for h2 in range(2):
                nc.vector.memset(vx[64 * h2:64 * h2 + 64, :, :, :, h2, HD], 1.0).then_inc(set_v, 1)
            nc.vector.tensor_reduce(head_mask[:, :], mask16[:, :].rearrange("p (g h) -> p h g", g=4),
                                    AX.X, ALU.add).then_inc(set_v, 1)

        @block.gpsimd
        def _(pool):
            for b in range(2):
                if b:
                    pool.wait_ge(set_g, 1)
                nc.gpsimd.iota(rel_i[64 * b:64 * b + 64, :], pattern=[[1, T]], base=0,
                               channel_multiplier=-1).then_inc(set_g, 1)
            pool.wait_ge(set_v, 3)
            pool.wait_ge(set_g, 2)
            nc.gpsimd.affine_select(out=ident[:, :], in_=ident[:, :], compare_op=ALU.not_equal, fill=1.0,
                                    base=0, pattern=[[-1, P]], channel_multiplier=1).then_inc(set_g, 1)
            nc.gpsimd.affine_select(out=mask16[:, :], in_=mask16[:, :], compare_op=ALU.is_ge, fill=0.0,
                                    base=0, pattern=[[-HD, H]], channel_multiplier=1).then_inc(set_g, 1)
            pool.wait_ge(set_g, 4)
            nc.gpsimd.affine_select(out=mask16[:, :], in_=mask16[:, :], compare_op=ALU.is_ge, fill=0.0,
                                    base=HD - 1, pattern=[[HD, H]], channel_multiplier=-1).then_inc(set_g, 1)
            nc.gpsimd.memset(vx[:, :, :, :, :, :], 0.0).then_inc(set_g, 1)
            pool.wait_ge(set_v, 8 + H)
            for b in range(2):
                pool.wait_ge(set_g, 6 + b)
                part = table[64 * b:64 * b + 64, :, :]
                nc.gpsimd.affine_select(out=part, in_=part, compare_op=ALU.is_ge, fill=MASKED,
                                        base=0, pattern=[[0, H], [-1, T]], channel_multiplier=1).then_inc(set_g, 1)


def self_attention(nc, sem, sb, ps, x, w_qkv, w_out, act, stats, ident, table, quad_scale, head_mask, vx):
    wqkv = sb("sa_wqkv", [P, 3 * D])
    wout = sb("sa_wout", [P, D])
    xs = sb("sa_xs", [P, D])
    xt = sb("sa_xt", [P, 2, 2, T])
    qm = sb("sa_qm", [P, 4, P])
    km = sb("sa_km", [P, 2, 4, T])
    logit = sb("sa_logit", [P, H * T])
    under = sb("sa_under", [P, H * T])
    prob = sb("sa_prob", [P, H * T])
    top = sb("sa_top", [P, H])
    pt = sb("sa_pt", [P, H // 2, P])
    rsum = sb("sa_rsum", [P, H])
    o = sb("sa_o", [P, H, HD])
    ot = sb("sa_ot", [P, P])
    ps_x, ps_qkv, ps_s0, ps_s1, ps_p0, ps_p1, ps_av, ps_o = ps
    ps_p = (ps_p0, ps_p1)
    ps_s = (ps_s0, ps_s1)
    av = ps_av[:, 0:8 * 2 * 2 * (HD + 1)].rearrange("p (j b h d) -> p j b h d", j=8, b=2, h=2)

    w_in, x_in, x_rest = sem("sa_w_in"), sem("sa_x_in"), sem("sa_x_rest")
    FIRST = 4
    s = {n: sem("sa_" + n) for n in (
        "xs", "xt_ps", "xt", "qkv", "qm", "km", "v", "score", "logit", "top", "shift", "prob",
        "pt_ps", "pt", "av", "rsum", "o", "ot_ps", "ot", "y_ps", "y", "st")}

    def has(i, back):
        return not isinstance(i, int) or 0 <= i - back < PAIRS

    def later(i, back):
        return not isinstance(i, int) or i > back

    def pipeline(eng, body):
        for i in range(5):
            body(i)
        with eng.Fori(5, PAIRS - 1) as i:
            body(i)
        for i in range(PAIRS - 1, PAIRS + 4):
            body(i)

    with nc.Block() as block:

        @block.sync
        def _(sp):
            sp.dma_start(wqkv[:, :], w_qkv).then_inc(w_in, 16)
            sp.dma_start(wout[:, :], w_out).then_inc(w_in, 16)
            sp.dma_start(act[:, 0:FIRST, :], x[:, 0:FIRST, :]).then_inc(x_in, 16)
            sp.dma_start(act[:, FIRST:, :], x[:, FIRST:, :]).then_inc(x_rest, 16)

        @block.tensor
        def _(pe):
            pe.wait_ge(w_in, 32)

            def body(i):
                if has(i, 0):
                    pe.wait_ge(s["xs"], i + 1)
                    if later(i, 0):
                        pe.wait_ge(s["v"], i * 2)
                    nc.tensor.transpose(ps_x[:, 0:P], xs[:, :], ident[:, :]).then_inc(s["xt_ps"], 1)
                if has(i, 1):
                    pe.wait_ge(s["qm"], i)
                    pe.wait_ge(s["km"], i)
                    if later(i, 1):
                        pe.wait_ge(s["logit"], i * 2 - 2)
                    for g in range(4):
                        for b in range(2):
                            ins = nc.tensor.matmul(ps_s[g // 2][64 * b:64 * b + 64, 256 * (g % 2):256 * (g % 2) + 256],
                                                   qm[:, g, 64 * b:64 * b + 64],
                                                   km[:, b, :, :].rearrange("p h k -> p (h k)"), start=True, stop=True)
                        if g % 2:
                            ins.then_inc(s["score"], 1)
                if has(i, 4):
                    pe.wait_ge(s["o"], i * 2 - 6)
                    if later(i, 4):
                        pe.wait_ge(s["y"], i - 4)
                    nc.tensor.transpose(ps_o[:, 0:P], o[:, :, :].rearrange("p h d -> p (h d)"),
                                        ident[:, :]).then_inc(s["ot_ps"], 1)
                if has(i, 0):
                    pe.wait_ge(s["xt"], i + 1)
                    if later(i, 0):
                        pe.wait_ge(s["qm"], i)
                        pe.wait_ge(s["km"], i)
                    for n in range(2):
                        nc.tensor.matmul(ps_qkv[:, P * n:P * n + P], wqkv[:, D * n:D * n + D], xt[:, :, 0, :],
                                         start=True, stop=True)
                    for b in range(2):
                        ins = nc.tensor.matmul(ps_x[:, P * (2 + b):P * (3 + b)],
                                               xt[:, b, :, :].rearrange("p c t -> p (c t)"),
                                               wqkv[:, 2 * D:3 * D], start=True, stop=True)
                    ins.then_inc(s["qkv"], 1)
                if has(i, 3):
                    pe.wait_ge(s["v"], i * 2 - 4)
                    if later(i, 3):
                        pe.wait_ge(s["o"], i * 2 - 6)
                    for j in range(8):
                        if j % 4 == 0:
                            pe.wait_ge(s["pt"], i * 2 - 5 + j // 4)
                        ins = nc.tensor.matmul(ps_av[:, 36 * j:36 * j + 36], pt[:, j, :],
                                               vx[:, ds(i - 3, 1), j, :, :, :].rearrange("p i b h d -> p (i b h d)"),
                                               start=True, stop=True)
                    ins.then_inc(s["av"], 1)
                if has(i, 4):
                    pe.wait_ge(s["ot"], i - 3)
                    nc.tensor.matmul(ps_o[:, P:2 * P], ot[:, :], wout[:, :], start=True, stop=True).then_inc(s["y_ps"], 1)
                if has(i, 2):
                    for half in range(2):
                        pe.wait_ge(s["prob"], i * 2 - 3 + half)
                        if later(i, 2):
                            pe.wait_ge(s["pt"], i * 2 - 5 + half)
                        for j in range(4):
                            ins = nc.tensor.transpose(ps_p[half][:, P * j:P * j + P],
                                                      prob[:, P * (4 * half + j):P * (4 * half + j + 1)], ident[:, :])
                        ins.then_inc(s["pt_ps"], 1)

            pipeline(pe, body)

        @block.vector
        def _(dve):
            def copy_x(i):
                nc.vector.tensor_scalar(xs[:, :].unsqueeze(1), act[:, ds(i, 1), :], 1.0, None,
                                        ALU.mult).then_inc(s["xs"], 1)

            dve.wait_ge(x_in, 16)
            copy_x(0)

            def body(i):
                if has(i, 0) and has(i, -1):
                    dve.wait_ge(s["xt_ps"], i + 1)
                    if isinstance(i, int) and i + 1 == FIRST:
                        dve.wait_ge(x_rest, 16)
                    copy_x(i + 1)
                if has(i, 1):
                    for half in range(2):
                        dve.wait_ge(s["score"], i * 2 - 1 + half)
                        if half == 0 and later(i, 1):
                            dve.wait_ge(s["shift"], i - 1)
                        nc.vector.tensor_tensor(heads(logit[:, 512 * half:512 * half + 512]),
                                                heads(ps_s[half][:, :]), table[:, 8 * half:8 * half + 8, :],
                                                ALU.add).then_inc(s["logit"], 1)
                if has(i, 0):
                    dve.wait_ge(s["qkv"], i + 1)
                    if later(i, 0):
                        dve.wait_ge(s["score"], i * 2)
                    nc.vector.tensor_tensor(km[:, :, :, :],
                                            ps_qkv[:, P:2 * P].rearrange("p (b k) -> p b k", b=2).unsqueeze(2)
                                            .broadcast_to((P, 2, 4, T)),
                                            head_mask[:, :].unsqueeze(1).unsqueeze(3).broadcast_to((P, 2, 4, T)),
                                            ALU.mult).then_inc(s["km"], 1)
                    nc.vector.tensor_tensor(qm[:, :, :], ps_qkv[:, 0:P].unsqueeze(1).broadcast_to((P, 4, P)),
                                            over_keys(quad_scale[:, :], P), ALU.mult).then_inc(s["qm"], 1)
                if has(i, 1):
                    dve.wait_ge(s["logit"], i * 2)
                    nc.vector.tensor_reduce(top[:, :], heads(logit[:, :]), AX.X, ALU.max).then_inc(s["top"], 1)
                if has(i, 3):
                    dve.wait_ge(s["av"], i - 2)
                    for b in range(2):
                        r = slice(64 * b, 64 * b + 64)
                        nc.vector.reciprocal(rsum[r, :].rearrange("p (j h) -> p j h", h=2),
                                             av[r, :, b, :, HD]).then_inc(s["rsum"], 1)
                    for b in range(2):
                        r = slice(64 * b, 64 * b + 64)
                        dve.wait_ge(s["rsum"], i * 2 - 5 + b)
                        if b == 0 and later(i, 3):
                            dve.wait_ge(s["ot_ps"], i - 3)
                        nc.vector.tensor_tensor(
                            o[r, :, :].rearrange("p (j h) d -> p j h d", h=2), av[r, :, b, :, 0:HD],
                            rsum[r, :].rearrange("p (j h) -> p j h", h=2).unsqueeze(3).broadcast_to((64, 8, 2, HD)),
                            ALU.mult).then_inc(s["o"], 1)
                if has(i, 4):
                    dve.wait_ge(s["y_ps"], i - 3)
                    nc.vector.tensor_tensor(act[:, ds(i - 4, 1), :], act[:, ds(i - 4, 1), :],
                                            ps_o[:, P:2 * P].unsqueeze(1), ALU.add).then_inc(s["y"], 1)
                    dve.wait_ge(s["y"], i - 3)
                    nc.vector.bn_stats(stats[:, ds(i - 4, 1), :], act[:, ds(i - 4, 1), :]).then_inc(s["st"], 1)

            pipeline(dve, body)

        @block.gpsimd
        def _(pool):
            def shift(i):
                pool.wait_ge(s["top"], i + 1)
                if later(i, 0):
                    pool.wait_ge(s["prob"], i * 2)
                nc.gpsimd.tensor_tensor(heads(under[:, :]), heads(logit[:, :]), over_keys(top[:, :]),
                                        ALU.subtract).then_inc(s["shift"], 1)

            shift(0)
            with pool.Fori(1, PAIRS) as i:
                shift(i)

        @block.scalar
        def _(actv):
            actv.preload_act_table(ACT.Exp)

            def body(i):
                if has(i, 3):
                    for half in range(2):
                        actv.wait_ge(s["pt_ps"], i * 2 - 5 + half)
                        if half == 0 and later(i, 3):
                            actv.wait_ge(s["av"], i - 3)
                        nc.scalar.activation(pt[:, 4 * half:4 * half + 4, :].rearrange("p j q -> p (j q)"),
                                             ps_p[half][:, :], ACT.Copy).then_inc(s["pt"], 1)
                if has(i, 0):
                    actv.wait_ge(s["xt_ps"], i + 1)
                    if later(i, 0):
                        actv.wait_ge(s["qkv"], i)
                    nc.scalar.activation(xt[:, :, :, :],
                                         ps_x[:, 0:P].rearrange("p (b t) -> p b t", b=2).unsqueeze(2)
                                         .broadcast_to((P, 2, 2, T)), ACT.Copy).then_inc(s["xt"], 1)
                if has(i, 2):
                    actv.wait_ge(s["shift"], i - 1)
                    if later(i, 2):
                        actv.wait_ge(s["pt_ps"], i * 2 - 4)
                    for half in range(2):
                        part = slice(512 * half, 512 * half + 512)
                        nc.scalar.activation(prob[:, part], under[:, part], ACT.Exp).then_inc(s["prob"], 1)
                if has(i, 4):
                    actv.wait_ge(s["ot_ps"], i - 3)
                    if later(i, 4):
                        actv.wait_ge(s["y_ps"], i - 4)
                    nc.scalar.activation(ot[:, :], ps_o[:, 0:P], ACT.Copy).then_inc(s["ot"], 1)
                if has(i, 0):
                    actv.wait_ge(s["qkv"], i + 1)
                    for h2 in range(2):
                        r = slice(64 * h2, 64 * h2 + 64)
                        nc.scalar.activation(
                            vx[r, ds(i, 1), :, :, h2, 0:HD],
                            ps_x[r, 2 * P:4 * P].rearrange("p (b j h d) -> p j b h d", b=2, j=8, h=2)[:, :, :, h2, :]
                            .unsqueeze(1), ACT.Copy).then_inc(s["v"], 1)

            pipeline(actv, body)


def inverse_std(nc, sem, name, stats, mean, var, rstd, power):
    v, g = sem(name + "_var"), sem(name + "_rstd")
    even, odd = stats[:, :, 1], stats[:, :, 4]
    with nc.Block() as block:

        @block.vector
        def _(dve):
            nc.vector.tensor_tensor(mean[:, :], even, odd, ALU.add).then_inc(v, 1)
            nc.vector.tensor_tensor(rstd[:, :], even, odd, ALU.subtract).then_inc(v, 1)
            nc.vector.tensor_tensor(var[:, :], stats[:, :, 2], stats[:, :, 5], ALU.add).then_inc(v, 1)
            dve.wait_ge(v, 3)
            nc.vector.tensor_scalar(mean[:, :], mean[:, :], 0.5, None, ALU.mult).then_inc(v, 1)
            nc.vector.tensor_tensor(rstd[:, :], rstd[:, :], rstd[:, :], ALU.mult).then_inc(v, 1)
            nc.vector.tensor_scalar(var[:, :], var[:, :], 1.0 / D, EPS, ALU.mult, ALU.add).then_inc(v, 1)
            dve.wait_ge(v, 6)
            nc.vector.scalar_tensor_tensor(out=var[:, :], in0=rstd[:, :], scalar=0.25, in1=var[:, :],
                                           op0=ALU.mult, op1=ALU.add).then_inc(v, 1)

        @block.gpsimd
        def _(pool):
            pool.wait_ge(v, 7)
            nc.gpsimd.tensor_tensor(rstd[:, :], var[:, :], power[:, :], ALU.pow).then_inc(g, 1)


def absorb_weights(nc, sem, sb, ps, w, ident, a_hi, a_lo, b_vec, n_hi, n_lo, y_bias):
    raw = [sb(f"ab_raw{n}", [P, H * HK]) for n in range(3)]
    tr = [sb(f"ab_tr{n}", [P, H // 2, P]) for n in range(3)]
    wu = sb("ab_wu", [P, H // 2, D])
    bq, bk, bv = (sb("ab_" + n, [P, H // 2]) for n in ("bq", "bk", "bv"))
    bu = sb("ab_bu", [P, 1])
    corr = sb("ab_corr", [P, H // 2])
    w_in, b_in = [sem(f"ab_w_in{n}") for n in range(4)], sem("ab_b_in")
    tr_ps, tr_act, tr_dve, corr_d, wq_ok = (sem("ab_" + n) for n in ("tr_ps", "tr_act", "tr_dve", "corr", "wq"))
    prod_ps, prod_hi, prod_lo, vec_ps, vec_ok = (sem("ab_" + n) for n in ("prod_ps", "hi", "lo", "vec_ps", "vec"))

    fills = [(n, h2, 4 * half) for n in range(2) for half in range(2) for h2 in range(2)]

    def dest(pair, h2, j0):
        return pair[:, :, :].rearrange("c (j h) e -> c j h e", h=2)[:, j0:j0 + 4, h2, :]

    with nc.Block() as block:

        @block.sync
        def _(sp):
            for n, name in enumerate(("Wq", "Wk", "Wv")):
                sp.dma_start(raw[n][:, :], w[name]).then_inc(w_in[n], 16)
            sp.dma_start(wu[:, :, :], w["Wu"].rearrange("(j p) n -> p j n", p=P)).then_inc(w_in[3], 16)
            for t, name in ((bq, "bq"), (bk, "bk"), (bv, "bv")):
                sp.dma_start(t[:, :], w[name]).then_inc(b_in, 16)
            sp.dma_start(bu[:, :], w["bu"].rearrange("(p a) -> p a", a=1)).then_inc(b_in, 16)

        @block.tensor
        def _(pe):
            for f in range(6):
                if f % 2 == 0:
                    pe.wait_ge(w_in[f // 2], 16)
                if f >= 4:
                    pe.wait_ge((tr_act, tr_dve)[f % 2], (f - 4) // 2 + 1)
                for j in range(4):
                    c = P * (4 * (f % 2) + j)
                    ins = nc.tensor.transpose(ps[f % 4][:, P * j:P * j + P], raw[f // 2][:, c:c + P], ident[:, :])
                ins.then_inc(tr_ps, 1)
            pe.wait_ge(w_in[3], 16)
            pe.wait_ge(wq_ok, 2)
            pe.wait_ge(tr_act, 3)
            pe.wait_ge(tr_dve, 3)
            for k, (n, h2, j0) in enumerate(fills):
                if k >= 4:
                    pe.wait_ge(prod_lo, k - 3)
                r = slice(64 * h2, 64 * h2 + 64)
                left, right = ((tr[1], tr[0]), (tr[2], wu))[n]
                for j in range(4):
                    ins = nc.tensor.matmul(ps[4 + k % 4][:, P * j:P * j + P], left[r, j0 + j, :], right[r, j0 + j, :],
                                           start=True, stop=True)
                ins.then_inc(prod_ps, 1)
            pe.wait_ge(b_in, 64)
            for h2 in range(2):
                r = slice(64 * h2, 64 * h2 + 64)
                for j in range(8):
                    nc.tensor.matmul(ps[h2][:, j:j + 1], tr[0][r, j, :], bk[r, j:j + 1], start=True, stop=True)
            for j in range(8):
                ins = nc.tensor.matmul(ps[2][:, 0:1], wu[:, j, :], bv[:, j:j + 1], start=(j == 0), stop=(j == 7))
            ins.then_inc(vec_ps, 1)

        @block.scalar
        def _(actv):
            actv.preload_act_table(ACT.Exp)
            for n in range(3):
                actv.wait_ge(tr_ps, 2 * n + 1)
                nc.scalar.activation(tr[n][:, 0:4, :].rearrange("p j e -> p (j e)"), ps[2 * n % 4][:, :],
                                     ACT.Copy).then_inc(tr_act, 1)
            for k, (n, h2, j0) in enumerate(fills):
                actv.wait_ge(prod_ps, k + 1)
                nc.scalar.activation(dest((a_hi, n_hi)[n], h2, j0), ps[4 + k % 4][:, :].rearrange("c (j e) -> c j e", j=4),
                                     ACT.Copy).then_inc(prod_hi, 1)

        @block.vector
        def _(dve):
            for n in range(3):
                dve.wait_ge(tr_ps, 2 * n + 2)
                nc.vector.tensor_copy(tr[n][:, 4:8, :].rearrange("p j e -> p (j e)"),
                                      ps[(2 * n + 1) % 4][:, :]).then_inc(tr_dve, 1)
            dve.wait_ge(tr_act, 1)
            dve.wait_ge(tr_dve, 1)
            nc.vector.tensor_reduce(corr[:, :], tr[0][:, :, :], AX.X, ALU.add).then_inc(corr_d, 1)
            dve.wait_ge(corr_d, 1)
            dve.wait_ge(b_in, 64)
            nc.vector.tensor_tensor(corr[:, :], bq[:, :], corr[:, :], ALU.subtract).then_inc(corr_d, 1)
            dve.wait_ge(corr_d, 2)
            nc.vector.tensor_scalar(corr[:, :], corr[:, :], 1.0 / D, None, ALU.mult).then_inc(corr_d, 1)
            dve.wait_ge(corr_d, 3)
            nc.vector.tensor_tensor(tr[0][:, :, :], tr[0][:, :, :], over_keys(corr[:, :], D), ALU.add).then_inc(wq_ok, 1)
            dve.wait_ge(wq_ok, 1)
            nc.vector.tensor_scalar(tr[0][:, :, :], tr[0][:, :, :], CA_SCALE, None, ALU.mult).then_inc(wq_ok, 1)
            for k, (n, h2, j0) in enumerate(fills):
                dve.wait_ge(prod_hi, k + 1)
                hi = dest((a_hi, n_hi)[n], h2, j0)
                nc.vector.tensor_tensor(dest((a_lo, n_lo)[n], h2, j0), ps[4 + k % 4][:, :].rearrange("c (j e) -> c j e", j=4),
                                        hi.bitcast(F32), ALU.subtract).then_inc(prod_lo, 1)
            dve.wait_ge(vec_ps, 1)
            for h2 in range(2):
                nc.vector.tensor_copy(b_vec[:, :].rearrange("p (j h) -> p j h", h=2)[:, :, h2],
                                      ps[h2][:, 0:8]).then_inc(vec_ok, 1)
            nc.vector.tensor_tensor(y_bias[:, :], ps[2][:, 0:1], bu[:, :], ALU.add).then_inc(vec_ok, 1)


STEPS = PAIRS // 2


def cross_attention(nc, sem, sb, ps, ctx, act, stats, mean, rstd, ident, a_hi, a_lo, b_vec, n_hi, n_lo, y_bias):
    xs = sb("ca_xs", [P, 2, D])
    cn = sb("ca_cn", [P, 2, D])
    cpad = sb("ca_cpad", [P, 4, 2, D])
    xt = sb("ca_xt", [P, 2, P])
    ct_hi, ct_lo = sb("ca_ct_hi", [P, 2 * P], F32R), sb("ca_ct_lo", [P, 2 * P], F32R)
    keys = sb("ca_keys", [P, H, 2 * P])
    prob = [sb(f"ca_prob{n}", [P, H * T]) for n in range(2)]
    top, rsum = sb("ca_top", [P, 2, H]), sb("ca_rsum", [P, 2, H])
    pts = [sb(f"ca_pt{n}", [P, H // 2, P]) for n in range(2)]
    r_hi, r_lo = sb("ca_r_hi", [P, H, 2 * P], F32R), sb("ca_r_lo", [P, H, 2 * P], F32R)
    yt = sb("ca_yt", [P, 2 * P])
    ring = (ps[0:2], ps[2:4])
    ps_s, ps_y, ps_t = ps[4:6], ps[6], ps[7]

    s = {n: sem("ca_" + n) for n in (
        "cn_in", "cpad_in", "zero", "xn", "xs", "t_ps", "xt", "ct_hi", "ct_lo", "g_ps", "g_act", "g_dve",
        "score", "top", "shift", "exp", "sum", "rsum", "norm", "pt_ps", "pt_act", "pt_dve",
        "r_ps", "r_hi", "r_lo", "y_ps", "yt", "yt_ps", "y", "st")}

    order = [("pt", 0), ("r", 0), ("r", 2), ("g", 0), ("g", 1), ("pt", 1), ("g", 2), ("g", 3), ("r", 4), ("r", 6)]

    def free(pe, which, pos, i):
        def exists(kind, i):
            return not isinstance(i, int) or (i < STEPS if kind == "g" else i >= 1) and i >= 0
        back, at = i, pos - 2
        while True:
            if at < 0:
                back, at = back - 1, at + len(order)
            if isinstance(back, int) and back < 0:
                return
            if exists(order[at][0], back):
                break
            at -= 2
        kind, n = order[at]
        if kind == "g":
            pe.wait_ge(s[("g_act", "g_dve")[which]], back * 4 + n + 1)
        elif kind == "pt":
            pe.wait_ge(s[("pt_act", "pt_dve")[which]], back * 2 - 2 + n + 1)
        else:
            pe.wait_ge(s["r_lo"], back * 8 - 8 + n + which + 1)

    def position(kind, n):
        return order.index((kind, n))

    def pipeline(eng, body):
        for i in range(3):
            body(i)
        with eng.Fori(3, STEPS - 1) as i:
            body(i)
        for i in range(STEPS - 1, STEPS + 2):
            body(i)

    def spans(i):
        if isinstance(i, int):
            return i < STEPS, 1 <= i <= STEPS, 2 <= i
        return True, True, True

    def past(i, n):
        return not isinstance(i, int) or i > n

    with nc.Block() as block:

        @block.sync
        def _(sp):
            sp.wait_ge(s["zero"], 2)

            def body(i):
                if past(i, 0):
                    sp.wait_ge(s["t_ps"], i)
                sp.dma_start(cn[:, :, :], ctx.rearrange("(i b) k d -> (b k) i d", b=2)[:, ds(i * 2, 2), :])\
                  .then_inc(s["cn_in"], 16)
                if past(i, 0):
                    sp.wait_ge(s["r_ps"], i * 8)
                for half in range(2):
                    sp.dma_start(cpad[64 * half:64 * half + 64, :, half, :],
                                 ctx.rearrange("b k d -> k b d")[:, ds(i * 4, 4), :]).then_inc(s["cpad_in"], 16)

            body(0)
            with sp.Fori(1, STEPS) as i:
                body(i)

        @block.tensor
        def _(pe):
            def transpose_in(i):
                pe.wait_ge(s["xs"], i * 2 + 2)
                pe.wait_ge(s["cn_in"], i * 16 + 16)
                if past(i, 0):
                    pe.wait_ge(s["xt"], i)
                    pe.wait_ge(s["ct_lo"], i)
                if past(i, 2):
                    pe.wait_ge(s["y"], i - 2)
                for p in range(2):
                    nc.tensor.transpose(ps_t[:, P * p:P * p + P], xs[:, p, :], ident[:, :])
                for p in range(2):
                    ins = nc.tensor.transpose(ps_t[:, P * (2 + p):P * (3 + p)], cn[:, p, :], ident[:, :])
                ins.then_inc(s["t_ps"], 1)

            def absorbed_keys(i, fills):
                if fills[0] == 0:
                    pe.wait_ge(s["ct_hi"], i + 1)
                    pe.wait_ge(s["ct_lo"], i + 1)
                for f in fills:
                    which, n = f % 2, f // 2
                    pos = position("g", n)
                    free(pe, which, pos, i)
                    for h in (2 * f, 2 * f + 1):
                        out = ring[which][pos % 2][:, 256 * (h % 2):256 * (h % 2) + 256]
                        nc.tensor.matmul(out, a_hi[:, h, :], ct_hi[:, :], start=True, stop=False)
                        nc.tensor.matmul(out, a_lo[:, h, :], ct_hi[:, :], start=False, stop=False)
                        ins = nc.tensor.matmul(out, a_hi[:, h, :], ct_lo[:, :], start=False, stop=True)
                    ins.then_inc(s["g_ps"], 1)

            def scores(i, p):
                if p == 0:
                    pe.wait_ge(s["xt"], i + 1)
                    pe.wait_ge(s["g_act"], i * 4 + 4)
                    pe.wait_ge(s["g_dve"], i * 4 + 4)
                if p or past(i, 0):
                    pe.wait_ge(s["shift"], i * 2 + p)
                for half in range(2):
                    for b in range(2):
                        c = P * p + T * b
                        ins = nc.tensor.matmul(ps_s[half][T * b:T * b + T, :], xt[:, p, T * b:T * b + T],
                                               keys[:, 8 * half:8 * half + 8, c:c + T], start=True, stop=True)
                    ins.then_inc(s["score"], 1)

            def transpose_prob(i, p):
                pe.wait_ge(s["norm"], i * 2 - 2 + p + 1)
                for which in range(2):
                    pos = position("pt", p)
                    free(pe, which, pos, i)
                    for j in range(4):
                        ins = nc.tensor.transpose(ring[which][pos % 2][:, P * j:P * j + P],
                                                  prob[p][:, P * (4 * which + j):P * (4 * which + j + 1)], ident[:, :])
                    ins.then_inc(s["pt_ps"], 1)

            def values(i, p):
                if p == 0:
                    pe.wait_ge(s["cpad_in"], i * 32)
                for n in range(4):
                    b, half, which = n // 2, n % 2, n % 2
                    pos = position("r", 4 * p + n - which)
                    free(pe, which, pos, i)
                    if n == 0:
                        pe.wait_ge(s["pt_act"], i * 2 - 2 + p + 1)
                        pe.wait_ge(s["pt_dve"], i * 2 - 2 + p + 1)
                    nc.tensor.matmul(ring[which][pos % 2][:, :], cpad[:, 2 * p + b, half, :],
                                     pts[p][:, :, T * b:T * b + T], start=True, stop=True).then_inc(s["r_ps"], 1)

            def output(i):
                pe.wait_ge(s["r_lo"], i * 8)
                if past(i, 1):
                    pe.wait_ge(s["yt"], i - 1)
                for h in range(H):
                    nc.tensor.matmul(ps_y[:, 0:2 * P], n_hi[:, h, :], r_hi[:, h, :], start=(h == 0), stop=False)
                    nc.tensor.matmul(ps_y[:, 0:2 * P], n_lo[:, h, :], r_hi[:, h, :], start=False, stop=False)
                    ins = nc.tensor.matmul(ps_y[:, 0:2 * P], n_hi[:, h, :], r_lo[:, h, :], start=False, stop=(h == H - 1))
                ins.then_inc(s["y_ps"], 1)

            def transpose_out(i):
                pe.wait_ge(s["yt"], i - 1)
                pe.wait_ge(s["xt"], i + 1 if not isinstance(i, int) else min(i + 1, STEPS))
                pe.wait_ge(s["ct_lo"], i + 1 if not isinstance(i, int) else min(i + 1, STEPS))
                if isinstance(i, int) and i >= STEPS:
                    pe.wait_ge(s["y"], i - 2)
                for p in range(2):
                    ins = nc.tensor.transpose(ps_t[:, P * p:P * p + P], yt[:, P * p:P * p + P], ident[:, :])
                ins.then_inc(s["yt_ps"], 1)

            def body(i):
                now, before, out = spans(i)
                if now:
                    transpose_in(i)
                if before:
                    transpose_prob(i, 0)
                    values(i, 0)
                if now:
                    absorbed_keys(i, range(0, 4))
                if out:
                    transpose_out(i)
                if before:
                    transpose_prob(i, 1)
                if now:
                    absorbed_keys(i, range(4, 8))
                if before:
                    values(i, 1)
                if now:
                    scores(i, 0)
                if before:
                    output(i)
                if now:
                    scores(i, 1)

            pipeline(pe, body)

        @block.vector
        def _(dve):
            def normalise(i):
                if past(i, 0):
                    dve.wait_ge(s["t_ps"], i)
                for p in range(2):
                    nc.vector.tensor_scalar(xs[:, p, :].unsqueeze(1), act[:, ds(i * 2 + p, 1), :],
                                            mean[:, ds(i * 2 + p, 1)], rstd[:, ds(i * 2 + p, 1)],
                                            ALU.subtract, ALU.mult).then_inc(s["xs"], 1)
                dve.wait_ge(s["xs"], i * 2 + 2)
                nc.vector.tensor_scalar(act[:, ds(i * 2, 2), :], xs[:, :, :], 1.0, None, ALU.mult).then_inc(s["xn"], 1)

            def softmax_in(i, p):
                for half in range(2):
                    dve.wait_ge(s["score"], i * 4 + 2 * p + half + 1)
                    nc.vector.tensor_reduce(top[:, p, 8 * half:8 * half + 8], heads(ps_s[half][:, :]), AX.X,
                                            ALU.max).then_inc(s["top"], 1)
                for half in range(2):
                    dve.wait_ge(s["top"], i * 4 + 2 * p + half + 1)
                    ins = nc.vector.tensor_tensor(heads(prob[p][:, 512 * half:512 * half + 512]),
                                                  heads(ps_s[half][:, :]),
                                                  over_keys(top[:, p, 8 * half:8 * half + 8]), ALU.subtract)
                ins.then_inc(s["shift"], 1)

            def softmax_sum(i, p):
                dve.wait_ge(s["exp"], i * 2 + p + 1)
                nc.vector.tensor_reduce(rsum[:, p, :], heads(prob[p][:, :]), AX.X, ALU.add).then_inc(s["sum"], 1)
                dve.wait_ge(s["sum"], i * 2 + p + 1)
                nc.vector.reciprocal(rsum[:, p, :], rsum[:, p, :]).then_inc(s["rsum"], 1)

            def transposed_prob(i, p):
                dve.wait_ge(s["pt_ps"], i * 4 - 4 + 2 * p + 2)
                if past(i, 1):
                    dve.wait_ge(s["r_ps"], i * 8 - 16 + 4 * p + 4)
                nc.vector.tensor_copy(pts[p][:, 4:8, :].rearrange("p j q -> p (j q)"),
                                      ring[1][position("pt", p) % 2][:, :]).then_inc(s["pt_dve"], 1)

            def values_low(i, p, ns):
                for n in ns:
                    b, half = n // 2, n % 2
                    bank = ring[half][position("r", 4 * p + n - half) % 2]
                    c = P * p + T * b
                    part = [r[:, :, c:c + T].rearrange("p (j h) q -> p j h q", h=2)[:, :, half, :] for r in (r_hi, r_lo)]
                    dve.wait_ge(s["r_hi"], i * 8 - 8 + 4 * p + n + 1)
                    nc.vector.tensor_tensor(part[1], bank[:, :].rearrange("p (j q) -> p j q", q=T),
                                            part[0].bitcast(F32), ALU.subtract).then_inc(s["r_lo"], 1)

            def keys_in(i, ns):
                for n in ns:
                    dve.wait_ge(s["g_ps"], i * 8 + 2 * n + 2)
                    if n == 0 and past(i, 0):
                        dve.wait_ge(s["score"], i * 4)
                    h = 4 * n + 2
                    nc.vector.tensor_tensor(keys[:, h:h + 2, :],
                                            ring[1][position("g", n) % 2][:, :].rearrange("p (h k) -> p h k", h=2),
                                            over_keys(b_vec[:, h:h + 2], 2 * P), ALU.add).then_inc(s["g_dve"], 1)

            nc.vector.memset(cpad[0:64, :, 1, :], 0.0).then_inc(s["zero"], 1)
            nc.vector.memset(cpad[64:128, :, 0, :], 0.0).then_inc(s["zero"], 1)
            normalise(0)

            def body(i):
                now, before, out = spans(i)
                if now:
                    dve.wait_ge(s["ct_hi"], i + 1)
                    nc.vector.tensor_tensor(ct_lo[:, :], ps_t[:, 2 * P:4 * P], ct_hi[:, :].bitcast(F32),
                                            ALU.subtract).then_inc(s["ct_lo"], 1)
                if before:
                    transposed_prob(i, 0)
                    values_low(i, 0, (0, 1))
                    softmax_sum(i - 1, 1)
                    values_low(i, 0, (2, 3))
                if now:
                    keys_in(i, (0, 1))
                if out:
                    dve.wait_ge(s["yt_ps"], i - 1)
                    nc.vector.tensor_tensor(act[:, ds(i * 2 - 4, 2), :], act[:, ds(i * 2 - 4, 2), :],
                                            ps_t[:, 0:2 * P].rearrange("p (i d) -> p i d", i=2),
                                            ALU.add).then_inc(s["y"], 1)
                if before:
                    transposed_prob(i, 1)
                if out:
                    dve.wait_ge(s["y"], i - 1)
                    for p in range(2):
                        nc.vector.bn_stats(stats[:, ds(i * 2 - 4 + p, 1), :],
                                           act[:, ds(i * 2 - 4 + p, 1), :]).then_inc(s["st"], 1)
                if now:
                    keys_in(i, (2, 3))
                if before:
                    values_low(i, 1, range(4))
                if now:
                    softmax_in(i, 0)
                    if not isinstance(i, int) or i + 1 < STEPS:
                        normalise(i + 1)
                    softmax_sum(i, 0)
                    softmax_in(i, 1)

            pipeline(dve, body)

        @block.scalar
        def _(actv):
            actv.preload_act_table(ACT.Exp)

            def exps(i, p):
                actv.wait_ge(s["shift"], i * 2 + p + 1)
                nc.scalar.activation(prob[p][:, :], prob[p][:, :], ACT.Exp).then_inc(s["exp"], 1)

            def transposed_prob(i, p):
                actv.wait_ge(s["pt_ps"], i * 4 - 4 + 2 * p + 1)
                if past(i, 1):
                    actv.wait_ge(s["r_ps"], i * 8 - 16 + 4 * p + 4)
                nc.scalar.activation(pts[p][:, 0:4, :].rearrange("p j q -> p (j q)"),
                                     ring[0][position("pt", p) % 2][:, :], ACT.Copy).then_inc(s["pt_act"], 1)

            def values_high(i, p):
                for n in range(4):
                    b, half = n // 2, n % 2
                    bank = ring[half][position("r", 4 * p + n - half) % 2]
                    c = P * p + T * b
                    actv.wait_ge(s["r_ps"], i * 8 - 8 + 4 * p + n + 1)
                    nc.scalar.activation(r_hi[:, :, c:c + T].rearrange("p (j h) q -> p j h q", h=2)[:, :, half, :],
                                         bank[:, :].rearrange("p (j q) -> p j q", q=T), ACT.Copy).then_inc(s["r_hi"], 1)

            def keys_in(i, ns):
                for n in ns:
                    actv.wait_ge(s["g_ps"], i * 8 + 2 * n + 1)
                    for h in (4 * n, 4 * n + 1):
                        ins = nc.scalar.activation(keys[:, h, :],
                                                   ring[0][position("g", n) % 2][:, 256 * (h % 2):256 * (h % 2) + 256],
                                                   ACT.Identity, bias=b_vec[:, h:h + 1])
                    ins.then_inc(s["g_act"], 1)

            def body(i):
                now, before, out = spans(i)
                if now:
                    actv.wait_ge(s["t_ps"], i + 1)
                    nc.scalar.activation(ct_hi[:, :], ps_t[:, 2 * P:4 * P], ACT.Copy).then_inc(s["ct_hi"], 1)
                if before:
                    transposed_prob(i, 0)
                    exps(i - 1, 1)
                if now:
                    if past(i, 0):
                        actv.wait_ge(s["score"], i * 4)
                    actv.wait_ge(s["ct_lo"], i + 1)
                    nc.scalar.activation(xt[:, :, :], ps_t[:, 0:2 * P].rearrange("p (i d) -> p i d", i=2),
                                         ACT.Copy, bias=1.0).then_inc(s["xt"], 1)
                if before:
                    values_high(i, 0)
                if now:
                    keys_in(i, (0, 1))
                if before:
                    transposed_prob(i, 1)
                if now:
                    keys_in(i, (2, 3))
                if before:
                    values_high(i, 1)
                if now:
                    exps(i, 0)
                if before:
                    actv.wait_ge(s["y_ps"], i)
                    if past(i, 1):
                        actv.wait_ge(s["yt_ps"], i - 1)
                    nc.scalar.activation(yt[:, :], ps_y[:, 0:2 * P], ACT.Identity,
                                         bias=y_bias[:, 0:1]).then_inc(s["yt"], 1)

            pipeline(actv, body)

        @block.gpsimd
        def _(pool):
            with pool.Fori(0, STEPS) as i:
                for p in range(2):
                    pool.wait_ge(s["rsum"], i * 2 + p + 1)
                    nc.gpsimd.tensor_tensor(heads(prob[p][:, :]), heads(prob[p][:, :]), over_keys(rsum[:, p, :]),
                                            ALU.mult).then_inc(s["norm"], 1)


TILES = 4
GROUPS = PAIRS // TILES
UNITS = (E + 1) * FF // P


def router(nc, sem, sb, ps, act, mean, rstd, ident, wg, raw, parts, x_hi, x_lo, wt_dram):
    xs = sb("ro_xs", [P, TILES, D])
    xt = sb("ro_xt", [P, TILES * P])
    logits = sb("ro_logits", [P, PAIRS, E])
    gate, sel, pick, count, rest = (sb("ro_" + n, [P, PAIRS, E]) for n in ("gate", "sel", "pick", "count", "rest"))
    keep = sb("ro_keep", [P, PAIRS, E])
    best, total = sb("ro_best", [P, PAIRS]), sb("ro_total", [P, PAIRS])
    wt = sb("ro_wt", [P, 2, P])
    ps_t, ps_l, ps_w = ps[0], ps[1], ps[2]
    s = {n: sem("ro_" + n) for n in ("xs", "xn", "t_ps", "xt", "x_hi", "x_lo", "l_ps", "logits", "exp", "chain",
                                     "wt_ps", "wt", "out", "w_hi", "w_lo", "keep")}

    with nc.Block() as block:

        @block.tensor
        def _(pe):
            def body(i):
                pe.wait_ge(s["xs"], i * TILES + TILES)
                if not isinstance(i, int):
                    pe.wait_ge(s["xt"], i)
                    pe.wait_ge(s["logits"], i)
                for t in range(TILES):
                    ins = nc.tensor.transpose(ps_t[:, P * t:P * t + P], xs[:, t, :], ident[:, :])
                ins.then_inc(s["t_ps"], 1)
                pe.wait_ge(s["xt"], i + 1)
                for t in range(TILES):
                    ins = nc.tensor.matmul(ps_l[:, E * t:E * t + E], xt[:, P * t:P * t + P], wg[:, :],
                                           start=True, stop=True)
                ins.then_inc(s["l_ps"], 1)

            body(0)
            with pe.Fori(1, GROUPS) as i:
                body(i)
            pe.wait_ge(s["wt"], 1)
            for n in range(2):
                ins = nc.tensor.transpose(ps_w[:, P * n:P * n + P],
                                          sel[:, 16 * n:16 * n + 16, :].rearrange("p t e -> p (t e)"), ident[:, :])
            ins.then_inc(s["wt_ps"], 1)

        @block.scalar
        def _(actv):
            actv.preload_act_table(ACT.Exp)

            def body(i):
                actv.wait_ge(s["t_ps"], i + 1)
                if not isinstance(i, int):
                    actv.wait_ge(s["l_ps"], i)
                    actv.wait_ge(s["x_lo"], i)
                nc.scalar.activation(xt[:, :], ps_t[:, :], ACT.Copy).then_inc(s["xt"], 1)
                actv.wait_ge(s["xt"], i + 1)
                nc.scalar.activation(x_hi[:, ds(i, 1), :], xt[:, :].unsqueeze(1), ACT.Copy).then_inc(s["x_hi"], 1)

            body(0)
            with actv.Fori(1, GROUPS) as i:
                body(i)
            actv.wait_ge(s["logits"], GROUPS)
            nc.scalar.activation(gate[:, :, :], logits[:, :, :], ACT.Exp, scale=-1.0).then_inc(s["exp"], 1)
            for r, (hi, _) in zip(raw, parts):
                nc.scalar.activation(hi, r, ACT.Copy).then_inc(s["w_hi"], 1)

        @block.vector
        def _(dve):
            def body(i):
                if not isinstance(i, int):
                    dve.wait_ge(s["t_ps"], i)
                    dve.wait_ge(s["xn"], i)
                for t in range(TILES):
                    at = ds(i * TILES + t, 1)
                    nc.vector.tensor_scalar(xs[:, t, :].unsqueeze(1), act[:, at, :], mean[:, at], rstd[:, at],
                                            ALU.subtract, ALU.mult).then_inc(s["xs"], 1)
                dve.wait_ge(s["xs"], i * TILES + TILES)
                nc.vector.tensor_scalar(act[:, ds(i * TILES, TILES), :], xs[:, :, :], 1.0, None,
                                        ALU.mult).then_inc(s["xn"], 1)
                dve.wait_ge(s["x_hi"], i + 1)
                nc.vector.tensor_tensor(x_lo[:, ds(i, 1), :], xt[:, :].unsqueeze(1),
                                        x_hi[:, ds(i, 1), :].bitcast(F32), ALU.subtract).then_inc(s["x_lo"], 1)
                dve.wait_ge(s["l_ps"], i + 1)
                nc.vector.tensor_scalar(logits[:, ds(i * TILES, TILES), :],
                                        ps_l[:, 0:E * TILES].rearrange("p (t e) -> p t e", e=E), 1.0, None,
                                        ALU.mult).then_inc(s["logits"], 1)

            body(0)
            with dve.Fori(1, GROUPS) as i:
                body(i)
            nc.vector.memset(keep[:, :, :], 1.0).then_inc(s["keep"], 1)
            dve.wait_ge(s["keep"], 1)
            nc.vector.memset(keep[:, :, 0], 0.0).then_inc(s["keep"], 1)
            dve.wait_ge(s["keep"], 2)

            done = [0]

            def then(ins):
                done[0] += 1
                ins.then_inc(s["chain"], 1)
                dve.wait_ge(s["chain"], done[0])

            def flat(ap):
                return ap[:, :, :].rearrange("p t e -> p (t e)")

            dve.wait_ge(s["exp"], 1)
            then(nc.vector.tensor_scalar(flat(gate), flat(gate), 1.0, None, ALU.add))
            then(nc.vector.reciprocal(flat(gate), flat(gate)))
            for n, (source, chosen) in enumerate(((gate, sel), (rest, pick))):
                then(nc.vector.tensor_reduce(best[:, :], source[:, :, :], AX.X, ALU.max))
                then(nc.vector.tensor_tensor(chosen[:, :, :], source[:, :, :], over_keys(best[:, :], E), ALU.is_equal))
                then(nc.vector.tensor_tensor_scan(flat(count), flat(keep), flat(chosen), 0.0, ALU.mult, ALU.add))
                then(nc.vector.scalar_tensor_tensor(out=flat(chosen), in0=flat(count), scalar=1.0, in1=flat(chosen),
                                                    op0=ALU.is_equal, op1=ALU.mult))
                if n == 0:
                    then(nc.vector.scalar_tensor_tensor(out=flat(rest), in0=flat(sel), scalar=-4.0, in1=flat(gate),
                                                        op0=ALU.mult, op1=ALU.add))
            then(nc.vector.tensor_tensor(flat(sel), flat(sel), flat(pick), ALU.add))
            then(nc.vector.tensor_tensor(flat(sel), flat(sel), flat(gate), ALU.mult))
            then(nc.vector.tensor_reduce(total[:, :], sel[:, :, :], AX.X, ALU.add))
            then(nc.vector.reciprocal(total[:, :], total[:, :]))
            nc.vector.tensor_tensor(sel[:, :, :], sel[:, :, :], over_keys(total[:, :], E), ALU.mult).then_inc(s["wt"], 1)
            for n, (r, (hi, lo)) in enumerate(zip(raw, parts)):
                dve.wait_ge(s["w_hi"], n + 1)
                nc.vector.tensor_tensor(lo, r, hi.bitcast(F32), ALU.subtract).then_inc(s["w_lo"], 1)
            dve.wait_ge(s["wt_ps"], 1)
            nc.vector.tensor_copy(wt[:, :, :], ps_w[:, 0:2 * P].rearrange("p (n k) -> p n k", n=2)).then_inc(s["wt"], 1)

        @block.sync
        def _(sp):
            sp.wait_ge(s["wt"], 2)
            for n in range(2):
                sp.dma_start(wt_dram[16 * n:16 * n + 16, :, :].rearrange("t e k -> (t e) k"), wt[:, n, :])\
                  .then_inc(s["out"], 16)
            sp.wait_ge(s["out"], 32)


def experts(nc, sem, sb, ps, act, stats, ident, w1, w3, w2, x_hi, x_lo, wt_dram):
    LAG, KEEP = 3, 6
    gated = sb("ff_gated", [P, 2, TILES * P])
    hidden = sb("ff_hidden", [P, 3, TILES * P])
    h_hi, h_lo = sb("ff_h_hi", [P, KEEP, TILES * P], F32R), sb("ff_h_lo", [P, KEEP, TILES * P], F32R)
    gates = sb("ff_gates", [P, E, TILES * P])
    yt = sb("ff_yt", [P, TILES * P])
    ps_1, ps_3, ps_y, ps_t = ps[0:2], ps[2:4], ps[4], ps[5]
    s = {n: sem("ff_" + n) for n in ("u1", "u3", "silu", "mul", "gate", "hi", "lo", "down", "y_ps", "yt", "yt_ps",
                                     "y", "st")}
    gate_in = [sem(f"ff_gate_in{e}") for e in range(E)]
    OUT_AT = 5

    def whole(pe_like, body, tail):
        body(0, True)
        with pe_like.Fori(1, GROUPS) as i:
            body(i, False)
        tail()

    with nc.Block() as block:

        @block.sync
        def _(sp):
            def load(i, e):
                src = wt_dram[ds(i * TILES, TILES), e, :].unsqueeze(0).broadcast_to((P, TILES, P))
                sp.dma_start(gates[:, e, :].rearrange("p (t k) -> p t k", t=TILES), src).then_inc(gate_in[e], 16)

            for e in range(E):
                load(0, e)
            with sp.Fori(1, GROUPS) as i:
                for e in range(E):
                    sp.wait_ge(s["gate"], i * 2 * E - 2 * E + 2 * e + 2)
                    load(i, e)

        @block.tensor
        def _(pe):
            def up(i, u):
                e, c = u // 2, u % 2
                cols = slice(FF * e + P * c, FF * e + P * c + P)
                n = i * UNITS + u
                for which, (w, bank, mark) in enumerate(((w1, ps_1[u % 2], "u1"), (w3, ps_3[u % 2], "u3"))):
                    if u >= 2 or not isinstance(i, int):
                        pe.wait_ge(s[("silu", "mul")[which]], n - 1)
                    x_h, x_l = x_hi[:, ds(i, 1), :], x_lo[:, ds(i, 1), :]
                    out = bank[:, :].unsqueeze(1)
                    nc.tensor.matmul(out, w[0][:, cols], x_h, start=True, stop=False)
                    nc.tensor.matmul(out, w[1][:, cols], x_h, start=False, stop=False)
                    nc.tensor.matmul(out, w[0][:, cols], x_l, start=False, stop=True).then_inc(s[mark], 1)

            def down(i, u, first):
                n = i * UNITS + u
                pe.wait_ge(s["lo"], n + 1)
                if u == 0 and not first:
                    pe.wait_ge(s["yt"], i)
                c = slice(D * u, D * u + D)
                k = u % KEEP
                nc.tensor.matmul(ps_y[:, :], w2[0][:, c], h_hi[:, k, :], start=(u == 0), stop=False)
                nc.tensor.matmul(ps_y[:, :], w2[1][:, c], h_hi[:, k, :], start=False, stop=False)
                ins = nc.tensor.matmul(ps_y[:, :], w2[0][:, c], h_lo[:, k, :], start=False, stop=(u == UNITS - 1))
                ins.then_inc(s["down"], 1)

            def out(count):
                pe.wait_ge(s["yt"], count)
                for t in range(TILES):
                    ins = nc.tensor.transpose(ps_t[:, P * t:P * t + P], yt[:, P * t:P * t + P], ident[:, :])
                ins.then_inc(s["yt_ps"], 1)

            def body(i, first):
                for u in range(UNITS):
                    up(i, u)
                    if u >= LAG:
                        down(i, u - LAG, first)
                    elif not first:
                        down(i - 1, u - LAG + UNITS, True)
                    if u == OUT_AT and not first:
                        out(i)

            def tail():
                for u in range(UNITS - LAG, UNITS):
                    down(GROUPS - 1, u, True)
                out(GROUPS)

            whole(pe, body, tail)

        @block.scalar
        def _(actv):
            actv.preload_act_table(ACT.Silu)

            def high(i, u):
                n = i * UNITS + u
                actv.wait_ge(s["mul"], n + 1)
                if u >= 2:
                    actv.wait_ge(s["gate"], i * 2 * E + u - 1)
                if u >= KEEP or not isinstance(i, int):
                    actv.wait_ge(s["down"], n - KEEP + 1)
                nc.scalar.activation(h_hi[:, u % KEEP, :], hidden[:, u % 3, :], ACT.Copy).then_inc(s["hi"], 1)

            def output(count):
                actv.wait_ge(s["down"], count * UNITS)
                nc.scalar.activation(yt[:, :], ps_y[:, :], ACT.Copy, scale=1.0 / 3.0).then_inc(s["yt"], 1)

            def body(i, first):
                for u in range(UNITS):
                    n = i * UNITS + u
                    actv.wait_ge(s["u1"], n + 1)
                    if u >= 2 or not first:
                        actv.wait_ge(s["mul"], n - 1)
                    nc.scalar.activation(gated[:, u % 2, :], ps_1[u % 2][:, :], ACT.Silu).then_inc(s["silu"], 1)
                    if u >= 2:
                        high(i, u - 2)
                    elif not first:
                        high(i - 1, u - 2 + UNITS)
                    if u == LAG - 1 and not first:
                        output(i)

            def tail():
                for u in range(UNITS - 2, UNITS):
                    high(GROUPS - 1, u)
                output(GROUPS)

            whole(actv, body, tail)

        @block.vector
        def _(dve):
            def low(i, u):
                n = i * UNITS + u
                dve.wait_ge(s["hi"], n + 1)
                nc.vector.tensor_tensor(h_lo[:, u % KEEP, :], hidden[:, u % 3, :], h_hi[:, u % KEEP, :].bitcast(F32),
                                        ALU.subtract).then_inc(s["lo"], 1)

            def add_out(at, count):
                dve.wait_ge(s["yt_ps"], count + 1)
                nc.vector.tensor_tensor(act[:, ds(at, TILES), :], act[:, ds(at, TILES), :],
                                        ps_t[:, :].rearrange("p (t d) -> p t d", t=TILES), ALU.add).then_inc(s["y"], 1)
                dve.wait_ge(s["y"], count + 1)
                for t in range(TILES):
                    nc.vector.bn_stats(stats[:, ds(at + t, 1), :], act[:, ds(at + t, 1), :]).then_inc(s["st"], 1)

            def body(i, first):
                for u in range(UNITS):
                    n = i * UNITS + u
                    dve.wait_ge(s["silu"], n + 1)
                    dve.wait_ge(s["u3"], n + 1)
                    if u >= 3 or not first:
                        dve.wait_ge(s["lo"], n - 2)
                    nc.vector.tensor_tensor(hidden[:, u % 3, :], gated[:, u % 2, :], ps_3[u % 2][:, :],
                                            ALU.mult).then_inc(s["mul"], 1)
                    if u >= 2:
                        low(i, u - 2)
                    elif not first:
                        low(i - 1, u - 2 + UNITS)
                    if u == OUT_AT + 1 and not first:
                        add_out(i * TILES - TILES, i - 1)

            def tail():
                for u in range(UNITS - 2, UNITS):
                    low(GROUPS - 1, u)
                add_out((GROUPS - 1) * TILES, GROUPS - 1)

            whole(dve, body, tail)

        @block.gpsimd
        def _(pool):
            with pool.Fori(0, GROUPS) as i:
                for u in range(2, UNITS):
                    e = u // 2 - 1
                    if u % 2 == 0:
                        pool.wait_ge(gate_in[e], i * 16 + 16)
                    pool.wait_ge(s["mul"], i * UNITS + u + 1)
                    nc.gpsimd.tensor_tensor(hidden[:, u % 3, :], hidden[:, u % 3, :], gates[:, e, :],
                                            ALU.mult).then_inc(s["gate"], 1)


def store(nc, sem, act, mean, rstd, out):
    norm, stored = sem("out_norm"), sem("out_stored")
    QUARTER = PAIRS // 4
    with nc.Block() as block:

        @block.vector
        def _(dve):
            for i in range(PAIRS):
                nc.vector.tensor_scalar(act[:, i, :], act[:, i, :], mean[:, i:i + 1], rstd[:, i:i + 1],
                                        ALU.subtract, ALU.mult).then_inc(norm, 1)

        @block.sync
        def _(sp):
            for q in range(4):
                sp.wait_ge(norm, QUARTER * (q + 1))
                sp.dma_start(out[:, QUARTER * q:QUARTER * (q + 1), :],
                             act[:, QUARTER * q:QUARTER * (q + 1), :]).then_inc(stored, 16)
            sp.wait_ge(stored, 64)


def decoder_layer(nc, i, out, wt_dram):
    with ExitStack() as whole:
        def allocator(ctx):
            return lambda name, shape, dt=F32: ctx.enter_context(nc.sbuf_tensor(name, shape, dt))

        def sem(name):
            return whole.enter_context(nc.semaphore(name))

        sb = allocator(whole)
        ps = [whole.enter_context(nc.psum_tensor(f"bank{n}", [P, 512], F32)) for n in range(8)]
        act = sb("act", [P, PAIRS, D])
        stats = sb("stats", [P, PAIRS, 6])
        mean, var, rstd, power = (sb(n, [P, PAIRS]) for n in ("mean", "var", "rstd", "power"))
        ident = sb("ident", [P, P])
        wg = sb("wg", [P, E])
        ff_raw = sb("ff_raw", [P, 3, (E + 1) * FF])
        by_pair = "(i b) t d -> (b t) i d"

        with ExitStack() as phase:
            sb1 = allocator(phase)
            table = sb1("table", [P, H, T])
            quad_scale, head_mask = sb1("quad_scale", [P, 4]), sb1("head_mask", [P, 4])
            vx = sb1("vx", [P, PAIRS, 8, 2, 2, HD + 1])
            rel_i, rel, mask16 = sb1("rel_i", [P, T], I32), sb1("rel", [P, T]), sb1("mask16", [P, H])
            constants(nc, sem, ident, table, quad_scale, head_mask, vx, rel_i, rel, mask16)
            self_attention(nc, sem, sb1, ps, i["x"].rearrange(by_pair, b=2), i["L0_attn_Wqkv"], i["L0_attn_Wout"],
                           act, stats, ident, table, quad_scale, head_mask, vx)

        with ExitStack() as phase:
            sb2 = allocator(phase)
            a_hi, a_lo, n_hi, n_lo = (sb2(n, [P, H, P], F32R) for n in ("a_hi", "a_lo", "n_hi", "n_lo"))
            b_vec, y_bias = sb2("b_vec", [P, H]), sb2("y_bias", [P, 1])
            load_ffn(nc, sem, power, wg, ff_raw, i)
            with ExitStack() as inner:
                absorb_weights(nc, sem, allocator(inner), ps, {n: i["L0_xattn_" + n] for n in (
                    "Wq", "Wk", "Wv", "Wu", "bq", "bk", "bv", "bu")}, ident, a_hi, a_lo, b_vec, n_hi, n_lo, y_bias)
            inverse_std(nc, sem, "ln1", stats, mean, var, rstd, power)
            cross_attention(nc, sem, sb2, ps, i["ctx_1024"], act, stats, mean, rstd, ident,
                            a_hi, a_lo, b_vec, n_hi, n_lo, y_bias)

        with ExitStack() as phase:
            sb3 = allocator(phase)
            ff_hi, ff_lo = (sb3(n, [P, 3, (E + 1) * FF], F32R) for n in ("ff_hi", "ff_lo"))
            x_hi, x_lo = (sb3(n, [P, GROUPS, TILES * P], F32R) for n in ("x_hi", "x_lo"))
            inverse_std(nc, sem, "ln2", stats, mean, var, rstd, power)
            with ExitStack() as inner:
                router(nc, sem, allocator(inner), ps, act, mean, rstd, ident, wg,
                       [ff_raw[:, n, :] for n in range(3)], [(ff_hi[:, n, :], ff_lo[:, n, :]) for n in range(3)],
                       x_hi, x_lo, wt_dram)
            w1, w3, w2 = ((ff_hi[:, n, :], ff_lo[:, n, :]) for n in range(3))
            experts(nc, sem, sb3, ps, act, stats, ident, w1, w3, w2, x_hi, x_lo, wt_dram)
            inverse_std(nc, sem, "ln3", stats, mean, var, rstd, power)
            store(nc, sem, act, mean, rstd, out.rearrange(by_pair, b=2))


def load_ffn(nc, sem, power, wg, ff_raw, i):
    loaded, filled = sem("ff_loaded"), sem("power_set")
    with nc.Block() as block:

        @block.sync
        def _(sp):
            sp.dma_start(wg[:, :], i["L0_ffn_Wg"]).then_inc(loaded, 16)
            for n, name in enumerate(("1", "3")):
                sp.dma_start(ff_raw[:, n, 0:FF], i["L0_ffn_Ws" + name]).then_inc(loaded, 16)
                sp.dma_start(ff_raw[:, n, FF:].rearrange("p (e f) -> p e f", e=E),
                             i["L0_ffn_We" + name].rearrange("e d f -> d e f")).then_inc(loaded, 16)
            sp.dma_start(ff_raw[:, 2, 0:FF].rearrange("p (c d) -> p c d", d=D),
                         i["L0_ffn_Ws2"].rearrange("(c p) d -> p c d", p=P)).then_inc(loaded, 16)
            sp.dma_start(ff_raw[:, 2, FF:].rearrange("p (u d) -> p u d", d=D),
                         i["L0_ffn_We2"].rearrange("e (c p) d -> p (e c) d", p=P)).then_inc(loaded, 16)
            sp.wait_ge(loaded, 16 * 7)

        @block.gpsimd
        def _(pool):
            nc.gpsimd.memset(power[:, :], -0.5).then_inc(filled, 1)


_INS = ["x", "ctx_1024", "L0_attn_Wqkv", "L0_attn_Wout", "L0_xattn_Wq", "L0_xattn_bq", "L0_xattn_Wk", "L0_xattn_bk",
        "L0_xattn_Wv", "L0_xattn_bv", "L0_xattn_Wu", "L0_xattn_bu", "L0_ffn_Wg", "L0_ffn_Ws1", "L0_ffn_Ws3",
        "L0_ffn_Ws2", "L0_ffn_We1", "L0_ffn_We3", "L0_ffn_We2"]


def kernel(**inputs):
    import concourse.bacc as bacc
    from concourse.bass_utils import run_bass_kernel_spmd

    nc = bacc.Bacc("TRN2", target_bir_lowering=False, num_devices=1)
    arrays, aps = {}, {}
    for name in _INS:
        a = np.asarray(inputs[name])
        if name.endswith(("bq", "bk", "bv")):
            a = a.reshape(-1, P).T
        a = np.ascontiguousarray(a)
        arrays[f"in_{name}"] = a
        aps[name] = nc.dram_tensor(f"in_{name}", a.shape, mybir.dt.from_np(a.dtype), kind="ExternalInput").ap()
    out = nc.dram_tensor("out", (B, T, D), F32, kind="ExternalOutput").ap()
    wt_dram = nc.dram_tensor("gate_weights", (PAIRS, E, P), F32, kind="Internal").ap()
    decoder_layer(nc, aps, out, wt_dram)
    result = run_bass_kernel_spmd(nc, [arrays], core_ids=[0])
    return result.results[0]["out"]
```

```python
import math
from contextlib import ExitStack

import numpy as np

import concourse.bass as bass
from concourse import mybir

F32 = mybir.dt.float32
F32R = mybir.dt.float32r
I32 = mybir.dt.int32
ALU = mybir.AluOpType
ACT = mybir.ActivationFunctionType
AX = mybir.AxisListType
ds = bass.ds

P = 128
B, T, D = 64, 64, 128
PAIRS = B // 2
H = 16
HD = D // H
HK = 64
E, FF = 8, 256
EPS = 1e-5
FIRST_PAIRS = 4
MASKED = -1e30
SA_SCALE = 1.0 / math.sqrt(HD)
CA_SCALE = 1.0 / math.sqrt(HK)
SLOPES = [float(np.float32(2.0 ** (-8.0 * (h + 1) / H))) for h in range(H)]


def heads(ap):
    return ap.rearrange("p (h k) -> p h k", k=T)


def over_keys(ap, n=T):
    return ap.unsqueeze(2).broadcast_to((ap.shape[0], ap.shape[1], n))


def constants(nc, sem, load_all, ident, table, quad_scale, head_mask, vx, rel_i, rel, mask16, power, eps, one):
    set_v, set_g = sem("const_dve"), sem("const_pool")
    ZERO_DVE = 12
    with nc.Block() as block:

        @block.sync
        def _(sp):
            load_all(sp)

        @block.vector
        def _(dve):
            nc.vector.memset(ident[:, :], 0.0).then_inc(set_v, 1)
            nc.vector.memset(mask16[:, :], 1.0).then_inc(set_v, 1)
            nc.vector.memset(quad_scale[:, :], 0.0).then_inc(set_v, 1)
            dve.wait_ge(set_v, 3)
            for g in range(4):
                nc.vector.memset(quad_scale[32 * g:32 * g + 32, g:g + 1], SA_SCALE).then_inc(set_v, 1)
            dve.wait_ge(set_g, 2)
            nc.vector.tensor_copy(rel[:, :], rel_i[:, :]).then_inc(set_v, 1)
            dve.wait_ge(set_v, 8)
            for h in range(H):
                nc.vector.tensor_scalar(table[:, h, :], rel[:, :], SLOPES[h], None, ALU.mult).then_inc(set_v, 1)
            nc.vector.memset(vx[:, 0:ZERO_DVE, :, :, :, :], 0.0).then_inc(set_v, 1)
            for t, value in ((power, -0.5), (eps, EPS), (one, 1.0)):
                nc.vector.memset(t[:, :], value).then_inc(set_v, 1)
            dve.wait_ge(set_v, 9 + H)
            dve.wait_ge(set_g, 6)
            for h2 in range(2):
                nc.vector.memset(vx[64 * h2:64 * h2 + 64, :, :, :, h2, HD], 1.0).then_inc(set_v, 1)
            nc.vector.tensor_reduce(head_mask[:, :], mask16[:, :].rearrange("p (g h) -> p h g", g=4),
                                    AX.X, ALU.add).then_inc(set_v, 1)

        @block.gpsimd
        def _(pool):
            for b in range(2):
                if b:
                    pool.wait_ge(set_g, 1)
                nc.gpsimd.iota(rel_i[64 * b:64 * b + 64, :], pattern=[[1, T]], base=0,
                               channel_multiplier=-1).then_inc(set_g, 1)
            pool.wait_ge(set_v, 3)
            pool.wait_ge(set_g, 2)
            nc.gpsimd.affine_select(out=ident[:, :], in_=ident[:, :], compare_op=ALU.not_equal, fill=1.0,
                                    base=0, pattern=[[-1, P]], channel_multiplier=1).then_inc(set_g, 1)
            nc.gpsimd.affine_select(out=mask16[:, :], in_=mask16[:, :], compare_op=ALU.is_ge, fill=0.0,
                                    base=0, pattern=[[-HD, H]], channel_multiplier=1).then_inc(set_g, 1)
            pool.wait_ge(set_g, 4)
            nc.gpsimd.affine_select(out=mask16[:, :], in_=mask16[:, :], compare_op=ALU.is_ge, fill=0.0,
                                    base=HD - 1, pattern=[[HD, H]], channel_multiplier=-1).then_inc(set_g, 1)
            nc.gpsimd.memset(vx[:, ZERO_DVE:, :, :, :, :], 0.0).then_inc(set_g, 1)
            pool.wait_ge(set_v, 8 + H)
            for b in range(2):
                pool.wait_ge(set_g, 6 + b)
                part = table[64 * b:64 * b + 64, :, :]
                nc.gpsimd.affine_select(out=part, in_=part, compare_op=ALU.is_ge, fill=MASKED,
                                        base=0, pattern=[[0, H], [-1, T]], channel_multiplier=1).then_inc(set_g, 1)


def self_attention(nc, sem, sb, ps, wqkv, wout, w_in, x_in, x_rest, act, stats, ident, table, quad_scale, head_mask, vx):
    xs = sb("sa_xs", [P, D])
    xt = sb("sa_xt", [P, 2, 2, T])
    qm = sb("sa_qm", [P, 4, P])
    km = sb("sa_km", [P, 2, 4, T])
    logit = sb("sa_logit", [P, H * T])
    under = sb("sa_under", [P, H * T])
    prob = sb("sa_prob", [P, H * T])
    top = sb("sa_top", [P, H])
    pt = sb("sa_pt", [P, H // 2, P])
    rsum = sb("sa_rsum", [P, H])
    o = sb("sa_o", [P, H, HD])
    ot = sb("sa_ot", [P, P])
    ps_x, ps_qkv, ps_s0, ps_s1, ps_p0, ps_p1, ps_av, ps_o = ps
    ps_p = (ps_p0, ps_p1)
    ps_s = (ps_s0, ps_s1)
    av = ps_av[:, 0:8 * 2 * 2 * (HD + 1)].rearrange("p (j b h d) -> p j b h d", j=8, b=2, h=2)

    s = {n: sem("sa_" + n) for n in (
        "xs", "xt_ps", "xt", "qkv", "qm", "km", "v", "score", "logit", "top", "shift", "prob",
        "pt_ps", "pt", "av", "rsum", "o", "ot_ps", "ot", "y_ps", "y", "st")}

    def has(i, back):
        return not isinstance(i, int) or 0 <= i - back < PAIRS

    def later(i, back):
        return not isinstance(i, int) or i > back

    def pipeline(eng, body):
        for i in range(5):
            body(i)
        with eng.Fori(5, PAIRS - 1) as i:
            body(i)
        for i in range(PAIRS - 1, PAIRS + 4):
            body(i)

    with nc.Block() as block:

        @block.tensor
        def _(pe):
            pe.wait_ge(w_in, 32)

            def body(i):
                if has(i, 0):
                    pe.wait_ge(s["xs"], i + 1)
                    if later(i, 0):
                        pe.wait_ge(s["v"], i * 2)
                    nc.tensor.transpose(ps_x[:, 0:P], xs[:, :], ident[:, :]).then_inc(s["xt_ps"], 1)
                if has(i, 1):
                    pe.wait_ge(s["qm"], i)
                    pe.wait_ge(s["km"], i)
                    if later(i, 1):
                        pe.wait_ge(s["logit"], i * 2 - 2)
                    for g in range(4):
                        for b in range(2):
                            ins = nc.tensor.matmul(ps_s[g // 2][64 * b:64 * b + 64, 256 * (g % 2):256 * (g % 2) + 256],
                                                   qm[:, g, 64 * b:64 * b + 64],
                                                   km[:, b, :, :].rearrange("p h k -> p (h k)"), start=True, stop=True)
                        if g % 2:
                            ins.then_inc(s["score"], 1)
                if has(i, 4):
                    pe.wait_ge(s["o"], i * 2 - 6)
                    if later(i, 4):
                        pe.wait_ge(s["y"], i - 4)
                    nc.tensor.transpose(ps_o[:, 0:P], o[:, :, :].rearrange("p h d -> p (h d)"),
                                        ident[:, :]).then_inc(s["ot_ps"], 1)
                if has(i, 0):
                    pe.wait_ge(s["xt"], i + 1)
                    if later(i, 0):
                        pe.wait_ge(s["qm"], i)
                        pe.wait_ge(s["km"], i)
                    for n in range(2):
                        nc.tensor.matmul(ps_qkv[:, P * n:P * n + P], wqkv[:, D * n:D * n + D], xt[:, :, 0, :],
                                         start=True, stop=True)
                    for b in range(2):
                        ins = nc.tensor.matmul(ps_x[:, P * (2 + b):P * (3 + b)],
                                               xt[:, b, :, :].rearrange("p c t -> p (c t)"),
                                               wqkv[:, 2 * D:3 * D], start=True, stop=True)
                    ins.then_inc(s["qkv"], 1)
                if has(i, 3):
                    pe.wait_ge(s["v"], i * 2 - 4)
                    if later(i, 3):
                        pe.wait_ge(s["o"], i * 2 - 6)
                    for j in range(8):
                        if j % 4 == 0:
                            pe.wait_ge(s["pt"], i * 2 - 5 + j // 4)
                        ins = nc.tensor.matmul(ps_av[:, 36 * j:36 * j + 36], pt[:, j, :],
                                               vx[:, ds(i - 3, 1), j, :, :, :].rearrange("p i b h d -> p (i b h d)"),
                                               start=True, stop=True)
                    ins.then_inc(s["av"], 1)
                if has(i, 4):
                    pe.wait_ge(s["ot"], i - 3)
                    nc.tensor.matmul(ps_o[:, P:2 * P], ot[:, :], wout[:, :], start=True, stop=True).then_inc(s["y_ps"], 1)
                if has(i, 2):
                    for half in range(2):
                        pe.wait_ge(s["prob"], i * 2 - 3 + half)
                        if later(i, 2):
                            pe.wait_ge(s["pt"], i * 2 - 5 + half)
                        for j in range(4):
                            ins = nc.tensor.transpose(ps_p[half][:, P * j:P * j + P],
                                                      prob[:, P * (4 * half + j):P * (4 * half + j + 1)], ident[:, :])
                        ins.then_inc(s["pt_ps"], 1)

            pipeline(pe, body)

        @block.vector
        def _(dve):
            def copy_x(i):
                nc.vector.tensor_scalar(xs[:, :].unsqueeze(1), act[:, ds(i, 1), :], 1.0, None,
                                        ALU.mult).then_inc(s["xs"], 1)

            dve.wait_ge(x_in, 16)
            copy_x(0)

            def body(i):
                if has(i, 0) and has(i, -1):
                    dve.wait_ge(s["xt_ps"], i + 1)
                    if isinstance(i, int) and i + 1 == FIRST_PAIRS:
                        dve.wait_ge(x_rest, 16)
                    copy_x(i + 1)
                if has(i, 1):
                    for half in range(2):
                        dve.wait_ge(s["score"], i * 2 - 1 + half)
                        if half == 0 and later(i, 1):
                            dve.wait_ge(s["shift"], i - 1)
                        nc.vector.tensor_tensor(heads(logit[:, 512 * half:512 * half + 512]),
                                                heads(ps_s[half][:, :]), table[:, 8 * half:8 * half + 8, :],
                                                ALU.add).then_inc(s["logit"], 1)
                if has(i, 0):
                    dve.wait_ge(s["qkv"], i + 1)
                    if later(i, 0):
                        dve.wait_ge(s["score"], i * 2)
                    nc.vector.tensor_tensor(km[:, :, :, :],
                                            ps_qkv[:, P:2 * P].rearrange("p (b k) -> p b k", b=2).unsqueeze(2)
                                            .broadcast_to((P, 2, 4, T)),
                                            head_mask[:, :].unsqueeze(1).unsqueeze(3).broadcast_to((P, 2, 4, T)),
                                            ALU.mult).then_inc(s["km"], 1)
                    nc.vector.tensor_tensor(qm[:, :, :], ps_qkv[:, 0:P].unsqueeze(1).broadcast_to((P, 4, P)),
                                            over_keys(quad_scale[:, :], P), ALU.mult).then_inc(s["qm"], 1)
                if has(i, 1):
                    dve.wait_ge(s["logit"], i * 2)
                    nc.vector.tensor_reduce(top[:, :], heads(logit[:, :]), AX.X, ALU.max).then_inc(s["top"], 1)
                if has(i, 3):
                    dve.wait_ge(s["av"], i - 2)
                    for b in range(2):
                        r = slice(64 * b, 64 * b + 64)
                        nc.vector.reciprocal(rsum[r, :].rearrange("p (j h) -> p j h", h=2),
                                             av[r, :, b, :, HD]).then_inc(s["rsum"], 1)
                    for b in range(2):
                        r = slice(64 * b, 64 * b + 64)
                        dve.wait_ge(s["rsum"], i * 2 - 5 + b)
                        if b == 0 and later(i, 3):
                            dve.wait_ge(s["ot_ps"], i - 3)
                        nc.vector.tensor_tensor(
                            o[r, :, :].rearrange("p (j h) d -> p j h d", h=2), av[r, :, b, :, 0:HD],
                            rsum[r, :].rearrange("p (j h) -> p j h", h=2).unsqueeze(3).broadcast_to((64, 8, 2, HD)),
                            ALU.mult).then_inc(s["o"], 1)
                if has(i, 4):
                    dve.wait_ge(s["y_ps"], i - 3)
                    nc.vector.tensor_tensor(act[:, ds(i - 4, 1), :], act[:, ds(i - 4, 1), :],
                                            ps_o[:, P:2 * P].unsqueeze(1), ALU.add).then_inc(s["y"], 1)
                    dve.wait_ge(s["y"], i - 3)
                    nc.vector.bn_stats(stats[:, ds(i - 4, 1), :], act[:, ds(i - 4, 1), :]).then_inc(s["st"], 1)

            pipeline(dve, body)

        @block.gpsimd
        def _(pool):
            def shift(i):
                pool.wait_ge(s["top"], i + 1)
                if later(i, 0):
                    pool.wait_ge(s["prob"], i * 2)
                nc.gpsimd.tensor_tensor(heads(under[:, :]), heads(logit[:, :]), over_keys(top[:, :]),
                                        ALU.subtract).then_inc(s["shift"], 1)

            shift(0)
            with pool.Fori(1, PAIRS) as i:
                shift(i)

        @block.scalar
        def _(actv):
            actv.preload_act_table(ACT.Exp)

            def body(i):
                if has(i, 3):
                    for half in range(2):
                        actv.wait_ge(s["pt_ps"], i * 2 - 5 + half)
                        if half == 0 and later(i, 3):
                            actv.wait_ge(s["av"], i - 3)
                        nc.scalar.activation(pt[:, 4 * half:4 * half + 4, :].rearrange("p j q -> p (j q)"),
                                             ps_p[half][:, :], ACT.Copy).then_inc(s["pt"], 1)
                if has(i, 0):
                    actv.wait_ge(s["xt_ps"], i + 1)
                    if later(i, 0):
                        actv.wait_ge(s["qkv"], i)
                    nc.scalar.activation(xt[:, :, :, :],
                                         ps_x[:, 0:P].rearrange("p (b t) -> p b t", b=2).unsqueeze(2)
                                         .broadcast_to((P, 2, 2, T)), ACT.Copy).then_inc(s["xt"], 1)
                if has(i, 2):
                    actv.wait_ge(s["shift"], i - 1)
                    if later(i, 2):
                        actv.wait_ge(s["pt_ps"], i * 2 - 4)
                    for half in range(2):
                        part = slice(512 * half, 512 * half + 512)
                        nc.scalar.activation(prob[:, part], under[:, part], ACT.Exp).then_inc(s["prob"], 1)
                if has(i, 4):
                    actv.wait_ge(s["ot_ps"], i - 3)
                    if later(i, 4):
                        actv.wait_ge(s["y_ps"], i - 4)
                    nc.scalar.activation(ot[:, :], ps_o[:, 0:P], ACT.Copy).then_inc(s["ot"], 1)
                if has(i, 0):
                    actv.wait_ge(s["qkv"], i + 1)
                    for h2 in range(2):
                        r = slice(64 * h2, 64 * h2 + 64)
                        nc.scalar.activation(
                            vx[r, ds(i, 1), :, :, h2, 0:HD],
                            ps_x[r, 2 * P:4 * P].rearrange("p (b j h d) -> p j b h d", b=2, j=8, h=2)[:, :, :, h2, :]
                            .unsqueeze(1), ACT.Copy).then_inc(s["v"], 1)

            pipeline(actv, body)


def absorb_weights(nc, sem, sb, ps, raw, wu, bq, bk, bv, bu, w_in, b_in, ident, a_hi, a_lo, b_vec, n_hi, n_lo,
                   y_bias, stats, mean, var, rstd, power, zero_cpad, first_context):
    tr = [sb(f"ab_tr{n}", [P, H // 2, P]) for n in range(3)]
    corr = sb("ab_corr", [P, H // 2])
    ln, ln_rstd = sem("ln1_var"), sem("ln1_rstd")
    even, odd = stats[:, :, 1], stats[:, :, 4]
    tr_ps, tr_act, tr_dve, corr_d, wq_ok = (sem("ab_" + n) for n in ("tr_ps", "tr_act", "tr_dve", "corr", "wq"))
    prod_ps, prod_hi, prod_lo, vec_ps, vec_ok = (sem("ab_" + n) for n in ("prod_ps", "hi", "lo", "vec_ps", "vec"))

    TURN = (0, 2, 1)
    fills = [(n, h2, 4 * half) for n in (1, 0) for half in range(2) for h2 in range(2)]

    def dest(pair, h2, j0):
        return pair[:, :, :].rearrange("c (j h) e -> c j h e", h=2)[:, j0:j0 + 4, h2, :]

    with nc.Block() as block:

        @block.sync
        def _(sp):
            first_context(sp)

        @block.gpsimd
        def _(pool):
            zero_cpad()
            pool.wait_ge(ln, 7)
            nc.gpsimd.tensor_tensor(rstd[:, :], var[:, :], power[:, :], ALU.pow).then_inc(ln_rstd, 1)

        @block.tensor
        def _(pe):
            for f in range(6):
                if f % 2 == 0:
                    pe.wait_ge(w_in[TURN[f // 2]], 16)
                if f >= 4:
                    pe.wait_ge((tr_act, tr_dve)[f % 2], (f - 4) // 2 + 1)
                for j in range(4):
                    c = P * (4 * (f % 2) + j)
                    ins = nc.tensor.transpose(ps[f % 4][:, P * j:P * j + P], raw[TURN[f // 2]][:, c:c + P],
                                              ident[:, :])
                ins.then_inc(tr_ps, 1)
            pe.wait_ge(w_in[3], 16)
            pe.wait_ge(tr_act, 2)
            pe.wait_ge(tr_dve, 2)
            for k, (n, h2, j0) in enumerate(fills):
                if k == 4:
                    pe.wait_ge(b_in, 80)
                    for j in range(8):
                        nc.tensor.matmul(ps[3][:, 0:1], wu[:, j, :], bv[:, j:j + 1], start=(j == 0), stop=(j == 7))
                    pe.wait_ge(wq_ok, 1)
                    pe.wait_ge(tr_act, 3)
                    pe.wait_ge(tr_dve, 3)
                if k >= 4:
                    pe.wait_ge(prod_lo, k - 3)
                r = slice(64 * h2, 64 * h2 + 64)
                left, right = ((tr[1], tr[0]), (tr[2], wu))[n]
                for j in range(4):
                    ins = nc.tensor.matmul(ps[4 + k % 4][:, P * j:P * j + P], left[r, j0 + j, :], right[r, j0 + j, :],
                                           start=True, stop=True)
                ins.then_inc(prod_ps, 1)
            for h2 in range(2):
                r = slice(64 * h2, 64 * h2 + 64)
                for j in range(8):
                    ins = nc.tensor.matmul(ps[h2][:, j:j + 1], tr[0][r, j, :], bk[r, j:j + 1], start=True, stop=True)
            ins.then_inc(vec_ps, 1)

        @block.scalar
        def _(actv):
            actv.preload_act_table(ACT.Exp)
            for n in range(3):
                actv.wait_ge(tr_ps, 2 * n + 1)
                nc.scalar.activation(tr[TURN[n]][:, 0:4, :].rearrange("p j e -> p (j e)"), ps[2 * n % 4][:, :],
                                     ACT.Copy).then_inc(tr_act, 1)
            for k, (n, h2, j0) in enumerate(fills):
                actv.wait_ge(prod_ps, k + 1)
                nc.scalar.activation(dest((a_hi, n_hi)[n], h2, j0), ps[4 + k % 4][:, :].rearrange("c (j e) -> c j e", j=4),
                                     ACT.Copy).then_inc(prod_hi, 1)

        @block.vector
        def _(dve):
            nc.vector.tensor_tensor(mean[:, :], even, odd, ALU.add).then_inc(ln, 1)
            nc.vector.tensor_tensor(rstd[:, :], even, odd, ALU.subtract).then_inc(ln, 1)
            nc.vector.tensor_tensor(var[:, :], stats[:, :, 2], stats[:, :, 5], ALU.add).then_inc(ln, 1)
            dve.wait_ge(ln, 3)
            nc.vector.tensor_scalar(mean[:, :], mean[:, :], 0.5, None, ALU.mult).then_inc(ln, 1)
            nc.vector.tensor_tensor(rstd[:, :], rstd[:, :], rstd[:, :], ALU.mult).then_inc(ln, 1)
            nc.vector.tensor_scalar(var[:, :], var[:, :], 1.0 / D, EPS, ALU.mult, ALU.add).then_inc(ln, 1)
            dve.wait_ge(ln, 6)
            nc.vector.scalar_tensor_tensor(out=var[:, :], in0=rstd[:, :], scalar=0.25, in1=var[:, :],
                                           op0=ALU.mult, op1=ALU.add).then_inc(ln, 1)
            def transposed(n):
                dve.wait_ge(tr_ps, 2 * n + 2)
                nc.vector.tensor_copy(tr[TURN[n]][:, 4:8, :].rearrange("p j e -> p (j e)"),
                                      ps[(2 * n + 1) % 4][:, :]).then_inc(tr_dve, 1)

            transposed(0)
            transposed(1)
            dve.wait_ge(tr_act, 1)
            dve.wait_ge(tr_dve, 1)
            nc.vector.tensor_reduce(corr[:, :], tr[0][:, :, :], AX.X, ALU.add).then_inc(corr_d, 1)
            transposed(2)
            dve.wait_ge(corr_d, 1)
            dve.wait_ge(b_in, 80)
            nc.vector.tensor_tensor(corr[:, :], bq[:, :], corr[:, :], ALU.subtract).then_inc(corr_d, 1)
            dve.wait_ge(corr_d, 2)
            nc.vector.tensor_scalar(corr[:, :], corr[:, :], CA_SCALE / D, None, ALU.mult).then_inc(corr_d, 1)
            dve.wait_ge(corr_d, 3)
            nc.vector.scalar_tensor_tensor(out=tr[0][:, :, :], in0=tr[0][:, :, :], scalar=CA_SCALE,
                                           in1=over_keys(corr[:, :], D), op0=ALU.mult, op1=ALU.add).then_inc(wq_ok, 1)
            for k, (n, h2, j0) in enumerate(fills):
                dve.wait_ge(prod_hi, k + 1)
                hi = dest((a_hi, n_hi)[n], h2, j0)
                nc.vector.tensor_tensor(dest((a_lo, n_lo)[n], h2, j0), ps[4 + k % 4][:, :].rearrange("c (j e) -> c j e", j=4),
                                        hi.bitcast(F32), ALU.subtract).then_inc(prod_lo, 1)
            dve.wait_ge(vec_ps, 1)
            for h2 in range(2):
                nc.vector.tensor_copy(b_vec[:, :].rearrange("p (j h) -> p j h", h=2)[:, :, h2],
                                      ps[h2][:, 0:8]).then_inc(vec_ok, 1)
            nc.vector.tensor_tensor(y_bias[:, :], ps[3][:, 0:1], bu[:, :], ALU.add).then_inc(vec_ok, 1)


STEPS = PAIRS // 2


def load_cn(nc, sp, ctx, cn, cn_in, i):
    sp.dma_start(cn[:, :, :], ctx.rearrange("(i b) k d -> (b k) i d", b=2)[:, ds(i * 2, 2), :]).then_inc(cn_in, 16)


def load_cpad(nc, sp, ctx, cpad, cpad_in, i):
    for half in range(2):
        sp.dma_start(cpad[64 * half:64 * half + 64, :, half, :],
                     ctx.rearrange("b k d -> k b d")[:, ds(i * 4, 4), :]).then_inc(cpad_in, 16)


def cross_attention(nc, sem, sb, ps, ctx, cn, cpad, cn_in, cpad_in, act, mean, rstd, ident, a_hi, a_lo, b_vec, n_hi, n_lo, y_bias,
                    power, eps, one, ff, ff_hi, ff_lo):
    xs = sb("ca_xs", [P, 2, D])
    xt = sb("ca_xt", [P, 2, P])
    ct_hi, ct_lo = sb("ca_ct_hi", [P, 2 * P], F32R), sb("ca_ct_lo", [P, 2 * P], F32R)
    keys = sb("ca_keys", [P, H, 2 * P])
    prob = [sb(f"ca_prob{n}", [P, H * T]) for n in range(2)]
    top, rsum = sb("ca_top", [P, 2, H]), sb("ca_rsum", [P, 2, H])
    pts = [sb(f"ca_pt{n}", [P, H // 2, P]) for n in range(2)]
    r_hi, r_lo = sb("ca_r_hi", [P, H, 2 * P], F32R), sb("ca_r_lo", [P, H, 2 * P], F32R)
    yt = sb("ca_yt", [P, 2 * P])
    y = sb("ca_y", [P, 2, D])
    y_stats, moments = sb("ca_y_stats", [P, 2, 6]), sb("ca_moments", [P, 2, 2])
    y_rstd = sb("ca_y_rstd", [P, 2])
    w_raw = sb("ca_w_raw", [P, 3, FF])
    w_hi, w_lo = (w[:, :, :].rearrange("p n (e f) -> p n e f", f=FF) for w in (ff_hi, ff_lo))
    ring = (ps[0:2], ps[2:4])
    ps_s, ps_y, ps_t = ps[4:6], ps[6], ps[7]

    s = {n: sem("ca_" + n) for n in (
        "xn", "xs", "t_ps", "xt", "ct_hi", "ct_lo", "g_ps", "g_act", "g_dve",
        "score", "top", "shift", "exp", "sum", "rsum", "norm", "pt_ps", "pt_act", "pt_dve",
        "r_ps", "r_hi", "r_lo", "y_ps", "yt", "yt_ps", "y", "st", "var", "eps", "rstd", "x2", "w_in", "w_hi", "w_lo")}

    order = [("pt", 0), ("g", 0), ("r", 0), ("r", 2), ("g", 1), ("pt", 1), ("g", 2), ("g", 3), ("r", 4), ("r", 6)]

    def free(pe, which, pos, i):
        def exists(kind, i):
            return not isinstance(i, int) or (i < STEPS if kind == "g" else i >= 1) and i >= 0
        back, at = i, pos - 2
        while True:
            if at < 0:
                back, at = back - 1, at + len(order)
            if isinstance(back, int) and back < 0:
                return
            if exists(order[at][0], back):
                break
            at -= 2
        kind, n = order[at]
        if kind == "g":
            pe.wait_ge(s[("g_act", "g_dve")[which]], back * 4 + n + 1)
        elif kind == "pt":
            pe.wait_ge(s[("pt_act", "pt_dve")[which]], back * 2 - 2 + n + 1)
        else:
            pe.wait_ge(s["r_lo"], back * 8 - 8 + n + which + 1)

    def position(kind, n):
        return order.index((kind, n))

    def pipeline(eng, body):
        for i in range(3):
            body(i)
        with eng.Fori(3, STEPS - 1) as i:
            body(i)
        for i in range(STEPS - 1, STEPS + 2):
            body(i)

    def spans(i):
        if isinstance(i, int):
            return i < STEPS, 1 <= i <= STEPS, 2 <= i
        return True, True, True

    def past(i, n):
        return not isinstance(i, int) or i > n

    def has_next(i):
        return not isinstance(i, int) or i + 1 < STEPS

    with nc.Block() as block:

        @block.sync
        def _(sp):
            def expert_weights(w1, w3, w2):
                for n, w in enumerate((w1, w3)):
                    sp.dma_start(w_raw[:, n, :].unsqueeze(1), w).then_inc(s["w_in"], 16)
                sp.dma_start(w_raw[:, 2, :].rearrange("p (c d) -> p c d", d=D).unsqueeze(1), w2).then_inc(s["w_in"], 16)

            expert_weights(ff["Ws1"].unsqueeze(1), ff["Ws3"].unsqueeze(1),
                           ff["Ws2"].rearrange("(c p) d -> p c d", p=P).unsqueeze(1))
            def body(i, e=None):
                if past(i, 0):
                    sp.wait_ge(s["t_ps"], i)
                    load_cn(nc, sp, ctx, cn, cn_in, i)
                    sp.wait_ge(s["r_ps"], i * 8)
                    load_cpad(nc, sp, ctx, cpad, cpad_in, i)
                if e is not None:
                    sp.wait_ge(s["w_lo"], e + 1)
                    expert_weights(ff["We1"].rearrange("e d f -> d e f")[:, ds(e, 1), :],
                                   ff["We3"].rearrange("e d f -> d e f")[:, ds(e, 1), :],
                                   ff["We2"].rearrange("e (c p) d -> p e c d", p=P)[:, ds(e, 1), :, :])

            body(0, 0)
            with sp.Fori(1, E) as i:
                body(i, i)
            with sp.Fori(E, STEPS) as i:
                body(i)

        @block.tensor
        def _(pe):
            def transpose_in(i):
                pe.wait_ge(s["xs"], i * 2 + 2)
                pe.wait_ge(cn_in, i * 16 + 16)
                if past(i, 0):
                    pe.wait_ge(s["xt"], i)
                    pe.wait_ge(s["ct_lo"], i)
                if past(i, 2):
                    pe.wait_ge(s["y"], i - 2)
                for p in range(2):
                    nc.tensor.transpose(ps_t[:, P * p:P * p + P], xs[:, p, :], ident[:, :])
                for p in range(2):
                    ins = nc.tensor.transpose(ps_t[:, P * (2 + p):P * (3 + p)], cn[:, p, :], ident[:, :])
                ins.then_inc(s["t_ps"], 1)

            def absorbed_keys(i, fills):
                if fills[0] == 0:
                    pe.wait_ge(s["ct_hi"], i + 1)
                    pe.wait_ge(s["ct_lo"], i + 1)
                for f in fills:
                    which, n = f % 2, f // 2
                    pos = position("g", n)
                    free(pe, which, pos, i)
                    for h in (2 * f, 2 * f + 1):
                        out = ring[which][pos % 2][:, 256 * (h % 2):256 * (h % 2) + 256]
                        nc.tensor.matmul(out, a_hi[:, h, :], ct_hi[:, :], start=True, stop=False)
                        nc.tensor.matmul(out, a_lo[:, h, :], ct_hi[:, :], start=False, stop=False)
                        ins = nc.tensor.matmul(out, a_hi[:, h, :], ct_lo[:, :], start=False, stop=True)
                    ins.then_inc(s["g_ps"], 1)

            def scores(i, p):
                if p == 0:
                    pe.wait_ge(s["xt"], i + 1)
                    pe.wait_ge(s["g_act"], i * 4 + 4)
                    pe.wait_ge(s["g_dve"], i * 4 + 4)
                if p or past(i, 0):
                    pe.wait_ge(s["shift"], i * 2 + p)
                for half in range(2):
                    for b in range(2):
                        c = P * p + T * b
                        ins = nc.tensor.matmul(ps_s[half][T * b:T * b + T, :], xt[:, p, T * b:T * b + T],
                                               keys[:, 8 * half:8 * half + 8, c:c + T], start=True, stop=True)
                    ins.then_inc(s["score"], 1)

            def transpose_prob(i, p):
                pe.wait_ge(s["norm"], i * 2 - 2 + p + 1)
                for which in range(2):
                    pos = position("pt", p)
                    free(pe, which, pos, i)
                    for j in range(4):
                        ins = nc.tensor.transpose(ring[which][pos % 2][:, P * j:P * j + P],
                                                  prob[p][:, P * (4 * which + j):P * (4 * which + j + 1)], ident[:, :])
                    ins.then_inc(s["pt_ps"], 1)

            def values(i, p):
                if p == 0:
                    pe.wait_ge(cpad_in, i * 32)
                for n in range(4):
                    b, half, which = n // 2, n % 2, n % 2
                    pos = position("r", 4 * p + n - which)
                    free(pe, which, pos, i)
                    if n == 0:
                        pe.wait_ge(s["pt_act"], i * 2 - 2 + p + 1)
                        pe.wait_ge(s["pt_dve"], i * 2 - 2 + p + 1)
                    nc.tensor.matmul(ring[which][pos % 2][:, :], cpad[:, 2 * p + b, half, :],
                                     pts[p][:, :, T * b:T * b + T], start=True, stop=True).then_inc(s["r_ps"], 1)

            def output(i, part):
                if part == 0:
                    pe.wait_ge(s["r_lo"], i * 8)
                    if past(i, 1):
                        pe.wait_ge(s["yt"], i - 1)
                for h in range(H // 2 * part, H // 2 * (part + 1)):
                    nc.tensor.matmul(ps_y[:, 0:2 * P], n_hi[:, h, :], r_hi[:, h, :], start=(h == 0), stop=False)
                    nc.tensor.matmul(ps_y[:, 0:2 * P], n_lo[:, h, :], r_hi[:, h, :], start=False, stop=False)
                    ins = nc.tensor.matmul(ps_y[:, 0:2 * P], n_hi[:, h, :], r_lo[:, h, :], start=False, stop=(h == H - 1))
                if part:
                    ins.then_inc(s["y_ps"], 1)

            def transpose_out(i):
                pe.wait_ge(s["yt"], i - 1)
                pe.wait_ge(s["xt"], i + 1 if not isinstance(i, int) else min(i + 1, STEPS))
                pe.wait_ge(s["ct_lo"], i + 1 if not isinstance(i, int) else min(i + 1, STEPS))
                if isinstance(i, int) and i >= STEPS:
                    pe.wait_ge(s["y"], i - 2)
                for p in range(2):
                    ins = nc.tensor.transpose(ps_t[:, P * p:P * p + P], yt[:, P * p:P * p + P], ident[:, :])
                ins.then_inc(s["yt_ps"], 1)

            def body(i):
                now, before, out = spans(i)
                if before:
                    transpose_prob(i, 0)
                if now:
                    absorbed_keys(i, range(0, 2))
                if before:
                    values(i, 0)
                if now:
                    absorbed_keys(i, range(2, 4))
                if out:
                    transpose_out(i)
                if before:
                    transpose_prob(i, 1)
                if now:
                    absorbed_keys(i, range(4, 8))
                if before:
                    values(i, 1)
                if now:
                    scores(i, 0)
                if before:
                    output(i, 0)
                if now:
                    scores(i, 1)
                if has_next(i):
                    transpose_in(i + 1)
                if before:
                    output(i, 1)

            transpose_in(0)
            pipeline(pe, body)

        @block.vector
        def _(dve):
            def normalise(i):
                if past(i, 0):
                    dve.wait_ge(s["t_ps"], i)
                for p in range(2):
                    nc.vector.tensor_scalar(xs[:, p, :].unsqueeze(1), act[:, ds(i * 2 + p, 1), :],
                                            mean[:, ds(i * 2 + p, 1)], rstd[:, ds(i * 2 + p, 1)],
                                            ALU.subtract, ALU.mult).then_inc(s["xs"], 1)
                dve.wait_ge(s["xs"], i * 2 + 2)
                nc.vector.tensor_scalar(act[:, ds(i * 2, 2), :], xs[:, :, :], 1.0, None, ALU.mult).then_inc(s["xn"], 1)

            def x2(i):
                dve.wait_ge(s["rstd"], i + 1)
                for p in range(2):
                    nc.vector.tensor_scalar(act[:, ds(i * 2 + p, 1), :], y[:, p, :].unsqueeze(1),
                                            moments[:, p, 0:1], y_rstd[:, p:p + 1],
                                            ALU.subtract, ALU.mult).then_inc(s["x2"], 1)

            def softmax_in(i, p):
                for half in range(2):
                    dve.wait_ge(s["score"], i * 4 + 2 * p + half + 1)
                    nc.vector.tensor_reduce(top[:, p, 8 * half:8 * half + 8], heads(ps_s[half][:, :]), AX.X,
                                            ALU.max).then_inc(s["top"], 1)
                for half in range(2):
                    dve.wait_ge(s["top"], i * 4 + 2 * p + half + 1)
                    ins = nc.vector.tensor_tensor(heads(prob[p][:, 512 * half:512 * half + 512]),
                                                  heads(ps_s[half][:, :]),
                                                  over_keys(top[:, p, 8 * half:8 * half + 8]), ALU.subtract)
                ins.then_inc(s["shift"], 1)

            def softmax_sum(i, p):
                dve.wait_ge(s["exp"], i * 2 + p + 1)
                nc.vector.tensor_reduce(rsum[:, p, :], heads(prob[p][:, :]), AX.X, ALU.add).then_inc(s["sum"], 1)
                dve.wait_ge(s["sum"], i * 2 + p + 1)
                nc.vector.reciprocal(rsum[:, p, :], rsum[:, p, :]).then_inc(s["rsum"], 1)

            def transposed_prob(i, p):
                dve.wait_ge(s["pt_ps"], i * 4 - 4 + 2 * p + 2)
                if past(i, 1):
                    dve.wait_ge(s["r_ps"], i * 8 - 16 + 4 * p + 4)
                nc.vector.tensor_copy(pts[p][:, 4:8, :].rearrange("p j q -> p (j q)"),
                                      ring[1][position("pt", p) % 2][:, :]).then_inc(s["pt_dve"], 1)

            def values_low(i, p, ns):
                for n in ns:
                    b, half = n // 2, n % 2
                    bank = ring[half][position("r", 4 * p + n - half) % 2]
                    c = P * p + T * b
                    part = [r[:, :, c:c + T].rearrange("p (j h) q -> p j h q", h=2)[:, :, half, :] for r in (r_hi, r_lo)]
                    dve.wait_ge(s["r_hi"], i * 8 - 8 + 4 * p + n + 1)
                    nc.vector.tensor_tensor(part[1], bank[:, :].rearrange("p (j q) -> p j q", q=T),
                                            part[0].bitcast(F32), ALU.subtract).then_inc(s["r_lo"], 1)

            def keys_in(i, ns):
                for n in ns:
                    dve.wait_ge(s["g_ps"], i * 8 + 2 * n + 2)
                    if n == 0 and past(i, 0):
                        dve.wait_ge(s["score"], i * 4)
                    h = 4 * n + 2
                    nc.vector.tensor_tensor(keys[:, h:h + 2, :],
                                            ring[1][position("g", n) % 2][:, :].rearrange("p (h k) -> p h k", h=2),
                                            over_keys(b_vec[:, h:h + 2], 2 * P), ALU.add).then_inc(s["g_dve"], 1)

            def context_low(i):
                dve.wait_ge(s["ct_hi"], i + 1)
                nc.vector.tensor_tensor(ct_lo[:, :], ps_t[:, 2 * P:4 * P], ct_hi[:, :].bitcast(F32),
                                        ALU.subtract).then_inc(s["ct_lo"], 1)

            normalise(0)
            context_low(0)

            def body(i):
                now, before, out = spans(i)
                if before:
                    transposed_prob(i, 0)
                if now:
                    keys_in(i, (0,))
                if before:
                    softmax_sum(i - 1, 1)
                    values_low(i, 0, range(4))
                if now:
                    keys_in(i, (1,))
                if out:
                    dve.wait_ge(s["yt_ps"], i - 1)
                    if past(i, 2):
                        dve.wait_ge(s["x2"], i * 2 - 4)
                    nc.vector.tensor_tensor(y[:, :, :], act[:, ds(i * 2 - 4, 2), :],
                                            ps_t[:, 0:2 * P].rearrange("p (i d) -> p i d", i=2),
                                            ALU.add).then_inc(s["y"], 1)
                if before:
                    transposed_prob(i, 1)
                if out:
                    dve.wait_ge(s["y"], i - 1)
                    for p in range(2):
                        nc.vector.bn_stats(y_stats[:, p, :], y[:, p, :]).then_inc(s["st"], 1)
                if now:
                    keys_in(i, (2, 3))
                if out:
                    dve.wait_ge(s["st"], i * 2 - 2)
                if before:
                    values_low(i, 1, (0,))
                if out:
                    for p in range(2):
                        nc.vector.bn_aggr(moments[:, p, :], y_stats[:, p, :]).then_inc(s["var"], 1)
                if before:
                    values_low(i, 1, (1, 2, 3))
                if out:
                    x2(i - 2)
                if now:
                    softmax_in(i, 0)
                    if has_next(i):
                        normalise(i + 1)
                    softmax_sum(i, 0)
                    softmax_in(i, 1)
                if has_next(i):
                    context_low(i + 1)

            pipeline(dve, body)

        @block.scalar
        def _(actv):
            def context_high(i):
                actv.wait_ge(s["t_ps"], i + 1)
                if past(i, 0):
                    actv.wait_ge(s["g_ps"], i * 8)
                nc.scalar.activation(ct_hi[:, :], ps_t[:, 2 * P:4 * P], ACT.Copy).then_inc(s["ct_hi"], 1)

            def exps(i, p):
                actv.wait_ge(s["shift"], i * 2 + p + 1)
                nc.scalar.activation(prob[p][:, :], prob[p][:, :], ACT.Exp).then_inc(s["exp"], 1)

            def transposed_prob(i, p):
                actv.wait_ge(s["pt_ps"], i * 4 - 4 + 2 * p + 1)
                if past(i, 1):
                    actv.wait_ge(s["r_ps"], i * 8 - 16 + 4 * p + 4)
                nc.scalar.activation(pts[p][:, 0:4, :].rearrange("p j q -> p (j q)"),
                                     ring[0][position("pt", p) % 2][:, :], ACT.Copy).then_inc(s["pt_act"], 1)

            def values_high(i, p):
                for n in range(4):
                    b, half = n // 2, n % 2
                    bank = ring[half][position("r", 4 * p + n - half) % 2]
                    c = P * p + T * b
                    actv.wait_ge(s["r_ps"], i * 8 - 8 + 4 * p + n + 1)
                    nc.scalar.activation(r_hi[:, :, c:c + T].rearrange("p (j h) q -> p j h q", h=2)[:, :, half, :],
                                         bank[:, :].rearrange("p (j q) -> p j q", q=T), ACT.Copy).then_inc(s["r_hi"], 1)

            def keys_in(i, ns):
                for n in ns:
                    actv.wait_ge(s["g_ps"], i * 8 + 2 * n + 1)
                    for h in (4 * n, 4 * n + 1):
                        ins = nc.scalar.activation(keys[:, h, :],
                                                   ring[0][position("g", n) % 2][:, 256 * (h % 2):256 * (h % 2) + 256],
                                                   ACT.Identity, bias=b_vec[:, h:h + 1])
                    ins.then_inc(s["g_act"], 1)

            def body(i):
                now, before, out = spans(i)
                if before:
                    transposed_prob(i, 0)
                    exps(i - 1, 1)
                if now:
                    keys_in(i, (0,))
                    if past(i, 0):
                        actv.wait_ge(s["score"], i * 4)
                    actv.wait_ge(s["ct_lo"], i + 1)
                    nc.scalar.activation(xt[:, :, :], ps_t[:, 0:2 * P].rearrange("p (i d) -> p i d", i=2),
                                         ACT.Copy, bias=1.0).then_inc(s["xt"], 1)
                if before:
                    values_high(i, 0)
                if now:
                    keys_in(i, (1,))
                if before:
                    transposed_prob(i, 1)
                if now:
                    keys_in(i, (2, 3))
                if before:
                    values_high(i, 1)
                if now:
                    exps(i, 0)
                if has_next(i):
                    context_high(i + 1)
                if before:
                    actv.wait_ge(s["y_ps"], i)
                    if past(i, 1):
                        actv.wait_ge(s["yt_ps"], i - 1)
                    nc.scalar.activation(yt[:, :], ps_y[:, 0:2 * P], ACT.Identity,
                                         bias=y_bias[:, 0:1]).then_inc(s["yt"], 1)

            context_high(0)
            pipeline(actv, body)

        @block.gpsimd
        def _(pool):
            def norm(i, p):
                pool.wait_ge(s["rsum"], i * 2 + p + 1)
                nc.gpsimd.tensor_tensor(heads(prob[p][:, :]), heads(prob[p][:, :]), over_keys(rsum[:, p, :]),
                                        ALU.mult).then_inc(s["norm"], 1)

            def y_scale(i):
                pool.wait_ge(s["var"], i * 2 + 2)
                nc.gpsimd.tensor_tensor(y_rstd[:, :], moments[:, :, 1], eps[:, 0:y_rstd.shape[1]],
                                        ALU.add).then_inc(s["eps"], 1)
                pool.wait_ge(s["eps"], i + 1)
                nc.gpsimd.tensor_tensor(y_rstd[:, :], y_rstd[:, :], power[:, 0:y_rstd.shape[1]],
                                        ALU.pow).then_inc(s["rstd"], 1)

            def cut(e):
                raw, hi, lo = w_raw[:, :, :].unsqueeze(2), w_hi[:, :, ds(e, 1), :], w_lo[:, :, ds(e, 1), :]
                pool.wait_ge(s["w_in"], e * 48 + 48)
                nc.gpsimd.tensor_tensor(hi, raw, one[:, 0:3].unsqueeze(2).unsqueeze(3).broadcast_to((P, 3, 1, FF)),
                                        ALU.mult).then_inc(s["w_hi"], 1)
                pool.wait_ge(s["w_hi"], e + 1)
                nc.gpsimd.tensor_tensor(lo, raw, hi.bitcast(F32), ALU.subtract).then_inc(s["w_lo"], 1)

            cut(0)

            def body(i, cutting=False):
                if not isinstance(i, int) or i >= 2:
                    y_scale(i - 2)
                if not isinstance(i, int) or i < STEPS:
                    norm(i, 0)
                    norm(i, 1)
                if cutting:
                    cut(i + 1)

            for i in range(2):
                body(i, True)
            with pool.Fori(2, E) as i:
                body(i, True)
            with pool.Fori(E, STEPS) as i:
                body(i)
            for i in range(STEPS, STEPS + 2):
                body(i)


TILES = 4
GROUPS = PAIRS // TILES
UNITS = (E + 1) * FF // P


def router(nc, sem, sb, ps, act, ident, wg, x_hi, x_lo, wt_dram, wt_stored):
    xs = [sb(f"ro_xs{n}", [P, TILES, D]) for n in range(2)]
    xt = [sb(f"ro_xt{n}", [P, TILES * P]) for n in range(2)]
    logits = sb("ro_logits", [P, PAIRS, E])
    gate, sel, pick, count, rest = (sb("ro_" + n, [P, PAIRS, E]) for n in ("gate", "sel", "pick", "count", "rest"))
    keep = sb("ro_keep", [P, PAIRS, E])
    best, total = sb("ro_best", [P, PAIRS]), sb("ro_total", [P, PAIRS])
    wt = sb("ro_wt", [P, 2, P])
    ps_t, ps_l, ps_w = ps[0:2], ps[2:4], ps[4]
    s = {n: sem("ro_" + n) for n in ("xs", "t_ps", "xt", "x_hi", "x_lo", "l_ps", "logits", "exp", "chain",
                                     "wt_ps", "wt", "keep")}

    def in_twos(eng, body):
        body(0, 0)
        body(1, 1)
        with eng.Fori(1, GROUPS // 2) as k:
            body(k * 2, 0)
            body(k * 2 + 1, 1)

    def reused(i):
        return not isinstance(i, int)

    with nc.Block() as block:

        @block.tensor
        def _(pe):
            def transposes(i, n):
                pe.wait_ge(s["xs"], i + 1)
                if reused(i):
                    pe.wait_ge(s["xt"], i - 1)
                for t in range(TILES):
                    ins = nc.tensor.transpose(ps_t[n][:, P * t:P * t + P], xs[n][:, t, :], ident[:, :])
                ins.then_inc(s["t_ps"], 1)

            def gate_logits(i, n):
                pe.wait_ge(s["xt"], i + 1)
                if reused(i):
                    pe.wait_ge(s["logits"], i - 1)
                for t in range(TILES):
                    ins = nc.tensor.matmul(ps_l[n][:, E * t:E * t + E], xt[n][:, P * t:P * t + P], wg[:, :],
                                           start=True, stop=True)
                ins.then_inc(s["l_ps"], 1)

            transposes(0, 0)
            transposes(1, 1)
            gate_logits(0, 0)
            with pe.Fori(1, GROUPS // 2) as k:
                transposes(k * 2, 0)
                gate_logits(k * 2 - 1, 1)
                transposes(k * 2 + 1, 1)
                gate_logits(k * 2, 0)
            gate_logits(GROUPS - 1, 1)
            pe.wait_ge(s["wt"], 1)
            for n in range(2):
                ins = nc.tensor.transpose(ps_w[:, P * n:P * n + P],
                                          sel[:, 16 * n:16 * n + 16, :].rearrange("p t e -> p (t e)"), ident[:, :])
            ins.then_inc(s["wt_ps"], 1)

        @block.scalar
        def _(actv):
            def body(i, n):
                actv.wait_ge(s["t_ps"], i + 1)
                if reused(i):
                    actv.wait_ge(s["l_ps"], i - 1)
                    actv.wait_ge(s["x_lo"], i - 1)
                nc.scalar.activation(xt[n][:, :], ps_t[n][:, :], ACT.Copy).then_inc(s["xt"], 1)
                actv.wait_ge(s["xt"], i + 1)
                nc.scalar.activation(x_hi[:, ds(i, 1), :], xt[n][:, :].unsqueeze(1), ACT.Copy).then_inc(s["x_hi"], 1)

            in_twos(actv, body)
            actv.wait_ge(s["logits"], GROUPS)
            nc.scalar.activation(gate[:, :, :], logits[:, :, :], ACT.Exp, scale=-1.0).then_inc(s["exp"], 1)
            actv.preload_act_table(ACT.Silu)

        @block.vector
        def _(dve):
            def fixed(i, n):
                if reused(i):
                    dve.wait_ge(s["t_ps"], i - 1)
                nc.vector.tensor_scalar(xs[n][:, :, :], act[:, ds(i * TILES, TILES), :], 1.0, None,
                                        ALU.mult).then_inc(s["xs"], 1)

            def low(i, n):
                dve.wait_ge(s["x_hi"], i + 1)
                nc.vector.tensor_tensor(x_lo[:, ds(i, 1), :], xt[n][:, :].unsqueeze(1),
                                        x_hi[:, ds(i, 1), :].bitcast(F32), ALU.subtract).then_inc(s["x_lo"], 1)
                dve.wait_ge(s["l_ps"], i + 1)
                nc.vector.tensor_scalar(logits[:, ds(i * TILES, TILES), :],
                                        ps_l[n][:, 0:E * TILES].rearrange("p (t e) -> p t e", e=E), 1.0, None,
                                        ALU.mult).then_inc(s["logits"], 1)

            fixed(0, 0)
            fixed(1, 1)
            nc.vector.memset(keep[:, :, :], 1.0).then_inc(s["keep"], 1)
            dve.wait_ge(s["keep"], 1)
            nc.vector.memset(keep[:, :, 0], 0.0).then_inc(s["keep"], 1)
            low(0, 0)
            with dve.Fori(1, GROUPS // 2) as k:
                fixed(k * 2, 0)
                low(k * 2 - 1, 1)
                fixed(k * 2 + 1, 1)
                low(k * 2, 0)
            low(GROUPS - 1, 1)
            dve.wait_ge(s["keep"], 2)

            done = [0]

            def then(ins):
                done[0] += 1
                ins.then_inc(s["chain"], 1)
                dve.wait_ge(s["chain"], done[0])

            def flat(ap):
                return ap[:, :, :].rearrange("p t e -> p (t e)")

            dve.wait_ge(s["exp"], 1)
            then(nc.vector.tensor_scalar(flat(gate), flat(gate), 1.0, None, ALU.add))
            then(nc.vector.reciprocal(flat(gate), flat(gate)))
            for n, (source, chosen) in enumerate(((gate, sel), (rest, pick))):
                then(nc.vector.tensor_reduce(best[:, :], source[:, :, :], AX.X, ALU.max))
                then(nc.vector.tensor_tensor(chosen[:, :, :], source[:, :, :], over_keys(best[:, :], E), ALU.is_equal))
                then(nc.vector.tensor_tensor_scan(flat(count), flat(keep), flat(chosen), 0.0, ALU.mult, ALU.add))
                then(nc.vector.scalar_tensor_tensor(out=flat(chosen), in0=flat(count), scalar=1.0, in1=flat(chosen),
                                                    op0=ALU.is_equal, op1=ALU.mult))
                if n == 0:
                    then(nc.vector.scalar_tensor_tensor(out=flat(rest), in0=flat(sel), scalar=-4.0, in1=flat(gate),
                                                        op0=ALU.mult, op1=ALU.add))
            then(nc.vector.tensor_tensor(flat(sel), flat(sel), flat(pick), ALU.add))
            then(nc.vector.tensor_tensor(flat(sel), flat(sel), flat(gate), ALU.mult))
            then(nc.vector.tensor_reduce(total[:, :], sel[:, :, :], AX.X, ALU.add))
            then(nc.vector.reciprocal(total[:, :], total[:, :]))
            nc.vector.tensor_tensor(sel[:, :, :], sel[:, :, :], over_keys(total[:, :], E), ALU.mult).then_inc(s["wt"], 1)
            dve.wait_ge(s["wt_ps"], 1)
            nc.vector.tensor_copy(wt[:, :, :], ps_w[:, 0:2 * P].rearrange("p (n k) -> p n k", n=2)).then_inc(s["wt"], 1)

        @block.sync
        def _(sp):
            sp.wait_ge(s["wt"], 2)
            for n in range(2):
                sp.dma_start(wt_dram[16 * n:16 * n + 16, :, :].rearrange("t e k -> (t e) k"), wt[:, n, :])\
                  .then_inc(wt_stored, 16)


def experts(nc, sem, sb, ps, act, ident, power, eps, w1, w3, w2, x_hi, x_lo, wt_dram, wt_stored, out):
    LAG, KEEP = 3, 6
    gated = sb("ff_gated", [P, 2, TILES * P])
    hidden = sb("ff_hidden", [P, 3, TILES * P])
    h_hi, h_lo = sb("ff_h_hi", [P, KEEP, TILES * P], F32R), sb("ff_h_lo", [P, KEEP, TILES * P], F32R)
    gates = sb("ff_gates", [P, E, TILES * P])
    yt = sb("ff_yt", [P, TILES * P])
    y = sb("ff_y", [P, TILES, D])
    y_stats, moments = sb("ff_y_stats", [P, TILES, 6]), sb("ff_moments", [P, TILES, 2])
    y_rstd = sb("ff_y_rstd", [P, TILES])
    ps_1, ps_3, ps_y, ps_t = ps[0:2], ps[2:4], ps[4], ps[5]
    s = {n: sem("ff_" + n) for n in ("u1", "u3", "silu", "mul", "gate", "hi", "lo", "down", "y_ps", "yt", "yt_ps",
                                     "y", "st", "var", "eps", "rstd", "x3", "stored")}
    gate_in = [sem(f"ff_gate_in{e}") for e in range(E)]
    OUT_AT = 5

    def whole(pe_like, body, tail):
        body(0, True)
        with pe_like.Fori(1, GROUPS) as i:
            body(i, False)
        tail()

    with nc.Block() as block:

        @block.sync
        def _(sp):
            def load(i, e):
                src = wt_dram[ds(i * TILES, TILES), e, :].unsqueeze(0).broadcast_to((P, TILES, P))
                sp.dma_start(gates[:, e, :].rearrange("p (t k) -> p t k", t=TILES), src).then_inc(gate_in[e], 16)

            def store(i):
                sp.wait_ge(s["x3"], i * TILES + TILES)
                sp.dma_start(out[:, ds(i * TILES, TILES), :], y[:, :, :]).then_inc(s["stored"], 16)

            sp.wait_ge(wt_stored, 32)
            for e in range(E):
                load(0, e)
            with sp.Fori(1, GROUPS) as i:
                for e in range(E):
                    sp.wait_ge(s["gate"], i * 2 * E - 2 * E + 2 * e + 2)
                    load(i, e)
                store(i - 1)
            store(GROUPS - 1)
            sp.wait_ge(s["stored"], 16 * GROUPS)

        @block.tensor
        def _(pe):
            def up(i, u):
                e, c = u // 2, u % 2
                cols = slice(FF * e + P * c, FF * e + P * c + P)
                n = i * UNITS + u
                for which, (w, bank, mark) in enumerate(((w1, ps_1[u % 2], "u1"), (w3, ps_3[u % 2], "u3"))):
                    if u >= 2 or not isinstance(i, int):
                        pe.wait_ge(s[("silu", "mul")[which]], n - 1)
                    x_h, x_l = x_hi[:, ds(i, 1), :], x_lo[:, ds(i, 1), :]
                    out = bank[:, :].unsqueeze(1)
                    nc.tensor.matmul(out, w[0][:, cols], x_h, start=True, stop=False)
                    nc.tensor.matmul(out, w[1][:, cols], x_h, start=False, stop=False)
                    nc.tensor.matmul(out, w[0][:, cols], x_l, start=False, stop=True).then_inc(s[mark], 1)

            def down(i, u, first):
                n = i * UNITS + u
                pe.wait_ge(s["lo"], n + 1)
                if u == 0 and not first:
                    pe.wait_ge(s["yt"], i)
                c = slice(D * u, D * u + D)
                k = u % KEEP
                nc.tensor.matmul(ps_y[:, :], w2[0][:, c], h_hi[:, k, :], start=(u == 0), stop=False)
                nc.tensor.matmul(ps_y[:, :], w2[1][:, c], h_hi[:, k, :], start=False, stop=False)
                ins = nc.tensor.matmul(ps_y[:, :], w2[0][:, c], h_lo[:, k, :], start=False, stop=(u == UNITS - 1))
                ins.then_inc(s["down"], 1)

            def out(count):
                pe.wait_ge(s["yt"], count)
                for t in range(TILES):
                    ins = nc.tensor.transpose(ps_t[:, P * t:P * t + P], yt[:, P * t:P * t + P], ident[:, :])
                ins.then_inc(s["yt_ps"], 1)

            def body(i, first):
                for u in range(UNITS):
                    up(i, u)
                    if u >= LAG:
                        down(i, u - LAG, first)
                    elif not first:
                        down(i - 1, u - LAG + UNITS, True)
                    if u == OUT_AT and not first:
                        out(i)

            def tail():
                for u in range(UNITS - LAG, UNITS):
                    down(GROUPS - 1, u, True)
                out(GROUPS)

            whole(pe, body, tail)

        @block.scalar
        def _(actv):
            actv.preload_act_table(ACT.Silu)

            def high(i, u):
                n = i * UNITS + u
                actv.wait_ge(s["mul"], n + 1)
                if u >= 2:
                    actv.wait_ge(s["gate"], i * 2 * E + u - 1)
                if u >= KEEP or not isinstance(i, int):
                    actv.wait_ge(s["down"], n - KEEP + 1)
                nc.scalar.activation(h_hi[:, u % KEEP, :], hidden[:, u % 3, :], ACT.Copy).then_inc(s["hi"], 1)

            def output(count):
                actv.wait_ge(s["down"], count * UNITS)
                nc.scalar.activation(yt[:, :], ps_y[:, :], ACT.Copy, scale=1.0 / 3.0).then_inc(s["yt"], 1)

            def body(i, first):
                for u in range(UNITS):
                    n = i * UNITS + u
                    actv.wait_ge(s["u1"], n + 1)
                    if u >= 2 or not first:
                        actv.wait_ge(s["mul"], n - 1)
                    nc.scalar.activation(gated[:, u % 2, :], ps_1[u % 2][:, :], ACT.Silu).then_inc(s["silu"], 1)
                    if u >= 2:
                        high(i, u - 2)
                    elif not first:
                        high(i - 1, u - 2 + UNITS)
                    if u == LAG - 1 and not first:
                        output(i)

            def tail():
                for u in range(UNITS - 2, UNITS):
                    high(GROUPS - 1, u)
                output(GROUPS)

            whole(actv, body, tail)

        @block.vector
        def _(dve):
            def low(i, u):
                n = i * UNITS + u
                dve.wait_ge(s["hi"], n + 1)
                nc.vector.tensor_tensor(h_lo[:, u % KEEP, :], hidden[:, u % 3, :], h_hi[:, u % KEEP, :].bitcast(F32),
                                        ALU.subtract).then_inc(s["lo"], 1)

            def add_out(i):
                dve.wait_ge(s["yt_ps"], i + 1)
                nc.vector.tensor_tensor(y[:, :, :], act[:, ds(i * TILES, TILES), :],
                                        ps_t[:, :].rearrange("p (t d) -> p t d", t=TILES), ALU.add).then_inc(s["y"], 1)

            def statistics(i):
                dve.wait_ge(s["y"], i + 1)
                for t in range(TILES):
                    nc.vector.bn_stats(y_stats[:, t, :], y[:, t, :]).then_inc(s["st"], 1)

            def variance(i):
                for t in range(TILES):
                    nc.vector.bn_aggr(moments[:, t, :], y_stats[:, t, :]).then_inc(s["var"], 1)

            def x3(i):
                dve.wait_ge(s["rstd"], i + 1)
                for t in range(TILES):
                    nc.vector.tensor_scalar(y[:, t, :], y[:, t, :], moments[:, t, 0:1], y_rstd[:, t:t + 1],
                                            ALU.subtract, ALU.mult).then_inc(s["x3"], 1)

            after_up = {OUT_AT + 1: add_out, OUT_AT + 2: statistics, OUT_AT + 3: variance, OUT_AT + 6: x3}

            def body(i, first):
                for u in range(UNITS):
                    n = i * UNITS + u
                    dve.wait_ge(s["silu"], n + 1)
                    dve.wait_ge(s["u3"], n + 1)
                    if u >= 3 or not first:
                        dve.wait_ge(s["lo"], n - 2)
                    if u == OUT_AT + 3 and not first:
                        dve.wait_ge(s["st"], i * TILES)
                    nc.vector.tensor_tensor(hidden[:, u % 3, :], gated[:, u % 2, :], ps_3[u % 2][:, :],
                                            ALU.mult).then_inc(s["mul"], 1)
                    if u >= 2:
                        low(i, u - 2)
                    elif not first:
                        low(i - 1, u - 2 + UNITS)
                    if u == UNITS - 1 and not first:
                        dve.wait_ge(s["stored"], i * 16)
                    if u in after_up and not first:
                        after_up[u](i - 1)

            def tail():
                for u in range(UNITS - 2, UNITS):
                    low(GROUPS - 1, u)
                add_out(GROUPS - 1)
                statistics(GROUPS - 1)
                dve.wait_ge(s["st"], GROUPS * TILES)
                variance(GROUPS - 1)
                x3(GROUPS - 1)

            whole(dve, body, tail)

        @block.gpsimd
        def _(pool):
            def y_scale(i):
                pool.wait_ge(s["var"], i * TILES + TILES)
                nc.gpsimd.tensor_tensor(y_rstd[:, :], moments[:, :, 1], eps[:, 0:y_rstd.shape[1]],
                                        ALU.add).then_inc(s["eps"], 1)
                pool.wait_ge(s["eps"], i + 1)
                nc.gpsimd.tensor_tensor(y_rstd[:, :], y_rstd[:, :], power[:, 0:y_rstd.shape[1]],
                                        ALU.pow).then_inc(s["rstd"], 1)

            def body(i, first):
                for u in range(2, UNITS):
                    e = u // 2 - 1
                    if u == OUT_AT + 5 and not first:
                        y_scale(i - 1)
                    if u % 2 == 0:
                        pool.wait_ge(gate_in[e], i * 16 + 16)
                    pool.wait_ge(s["mul"], i * UNITS + u + 1)
                    nc.gpsimd.tensor_tensor(hidden[:, u % 3, :], hidden[:, u % 3, :], gates[:, e, :],
                                            ALU.mult).then_inc(s["gate"], 1)

            whole(pool, body, lambda: y_scale(GROUPS - 1))


def decoder_layer(nc, i, out, wt_dram):
    with ExitStack() as whole:
        def allocator(ctx):
            return lambda name, shape, dt=F32: ctx.enter_context(nc.sbuf_tensor(name, shape, dt))

        def sem(name):
            return whole.enter_context(nc.semaphore(name))

        sb = allocator(whole)
        ps = [whole.enter_context(nc.psum_tensor(f"bank{n}", [P, 512], F32)) for n in range(8)]
        act = sb("act", [P, PAIRS, D])
        stats = sb("stats", [P, PAIRS, 6])
        mean, var, rstd, power = (sb(n, [P, PAIRS]) for n in ("mean", "var", "rstd", "power"))
        eps, one = sb("eps", [P, TILES]), sb("one", [P, TILES])
        ident = sb("ident", [P, P])
        wg = sb("wg", [P, E])
        ff_hi, ff_lo = (sb(n, [P, 3, (E + 1) * FF], F32R) for n in ("ff_hi", "ff_lo"))
        x, out = (a.rearrange("(i b) t d -> (b t) i d", b=2) for a in (i["x"], out))
        sa_w_in, x_in, x_rest, ab_b_in, wt_stored, cn_in, cpad_in, cpad_zero = (
            sem(n) for n in ("sa_w_in", "x_in", "x_rest", "ab_b_in", "wt_stored", "cn_in", "cpad_in", "cpad_zero"))
        ab_w_in = [sem(f"ab_w_in{n}") for n in range(4)]

        with ExitStack() as before_experts:
            sb2 = allocator(before_experts)
            a_hi, a_lo, n_hi, n_lo = (sb2(n, [P, H, P], F32R) for n in ("a_hi", "a_lo", "n_hi", "n_lo"))
            b_vec, y_bias = sb2("b_vec", [P, H]), sb2("y_bias", [P, 1])
            cn = sb2("ca_cn", [P, 2, D])
            cpad = sb2("ca_cpad", [P, 4, 2, D])

            with ExitStack() as before_cross:
                sb0 = allocator(before_cross)
                raw = [sb0("raw_" + n, [P, H * HK]) for n in ("Wq", "Wk", "Wv")]
                wu = sb0("Wu", [P, H // 2, D])
                bq, bk, bv = (sb0(n, [P, H // 2]) for n in ("bq", "bk", "bv"))
                bu = sb0("bu", [P, 1])

                with ExitStack() as phase:
                    sb1 = allocator(phase)
                    wqkv, wout = sb1("sa_wqkv", [P, 3 * D]), sb1("sa_wout", [P, D])
                    table = sb1("table", [P, H, T])
                    quad_scale, head_mask = sb1("quad_scale", [P, 4]), sb1("head_mask", [P, 4])
                    vx = sb1("vx", [P, PAIRS, 8, 2, 2, HD + 1])
                    rel_i, rel, mask16 = sb1("rel_i", [P, T], I32), sb1("rel", [P, T]), sb1("mask16", [P, H])

                    def load_all(sp):
                        sp.dma_start(act[:, 0:FIRST_PAIRS, :], x[:, 0:FIRST_PAIRS, :]).then_inc(x_in, 16)
                        sp.dma_start(wqkv[:, :], i["L0_attn_Wqkv"]).then_inc(sa_w_in, 16)
                        sp.dma_start(wout[:, :], i["L0_attn_Wout"]).then_inc(sa_w_in, 16)
                        sp.dma_start(act[:, FIRST_PAIRS:, :], x[:, FIRST_PAIRS:, :]).then_inc(x_rest, 16)
                        for n, name in enumerate(("Wq", "Wk", "Wv")):
                            sp.dma_start(raw[n][:, :], i["L0_xattn_" + name]).then_inc(ab_w_in[n], 16)
                        sp.dma_start(wu[:, :, :], i["L0_xattn_Wu"].rearrange("(j p) n -> p j n", p=P))\
                          .then_inc(ab_w_in[3], 16)
                        for t, name in ((bq, "bq"), (bk, "bk"), (bv, "bv")):
                            sp.dma_start(t[:, :], i["L0_xattn_" + name]).then_inc(ab_b_in, 16)
                        sp.dma_start(bu[:, :], i["L0_xattn_bu"].rearrange("(p a) -> p a", a=1)).then_inc(ab_b_in, 16)
                        sp.dma_start(wg[:, :], i["L0_ffn_Wg"]).then_inc(ab_b_in, 16)

                    constants(nc, sem, load_all, ident, table, quad_scale, head_mask, vx, rel_i, rel, mask16, power, eps,
                              one)
                    self_attention(nc, sem, sb1, ps, wqkv, wout, sa_w_in, x_in, x_rest, act, stats, ident, table,
                                   quad_scale, head_mask, vx)

                def zero_cpad():
                    nc.gpsimd.memset(cpad[:, :, :, :], 0.0).then_inc(cpad_zero, 1)

                def first_context(sp):
                    load_cn(nc, sp, i["ctx_1024"], cn, cn_in, 0)
                    sp.wait_ge(cpad_zero, 1)
                    load_cpad(nc, sp, i["ctx_1024"], cpad, cpad_in, 0)

                with ExitStack() as inner:
                    absorb_weights(nc, sem, allocator(inner), ps, raw, wu, bq, bk, bv, bu, ab_w_in, ab_b_in, ident,
                                   a_hi, a_lo, b_vec, n_hi, n_lo, y_bias, stats, mean, var, rstd, power,
                                   zero_cpad, first_context)
            cross_attention(nc, sem, sb2, ps, i["ctx_1024"], cn, cpad, cn_in, cpad_in, act, mean, rstd, ident,
                            a_hi, a_lo, b_vec, n_hi, n_lo, y_bias, power, eps, one, {n: i["L0_ffn_" + n] for n in (
                                "Ws1", "Ws3", "Ws2", "We1", "We3", "We2")}, ff_hi, ff_lo)

        with ExitStack() as phase:
            sb3 = allocator(phase)
            x_hi, x_lo = (sb3(n, [P, GROUPS, TILES * P], F32R) for n in ("x_hi", "x_lo"))
            with ExitStack() as inner:
                router(nc, sem, allocator(inner), ps, act, ident, wg, x_hi, x_lo, wt_dram, wt_stored)
            w1, w3, w2 = ((ff_hi[:, n, :], ff_lo[:, n, :]) for n in range(3))
            experts(nc, sem, sb3, ps, act, ident, power, eps, w1, w3, w2, x_hi, x_lo, wt_dram, wt_stored, out)


_INS = ["x", "ctx_1024", "L0_attn_Wqkv", "L0_attn_Wout", "L0_xattn_Wq", "L0_xattn_bq", "L0_xattn_Wk", "L0_xattn_bk",
        "L0_xattn_Wv", "L0_xattn_bv", "L0_xattn_Wu", "L0_xattn_bu", "L0_ffn_Wg", "L0_ffn_Ws1", "L0_ffn_Ws3",
        "L0_ffn_Ws2", "L0_ffn_We1", "L0_ffn_We3", "L0_ffn_We2"]


def kernel(**inputs):
    import concourse.bacc as bacc
    from concourse.bass_utils import run_bass_kernel_spmd

    nc = bacc.Bacc("TRN2", target_bir_lowering=False, num_devices=1)
    arrays, aps = {}, {}
    for name in _INS:
        a = np.asarray(inputs[name])
        if name.endswith(("bq", "bk", "bv")):
            a = a.reshape(-1, P).T
        a = np.ascontiguousarray(a)
        arrays[f"in_{name}"] = a
        aps[name] = nc.dram_tensor(f"in_{name}", a.shape, mybir.dt.from_np(a.dtype), kind="ExternalInput").ap()
    out = nc.dram_tensor("out", (B, T, D), F32, kind="ExternalOutput").ap()
    wt_dram = nc.dram_tensor("gate_weights", (PAIRS, E, P), F32, kind="Internal").ap()
    decoder_layer(nc, aps, out, wt_dram)
    result = run_bass_kernel_spmd(nc, [arrays], core_ids=[0])
    return result.results[0]["out"]
```

```python
import math
from contextlib import ExitStack

import numpy as np

import concourse.bass as bass
from concourse import mybir

F32 = mybir.dt.float32
F32R = mybir.dt.float32r
I32 = mybir.dt.int32
ALU = mybir.AluOpType
ACT = mybir.ActivationFunctionType
AX = mybir.AxisListType
ds = bass.ds

P = 128
B, T, D = 64, 64, 128
PAIRS = B // 2
H = 16
HD = D // H
HK = 64
E, FF = 8, 256
EPS = 1e-5
FIRST_PAIRS = 4
MASKED = -1e30
SA_SCALE = 1.0 / math.sqrt(HD)
CA_SCALE = 1.0 / math.sqrt(HK)
SLOPES = [float(np.float32(2.0 ** (-8.0 * (h + 1) / H))) for h in range(H)]


def heads(ap):
    return ap.rearrange("p (h k) -> p h k", k=T)


def over_keys(ap, n=T):
    return ap.unsqueeze(2).broadcast_to((ap.shape[0], ap.shape[1], n))


def constants(nc, sem, load_first, ident, table, quad_scale, head_mask, parity, rel_i, rel, mask16, power, eps,
              one):
    set_v, set_g = sem("const_dve"), sem("const_pool")
    with nc.Block() as block:

        @block.sync
        def _(sp):
            load_first(sp)

        @block.vector
        def _(dve):
            nc.vector.memset(ident[:, :], 0.0).then_inc(set_v, 1)
            nc.vector.memset(mask16[:, :], 1.0).then_inc(set_v, 1)
            nc.vector.memset(quad_scale[:, :], 0.0).then_inc(set_v, 1)
            nc.vector.memset(parity[:, :], 0.0).then_inc(set_v, 1)
            dve.wait_ge(set_v, 4)
            for h2 in range(2):
                nc.vector.memset(parity[64 * h2:64 * h2 + 64, h2:h2 + 1], 1.0).then_inc(set_v, 1)
            for g in range(4):
                nc.vector.memset(quad_scale[32 * g:32 * g + 32, g:g + 1], SA_SCALE).then_inc(set_v, 1)
            dve.wait_ge(set_g, 2)
            nc.vector.tensor_copy(rel[:, :], rel_i[:, :]).then_inc(set_v, 1)
            dve.wait_ge(set_v, 11)
            for h in range(H):
                nc.vector.tensor_scalar(table[:, h, :], rel[:, :], SLOPES[h], None, ALU.mult).then_inc(set_v, 1)
            for t, value in ((power, -0.5), (eps, EPS), (one, 1.0)):
                nc.vector.memset(t[:, :], value).then_inc(set_v, 1)
            dve.wait_ge(set_g, 5)
            nc.vector.tensor_reduce(head_mask[:, :], mask16[:, :].rearrange("p (g h) -> p h g", g=4),
                                    AX.X, ALU.add).then_inc(set_v, 1)

        @block.gpsimd
        def _(pool):
            for b in range(2):
                if b:
                    pool.wait_ge(set_g, 1)
                nc.gpsimd.iota(rel_i[64 * b:64 * b + 64, :], pattern=[[1, T]], base=0,
                               channel_multiplier=-1).then_inc(set_g, 1)
            pool.wait_ge(set_v, 3)
            pool.wait_ge(set_g, 2)
            nc.gpsimd.affine_select(out=ident[:, :], in_=ident[:, :], compare_op=ALU.not_equal, fill=1.0,
                                    base=0, pattern=[[-1, P]], channel_multiplier=1).then_inc(set_g, 1)
            nc.gpsimd.affine_select(out=mask16[:, :], in_=mask16[:, :], compare_op=ALU.is_ge, fill=0.0,
                                    base=0, pattern=[[-HD, H]], channel_multiplier=1).then_inc(set_g, 1)
            pool.wait_ge(set_g, 4)
            nc.gpsimd.affine_select(out=mask16[:, :], in_=mask16[:, :], compare_op=ALU.is_ge, fill=0.0,
                                    base=HD - 1, pattern=[[HD, H]], channel_multiplier=-1).then_inc(set_g, 1)


def self_attention(nc, sem, sb, ps, load_rest, wqkv, wout, w_in, x_in, x_rest, act, stats, ident, table, quad_scale, head_mask, parity):
    xs = sb("sa_xs", [P, D])
    xt = sb("sa_xt", [P, 2, 2, T])
    qm = sb("sa_qm", [P, 4, P])
    km = sb("sa_km", [P, 2, 4, T])
    logit = [sb(f"sa_logit{n}", [P, H * T]) for n in range(2)]
    under = sb("sa_under", [P, H * T])
    prob = sb("sa_prob", [P, H * T])
    top = [sb(f"sa_top{n}", [P, H]) for n in range(2)]
    pt = sb("sa_pt", [P, H // 2, P])
    v_all = sb("sa_v_all", [P, PAIRS, 2 * H // 2, HD])
    VW = 2 * HD
    vx = sb("sa_vx", [P, 2 * H // 2, 2, VW])
    av_t = sb("sa_av_t", [P, 2 * P])
    rsum = sb("sa_rsum", [P, H])
    o = sb("sa_o", [P, H, HD])
    ot = sb("sa_ot", [P, P])
    ps_x, ps_qkv, ps_s0, ps_s1, ps_p0, ps_p1, ps_av, ps_o = ps
    ps_p = (ps_p0, ps_p1)
    ps_s = (ps_s0, ps_s1)
    av = ps_av[:, 2 * P:4 * P].rearrange("p (h d) -> p h d", h=H)

    s = {n: sem("sa_" + n) for n in (
        "xs", "xt_ps", "xt", "qkv", "qm", "km", "v", "score", "logit", "top", "shift", "prob",
        "pt_ps", "pt", "av", "rsum", "o", "ot_ps", "ot", "y_ps", "y", "st", "causal", "vx_fixed", "vx", "av_t", "av_ps")}

    def has(i, back):
        return not isinstance(i, int) or 0 <= i - back < PAIRS

    def later(i, back):
        return not isinstance(i, int) or i > back

    def pipeline(eng, body):
        for i in range(6):
            body(i, i % 2)
        with eng.Fori(3, PAIRS // 2 - 1) as k:
            body(k * 2, 0)
            body(k * 2 + 1, 1)
        for i in range(PAIRS - 2, PAIRS + 5):
            body(i, i % 2)

    with nc.Block() as block:

        @block.sync
        def _(sp):
            load_rest(sp)

        @block.tensor
        def _(pe):
            pe.wait_ge(w_in, 32)

            def body(i, n):
                if has(i, 0):
                    pe.wait_ge(s["xs"], i + 1)
                    if later(i, 0):
                        pe.wait_ge(s["v"], i * 2)
                    nc.tensor.transpose(ps_x[:, 0:P], xs[:, :], ident[:, :]).then_inc(s["xt_ps"], 1)
                if has(i, 4):
                    pe.wait_ge(s["av_t"], i - 3)
                    for half in range(2):
                        ins = nc.tensor.transpose(ps_av[:, P * (2 + half):P * (3 + half)],
                                                  av_t[:, P * half:P * half + P], ident[:, :])
                    ins.then_inc(s["av_ps"], 1)
                if has(i, 1):
                    pe.wait_ge(s["qm"], i)
                    pe.wait_ge(s["km"], i)
                    if later(i, 1):
                        pe.wait_ge(s["logit"], i * 2 - 2)
                    for g in range(4):
                        for b in range(2):
                            ins = nc.tensor.matmul(ps_s[g // 2][64 * b:64 * b + 64, 256 * (g % 2):256 * (g % 2) + 256],
                                                   qm[:, g, 64 * b:64 * b + 64],
                                                   km[:, b, :, :].rearrange("p h k -> p (h k)"), start=True, stop=True)
                        if g % 2:
                            ins.then_inc(s["score"], 1)
                if has(i, 0):
                    pe.wait_ge(s["xt"], i + 1)
                    if later(i, 0):
                        pe.wait_ge(s["qm"], i)
                        pe.wait_ge(s["km"], i)
                    for n in range(2):
                        nc.tensor.matmul(ps_qkv[:, P * n:P * n + P], wqkv[:, D * n:D * n + D], xt[:, :, 0, :],
                                         start=True, stop=True)
                    for b in range(2):
                        ins = nc.tensor.matmul(ps_x[:, P * (2 + b):P * (3 + b)],
                                               xt[:, b, :, :].rearrange("p c t -> p (c t)"),
                                               wqkv[:, 2 * D:3 * D], start=True, stop=True)
                    ins.then_inc(s["qkv"], 1)
                if has(i, 4):
                    pe.wait_ge(s["o"], i - 3)
                    if later(i, 4):
                        pe.wait_ge(s["y"], i - 4)
                    nc.tensor.transpose(ps_o[:, 0:P], o[:, :, :].rearrange("p h d -> p (h d)"),
                                        ident[:, :]).then_inc(s["ot_ps"], 1)
                if has(i, 3):
                    pe.wait_ge(s["vx"], i - 2)
                    if later(i, 3):
                        pe.wait_ge(s["o"], i - 3)
                    for half in range(2):
                        pe.wait_ge(s["pt"], i * 2 - 5 + half)
                        for b in range(2):
                            for j4 in range(4):
                                ins = nc.tensor.matmul(
                                    ps_av[32 * j4:32 * j4 + 32, P * half + T * b:P * half + T * b + T],
                                    vx[:, 8 * b + 4 * half + j4, :, :].rearrange("p h d -> p (h d)"),
                                    pt[:, 4 * half + j4, T * b:T * b + T], start=True, stop=True)
                    ins.then_inc(s["av"], 1)
                if has(i, 4):
                    pe.wait_ge(s["ot"], i - 3)
                    nc.tensor.matmul(ps_o[:, P:2 * P], ot[:, :], wout[:, :], start=True, stop=True).then_inc(s["y_ps"], 1)
                if has(i, 2):
                    for half in range(2):
                        pe.wait_ge(s["prob"], i * 2 - 3 + half)
                        if later(i, 2):
                            pe.wait_ge(s["pt"], i * 2 - 5 + half)
                        for j in range(4):
                            ins = nc.tensor.transpose(ps_p[half][:, P * j:P * j + P],
                                                      prob[:, P * (4 * half + j):P * (4 * half + j + 1)], ident[:, :])
                        ins.then_inc(s["pt_ps"], 1)

            pipeline(pe, body)

        @block.vector
        def _(dve):
            def copy_x(i):
                nc.vector.tensor_scalar(xs[:, :].unsqueeze(1), act[:, ds(i, 1), :], 1.0, None,
                                        ALU.mult).then_inc(s["xs"], 1)

            dve.wait_ge(x_in, 16)
            copy_x(0)

            def body(i, n):
                if has(i, 4):
                    dve.wait_ge(s["av_ps"], i - 3)
                    nc.vector.reciprocal(rsum[:, :], av[:, :, HD]).then_inc(s["rsum"], 1)
                if has(i, 5):
                    dve.wait_ge(s["y"], i - 4)
                    nc.vector.bn_stats(stats[:, ds(i - 5, 1), :], act[:, ds(i - 5, 1), :]).then_inc(s["st"], 1)
                if has(i, 0) and has(i, -1):
                    dve.wait_ge(s["xt_ps"], i + 1)
                    if isinstance(i, int) and i + 1 == FIRST_PAIRS:
                        dve.wait_ge(x_rest, 16)
                    copy_x(i + 1)
                if has(i, 4):
                    dve.wait_ge(s["rsum"], i - 3)
                    if later(i, 4):
                        dve.wait_ge(s["ot_ps"], i - 4)
                    nc.vector.tensor_tensor(o[:, :, :], av[:, :, 0:HD], over_keys(rsum[:, :], HD),
                                            ALU.mult).then_inc(s["o"], 1)
                if isinstance(i, int) and i == 1:
                    dve.wait_ge(s["causal"], 2)
                if has(i, 1):
                    for half in range(2):
                        dve.wait_ge(s["score"], i * 2 - 1 + half)
                        if half == 0 and later(i, 2):
                            dve.wait_ge(s["shift"], i - 2)
                        nc.vector.tensor_tensor(heads(logit[1 - n][:, 512 * half:512 * half + 512]),
                                                heads(ps_s[half][:, :]), table[:, 8 * half:8 * half + 8, :],
                                                ALU.add).then_inc(s["logit"], 1)
                if has(i, 0):
                    dve.wait_ge(s["qkv"], i + 1)
                    if later(i, 0):
                        dve.wait_ge(s["score"], i * 2)
                    nc.vector.tensor_tensor(km[:, :, :, :],
                                            ps_qkv[:, P:2 * P].rearrange("p (b k) -> p b k", b=2).unsqueeze(2)
                                            .broadcast_to((P, 2, 4, T)),
                                            head_mask[:, :].unsqueeze(1).unsqueeze(3).broadcast_to((P, 2, 4, T)),
                                            ALU.mult).then_inc(s["km"], 1)
                    nc.vector.tensor_tensor(qm[:, :, :], ps_qkv[:, 0:P].unsqueeze(1).broadcast_to((P, 4, P)),
                                            over_keys(quad_scale[:, :], P), ALU.mult).then_inc(s["qm"], 1)
                if has(i, 1):
                    dve.wait_ge(s["logit"], i * 2)
                    nc.vector.tensor_reduce(top[1 - n][:, :], heads(logit[1 - n][:, :]), AX.X, ALU.max).then_inc(s["top"], 1)
                if has(i, 4):
                    dve.wait_ge(s["y_ps"], i - 3)
                    nc.vector.tensor_tensor(act[:, ds(i - 4, 1), :], act[:, ds(i - 4, 1), :],
                                            ps_o[:, P:2 * P].unsqueeze(1), ALU.add).then_inc(s["y"], 1)

            pipeline(dve, body)

        @block.gpsimd
        def _(pool):
            def shift(i, n):
                pool.wait_ge(s["top"], i + 1)
                if later(i, 0):
                    pool.wait_ge(s["prob"], i * 2)
                nc.gpsimd.tensor_tensor(heads(under[:, :]), heads(logit[n][:, :]), over_keys(top[n][:, :]),
                                        ALU.subtract).then_inc(s["shift"], 1)

            for b in range(2):
                if b:
                    pool.wait_ge(s["causal"], 1)
                part = table[64 * b:64 * b + 64, :, :]
                nc.gpsimd.affine_select(out=part, in_=part, compare_op=ALU.is_ge, fill=MASKED,
                                        base=0, pattern=[[0, H], [-1, T]], channel_multiplier=1)\
                  .then_inc(s["causal"], 1)
            pool.wait_ge(s["causal"], 2)
            nc.gpsimd.memset(vx[:, :, :, :], 0.0).then_inc(s["vx_fixed"], 1)
            pool.wait_ge(s["vx_fixed"], 1)
            nc.gpsimd.memset(vx[:, :, :, HD], 1.0).then_inc(s["vx_fixed"], 1)
            pool.wait_ge(s["vx_fixed"], 2)
            nc.gpsimd.tensor_tensor(vx[:, :, :, HD], vx[:, :, :, HD],
                                    parity[:, :].unsqueeze(1).broadcast_to((P, H, 2)), ALU.mult).then_inc(s["vx_fixed"], 1)
            pool.wait_ge(s["vx_fixed"], 3)

            def spread(i):
                pool.wait_ge(s["v"], i * 2 + 2)
                if later(i, 0):
                    pool.wait_ge(s["av"], i)
                shape = (P, H, 2, HD)
                nc.gpsimd.tensor_tensor(vx[:, :, :, 0:HD],
                                        v_all[:, ds(i, 1), :, :].rearrange("p i n d -> p (i n) d").unsqueeze(2)
                                        .broadcast_to(shape),
                                        parity[:, :].unsqueeze(1).unsqueeze(3).broadcast_to(shape),
                                        ALU.mult).then_inc(s["vx"], 1)

            shift(0, 0)
            shift(1, 1)
            spread(0)
            with pool.Fori(1, PAIRS // 2) as k:
                for n in range(2):
                    shift(k * 2 + n, n)
                    spread(k * 2 + n - 1)
            spread(PAIRS - 1)

        @block.scalar
        def _(actv):
            actv.preload_act_table(ACT.Exp)

            def body(i, n):
                if has(i, 3):
                    for half in range(2):
                        actv.wait_ge(s["pt_ps"], i * 2 - 5 + half)
                        if half == 0 and later(i, 3):
                            actv.wait_ge(s["av"], i - 3)
                        nc.scalar.activation(pt[:, 4 * half:4 * half + 4, :].rearrange("p j q -> p (j q)"),
                                             ps_p[half][:, :], ACT.Copy).then_inc(s["pt"], 1)
                if has(i, 0):
                    actv.wait_ge(s["xt_ps"], i + 1)
                    if later(i, 0):
                        actv.wait_ge(s["qkv"], i)
                    nc.scalar.activation(xt[:, :, :, :],
                                         ps_x[:, 0:P].rearrange("p (b t) -> p b t", b=2).unsqueeze(2)
                                         .broadcast_to((P, 2, 2, T)), ACT.Copy).then_inc(s["xt"], 1)
                if has(i, 2):
                    actv.wait_ge(s["shift"], i - 1)
                    if later(i, 2):
                        actv.wait_ge(s["pt_ps"], i * 2 - 4)
                    for half in range(2):
                        part = slice(512 * half, 512 * half + 512)
                        nc.scalar.activation(prob[:, part], under[:, part], ACT.Exp).then_inc(s["prob"], 1)
                if has(i, 4):
                    actv.wait_ge(s["ot_ps"], i - 3)
                    if later(i, 4):
                        actv.wait_ge(s["y_ps"], i - 4)
                    nc.scalar.activation(ot[:, :], ps_o[:, 0:P], ACT.Copy).then_inc(s["ot"], 1)
                if has(i, 0):
                    actv.wait_ge(s["qkv"], i + 1)
                    for h2 in range(2):
                        r = slice(64 * h2, 64 * h2 + 64)
                        nc.scalar.activation(
                            v_all[r, ds(i, 1), :, :],
                            ps_x[r, 2 * P:4 * P].rearrange("p (b j h d) -> p (b j) h d", b=2, j=8, h=2)[:, :, h2, :]
                            .unsqueeze(1), ACT.Copy).then_inc(s["v"], 1)
                if has(i, 3):
                    actv.wait_ge(s["av"], i - 2)
                    if later(i, 3):
                        actv.wait_ge(s["av_ps"], i - 3)
                    nc.scalar.activation(av_t[:, :], ps_av[:, 0:2 * P], ACT.Copy).then_inc(s["av_t"], 1)

            pipeline(actv, body)


def absorb_weights(nc, sem, sb, ps, raw, wu, bq, bk, bv, bu, w_in, b_in, ident, a_hi, a_lo, b_vec, n_hi, n_lo,
                   y_bias, stats, mean, var, rstd, power, zero_cpad, first_context):
    tr = [sb(f"ab_tr{n}", [P, H // 2, P]) for n in range(3)]
    corr = sb("ab_corr", [P, H // 2])
    bk2 = sb("ab_bk2", [P, H // 2, 2])
    ln, ln_rstd = sem("ln1_var"), sem("ln1_rstd")
    even, odd = stats[:, :, 1], stats[:, :, 4]
    tr_ps, tr_act, tr_dve, corr_d, wq_ok = (sem("ab_" + n) for n in ("tr_ps", "tr_act", "tr_dve", "corr", "wq"))
    prod_ps, prod_hi, prod_lo, vec_ps, vec_ok = (sem("ab_" + n) for n in ("prod_ps", "hi", "lo", "vec_ps", "vec"))

    TURN = (0, 2, 1)
    fills = [(n, h2, 4 * half) for n in (1, 0) for half in range(2) for h2 in range(2)]

    def dest(pair, h2, j0):
        return pair[:, :, :].rearrange("c (j h) e -> c j h e", h=2)[:, j0:j0 + 4, h2, :]

    with nc.Block() as block:

        @block.sync
        def _(sp):
            first_context(sp)

        @block.gpsimd
        def _(pool):
            zero_cpad()
            pool.wait_ge(ln, 7)
            nc.gpsimd.tensor_tensor(rstd[:, :], var[:, :], power[:, :], ALU.pow).then_inc(ln_rstd, 1)

        @block.tensor
        def _(pe):
            for f in range(6):
                if f % 2 == 0:
                    pe.wait_ge(w_in[TURN[f // 2]], 16)
                if f >= 4:
                    pe.wait_ge((tr_act, tr_dve)[f % 2], (f - 4) // 2 + 1)
                for j in range(4):
                    c = P * (4 * (f % 2) + j)
                    ins = nc.tensor.transpose(ps[f % 4][:, P * j:P * j + P], raw[TURN[f // 2]][:, c:c + P],
                                              ident[:, :])
                ins.then_inc(tr_ps, 1)
            pe.wait_ge(w_in[3], 16)
            pe.wait_ge(tr_act, 2)
            pe.wait_ge(tr_dve, 2)
            for k, (n, h2, j0) in enumerate(fills):
                if k == 4:
                    pe.wait_ge(b_in, 80)
                    for j in range(8):
                        nc.tensor.matmul(ps[3][:, 0:1], wu[:, j, :], bv[:, j:j + 1], start=(j == 0), stop=(j == 7))
                    pe.wait_ge(wq_ok, 1)
                    pe.wait_ge(tr_act, 3)
                    pe.wait_ge(tr_dve, 3)
                if k >= 4:
                    pe.wait_ge(prod_lo, k - 3)
                r = slice(64 * h2, 64 * h2 + 64)
                left, right = ((tr[1], tr[0]), (tr[2], wu))[n]
                for j in range(4):
                    ins = nc.tensor.matmul(ps[4 + k % 4][:, P * j:P * j + P], left[r, j0 + j, :], right[r, j0 + j, :],
                                           start=True, stop=True)
                ins.then_inc(prod_ps, 1)
            pe.wait_ge(vec_ok, 3)
            for j in range(8):
                ins = nc.tensor.matmul(ps[0][:, 2 * j:2 * j + 2], tr[0][:, j, :], bk2[:, j, :], start=True, stop=True)
            ins.then_inc(vec_ps, 1)

        @block.scalar
        def _(actv):
            actv.preload_act_table(ACT.Exp)
            for n in range(3):
                actv.wait_ge(tr_ps, 2 * n + 1)
                nc.scalar.activation(tr[TURN[n]][:, 0:4, :].rearrange("p j e -> p (j e)"), ps[2 * n % 4][:, :],
                                     ACT.Copy).then_inc(tr_act, 1)
            for k, (n, h2, j0) in enumerate(fills):
                actv.wait_ge(prod_ps, k + 1)
                nc.scalar.activation(dest((a_hi, n_hi)[n], h2, j0), ps[4 + k % 4][:, :].rearrange("c (j e) -> c j e", j=4),
                                     ACT.Copy).then_inc(prod_hi, 1)

        @block.vector
        def _(dve):
            nc.vector.tensor_tensor(mean[:, :], even, odd, ALU.add).then_inc(ln, 1)
            nc.vector.tensor_tensor(rstd[:, :], even, odd, ALU.subtract).then_inc(ln, 1)
            nc.vector.tensor_tensor(var[:, :], stats[:, :, 2], stats[:, :, 5], ALU.add).then_inc(ln, 1)
            dve.wait_ge(ln, 3)
            nc.vector.tensor_scalar(mean[:, :], mean[:, :], 0.5, None, ALU.mult).then_inc(ln, 1)
            nc.vector.tensor_tensor(rstd[:, :], rstd[:, :], rstd[:, :], ALU.mult).then_inc(ln, 1)
            nc.vector.tensor_scalar(var[:, :], var[:, :], 1.0 / D, EPS, ALU.mult, ALU.add).then_inc(ln, 1)
            dve.wait_ge(ln, 6)
            nc.vector.scalar_tensor_tensor(out=var[:, :], in0=rstd[:, :], scalar=0.25, in1=var[:, :],
                                           op0=ALU.mult, op1=ALU.add).then_inc(ln, 1)
            def transposed(n):
                dve.wait_ge(tr_ps, 2 * n + 2)
                nc.vector.tensor_copy(tr[TURN[n]][:, 4:8, :].rearrange("p j e -> p (j e)"),
                                      ps[(2 * n + 1) % 4][:, :]).then_inc(tr_dve, 1)

            nc.vector.memset(bk2[:, :, :], 0.0).then_inc(vec_ok, 1)
            transposed(0)
            transposed(1)
            dve.wait_ge(b_in, 80)
            dve.wait_ge(vec_ok, 1)
            for h2 in range(2):
                r = slice(64 * h2, 64 * h2 + 64)
                nc.vector.tensor_copy(bk2[r, :, h2], bk[r, :]).then_inc(vec_ok, 1)
            dve.wait_ge(tr_act, 1)
            dve.wait_ge(tr_dve, 1)
            nc.vector.tensor_reduce(corr[:, :], tr[0][:, :, :], AX.X, ALU.add).then_inc(corr_d, 1)
            transposed(2)
            dve.wait_ge(corr_d, 1)
            dve.wait_ge(b_in, 80)
            nc.vector.tensor_tensor(corr[:, :], bq[:, :], corr[:, :], ALU.subtract).then_inc(corr_d, 1)
            dve.wait_ge(corr_d, 2)
            nc.vector.tensor_scalar(corr[:, :], corr[:, :], CA_SCALE / D, None, ALU.mult).then_inc(corr_d, 1)
            dve.wait_ge(corr_d, 3)
            nc.vector.scalar_tensor_tensor(out=tr[0][:, :, :], in0=tr[0][:, :, :], scalar=CA_SCALE,
                                           in1=over_keys(corr[:, :], D), op0=ALU.mult, op1=ALU.add).then_inc(wq_ok, 1)
            for k, (n, h2, j0) in enumerate(fills):
                dve.wait_ge(prod_hi, k + 1)
                hi = dest((a_hi, n_hi)[n], h2, j0)
                nc.vector.tensor_tensor(dest((a_lo, n_lo)[n], h2, j0), ps[4 + k % 4][:, :].rearrange("c (j e) -> c j e", j=4),
                                        hi.bitcast(F32), ALU.subtract).then_inc(prod_lo, 1)
            dve.wait_ge(vec_ps, 1)
            nc.vector.tensor_copy(b_vec[:, :], ps[0][:, 0:H]).then_inc(vec_ok, 1)
            nc.vector.tensor_tensor(y_bias[:, :], ps[3][:, 0:1], bu[:, :], ALU.add).then_inc(vec_ok, 1)


STEPS = PAIRS // 2
TILES = 4
GROUPS = PAIRS // TILES
UNITS = (E + 1) * FF // P
GATE_STEPS = 18
EARLY = 28


def load_cn(nc, sp, ctx, cn, cn_in, i):
    sp.dma_start(cn[:, :, :], ctx.rearrange("(i b) k d -> (b k) i d", b=2)[:, ds(i * 2, 2), :]).then_inc(cn_in, 16)


def load_cpad(nc, sp, ctx, cpad, cpad_in, i):
    for half in range(2):
        sp.dma_start(cpad[64 * half:64 * half + 64, :, half, :],
                     ctx.rearrange("b k d -> k b d")[:, ds(i * 4, 4), :]).then_inc(cpad_in, 16)


def cross_attention(nc, sem, sb, ps, ctx, cn, cpad, cn_in, cpad_in, act, mean, rstd, ident, a_hi, a_lo, b_vec, n_hi, n_lo, y_bias,
                    power, eps, one, ff, ff_hi, ff_lo, wg, g, x0_hi, x0_lo, wt_dram,
                    wt_stored):
    xs = sb("ca_xs", [P, 2, D])
    xt = sb("ca_xt", [P, 2, P])
    ct_hi, ct_lo = sb("ca_ct_hi", [P, 2 * P], F32R), sb("ca_ct_lo", [P, 2 * P], F32R)
    keys = sb("ca_keys", [P, H, 2 * P])
    prob = [sb(f"ca_prob{n}", [P, H * T]) for n in range(2)]
    top, rsum = sb("ca_top", [P, 2, H]), sb("ca_rsum", [P, 2, H])
    pt_hi, pt_lo = ([sb(f"ca_pt_{part}{n}", [P, H // 2, P], F32R) for n in range(2)] for part in ("hi", "lo"))
    c_hi, c_lo = (sb("ca_c_" + part, [P, 4, 2, D], F32R) for part in ("hi", "lo"))
    r_hi, r_lo = sb("ca_r_hi", [P, H, 2 * P], F32R), sb("ca_r_lo", [P, H, 2 * P], F32R)
    yt = sb("ca_yt", [P, 2 * P])
    y = sb("ca_y", [P, 2, D])
    y_stats, moments = sb("ca_y_stats", [P, 2, 6]), sb("ca_moments", [P, 2, 2])
    y_rstd = sb("ca_y_rstd", [P, 2])
    x2t = sb("ca_x2t", [P, 2 * P])
    w_raw = sb("ca_w_raw", [P, 3, FF])
    w_hi, w_lo = (w[:, :, :].rearrange("p n (e f) -> p n e f", f=FF) for w in (ff_hi, ff_lo))
    ring = (ps[0:2], ps[2:4])
    ps_s, ps_y, ps_t = ps[4:6], ps[6], ps[7]
    early = slice(0, EARLY)
    g = {**g, **{n: keys[:, k, :].rearrange("p (t e) -> p t e", e=E) for k, n in enumerate(SCRATCH)}}
    sel_rows = (slice(0, P), slice(P, EARLY * E))

    s = {n: sem("ca_" + n) for n in (
        "xn", "xs", "t_ps", "xt", "ct_hi", "ct_lo", "g_ps", "g_act", "g_dve",
        "score", "top", "shift", "exp", "sum", "rsum", "norm", "pt_ps", "pt_hi", "pt_lo", "c_hi", "c_lo",
        "r_ps", "r_hi", "r_lo", "y_ps", "yt", "yt_ps", "y", "st", "var", "eps", "rstd", "x2", "xa", "w_in", "w_hi", "w_lo",
        "x2_ps", "x2t", "l_ps", "logits", "l_exp", "keep", "gates", "wt_ps", "wt",
        "x0_ps", "x0_hi", "x0_lo")}

    order = [("pt", 0), ("g", 0), ("r", 0), ("r", 2), ("g", 1), ("pt", 1), ("g", 2), ("g", 3), ("r", 4), ("r", 6)]

    def free(pe, which, pos, i):
        def exists(kind, i):
            return not isinstance(i, int) or (i < STEPS if kind == "g" else i >= 1) and i >= 0
        back, at = i, pos - 2
        while True:
            if at < 0:
                back, at = back - 1, at + len(order)
            if isinstance(back, int) and back < 0:
                return
            if exists(order[at][0], back):
                break
            at -= 2
        kind, n = order[at]
        if kind == "g":
            pe.wait_ge(s[("g_act", "g_dve")[which]], back * 4 + n + 1)
        elif kind == "pt":
            pe.wait_ge(s["pt_lo"], back * 4 - 4 + 2 * n + which + 1)
        else:
            pe.wait_ge(s["r_lo"], back * 8 - 8 + n + which + 1)

    def position(kind, n):
        return order.index((kind, n))

    def pipeline(eng, body):
        for i in range(3):
            body(i)
        with eng.Fori(3, STEPS - 1) as i:
            body(i)
        for i in range(STEPS - 1, STEPS + 3):
            body(i)

    def spans(i):
        if isinstance(i, int):
            return i < STEPS, 1 <= i <= STEPS, 2 <= i <= STEPS + 1, 3 <= i
        return True, True, True, True

    def past(i, n):
        return not isinstance(i, int) or i > n

    def has_next(i):
        return not isinstance(i, int) or i + 1 < STEPS

    with nc.Block() as block:

        @block.sync
        def _(sp):
            def expert_weights(w1, w3, w2):
                for n, w in enumerate((w1, w3)):
                    sp.dma_start(w_raw[:, n, :].unsqueeze(1), w).then_inc(s["w_in"], 16)
                sp.dma_start(w_raw[:, 2, :].rearrange("p (c d) -> p c d", d=D).unsqueeze(1), w2).then_inc(s["w_in"], 16)

            expert_weights(ff["Ws1"].unsqueeze(1), ff["Ws3"].unsqueeze(1),
                           ff["Ws2"].rearrange("(c p) d -> p c d", p=P).unsqueeze(1))
            def body(i, e=None):
                if past(i, 0):
                    sp.wait_ge(s["t_ps"], i)
                    load_cn(nc, sp, ctx, cn, cn_in, i)
                    sp.wait_ge(s["c_lo"], i)
                    load_cpad(nc, sp, ctx, cpad, cpad_in, i)
                if e is not None:
                    sp.wait_ge(s["w_lo"], e + 1)
                    expert_weights(ff["We1"].rearrange("e d f -> d e f")[:, ds(e, 1), :],
                                   ff["We3"].rearrange("e d f -> d e f")[:, ds(e, 1), :],
                                   ff["We2"].rearrange("e (c p) d -> p e c d", p=P)[:, ds(e, 1), :, :])

            body(0, 0)
            with sp.Fori(1, E) as i:
                body(i, i)
            with sp.Fori(E, STEPS) as i:
                body(i)
            sp.wait_ge(s["wt"], 2)
            for n, rows in enumerate(sel_rows):
                store_weights(sp, wt_dram, g, n, rows, wt_stored)

        @block.tensor
        def _(pe):
            def transpose_in(i):
                pe.wait_ge(s["xs"], i * 2 + 2)
                pe.wait_ge(cn_in, i * 16 + 16)
                if past(i, 0):
                    pe.wait_ge(s["xt"], i)
                    pe.wait_ge(s["ct_lo"], i)
                if past(i, 2):
                    pe.wait_ge(s["y"], i - 2)
                for p in range(2):
                    nc.tensor.transpose(ps_t[:, P * p:P * p + P], xs[:, p, :], ident[:, :])
                for p in range(2):
                    ins = nc.tensor.transpose(ps_t[:, P * (2 + p):P * (3 + p)], cn[:, p, :], ident[:, :])
                ins.then_inc(s["t_ps"], 1)

            def absorbed_keys(i, fills):
                if fills[0] == 0:
                    pe.wait_ge(s["ct_hi"], i + 1)
                    pe.wait_ge(s["ct_lo"], i + 1)
                for f in fills:
                    which, n = f % 2, f // 2
                    pos = position("g", n)
                    free(pe, which, pos, i)
                    for h in (2 * f, 2 * f + 1):
                        out = ring[which][pos % 2][:, 256 * (h % 2):256 * (h % 2) + 256]
                        nc.tensor.matmul(out, a_hi[:, h, :], ct_hi[:, :], start=True, stop=False)
                        nc.tensor.matmul(out, a_lo[:, h, :], ct_hi[:, :], start=False, stop=False)
                        ins = nc.tensor.matmul(out, a_hi[:, h, :], ct_lo[:, :], start=False, stop=True)
                    ins.then_inc(s["g_ps"], 1)

            def scores(i, p):
                if p == 0:
                    pe.wait_ge(s["xt"], i + 1)
                    pe.wait_ge(s["g_act"], i * 4 + 4)
                    pe.wait_ge(s["g_dve"], i * 4 + 4)
                if p or past(i, 0):
                    pe.wait_ge(s["shift"], i * 2 + p)
                for half in range(2):
                    for b in range(2):
                        c = P * p + T * b
                        ins = nc.tensor.matmul(ps_s[half][T * b:T * b + T, :], xt[:, p, T * b:T * b + T],
                                               keys[:, 8 * half:8 * half + 8, c:c + T], start=True, stop=True)
                    ins.then_inc(s["score"], 1)

            def transpose_prob(i, p):
                pe.wait_ge(s["norm"], i * 2 - 2 + p + 1)
                for which in range(2):
                    pos = position("pt", p)
                    free(pe, which, pos, i)
                    for j in range(4):
                        ins = nc.tensor.transpose(ring[which][pos % 2][:, P * j:P * j + P],
                                                  prob[p][:, P * (4 * which + j):P * (4 * which + j + 1)], ident[:, :])
                    ins.then_inc(s["pt_ps"], 1)

            def values(i, p):
                if p == 0:
                    pe.wait_ge(s["c_lo"], i)
                for n in range(4):
                    b, half, which = n // 2, n % 2, n % 2
                    pos = position("r", 4 * p + n - which)
                    free(pe, which, pos, i)
                    if n == 0:
                        pe.wait_ge(s["pt_lo"], i * 4 - 4 + 2 * p + 2)
                    out = ring[which][pos % 2][:, :]
                    hi, lo = (c[:, 2 * p + b, half, :] for c in (c_hi, c_lo))
                    nc.tensor.matmul(out, hi, pt_hi[p][:, :, T * b:T * b + T], start=True, stop=False)
                    nc.tensor.matmul(out, lo, pt_hi[p][:, :, T * b:T * b + T], start=False, stop=False)
                    nc.tensor.matmul(out, hi, pt_lo[p][:, :, T * b:T * b + T], start=False,
                                     stop=True).then_inc(s["r_ps"], 1)

            def output(i, part):
                if part == 0:
                    pe.wait_ge(s["r_lo"], i * 8)
                    if past(i, 1):
                        pe.wait_ge(s["yt"], i - 1)
                    if past(i, 2):
                        pe.wait_ge(s["logits"], i - 2)
                for h in range(H // 2 * part, H // 2 * (part + 1)):
                    nc.tensor.matmul(ps_y[:, 0:2 * P], n_hi[:, h, :], r_hi[:, h, :], start=(h == 0), stop=False)
                    nc.tensor.matmul(ps_y[:, 0:2 * P], n_lo[:, h, :], r_hi[:, h, :], start=False, stop=False)
                    ins = nc.tensor.matmul(ps_y[:, 0:2 * P], n_hi[:, h, :], r_lo[:, h, :], start=False, stop=(h == H - 1))
                if part:
                    ins.then_inc(s["y_ps"], 1)

            def transpose_x2(i):
                pe.wait_ge(s["x2"], i * 2 - 4)
                pe.wait_ge(s["yt"], min(i - 1, STEPS) if isinstance(i, int) else i - 1)
                for p in range(2):
                    ins = nc.tensor.transpose(ps_y[:, P * (2 + p):P * (3 + p)], y[:, p, :], ident[:, :])
                ins.then_inc(s["x2_ps"], 1)

            def gate_logits(i):
                pe.wait_ge(s["x2t"], i - 2)
                for p in range(2):
                    ins = nc.tensor.matmul(ps_y[:, 2 * P + E * p:2 * P + E * p + E], x2t[:, P * p:P * p + P], wg[:, :],
                                           start=True, stop=True)
                ins.then_inc(s["l_ps"], 1)

            def transpose_out(i):
                pe.wait_ge(s["yt"], i - 1)
                pe.wait_ge(s["xt"], i + 1 if not isinstance(i, int) else min(i + 1, STEPS))
                pe.wait_ge(s["ct_lo"], i + 1 if not isinstance(i, int) else min(i + 1, STEPS))
                if isinstance(i, int) and i >= STEPS:
                    pe.wait_ge(s["y"], i - 2)
                for p in range(2):
                    ins = nc.tensor.transpose(ps_t[:, P * p:P * p + P], yt[:, P * p:P * p + P], ident[:, :])
                ins.then_inc(s["yt_ps"], 1)

            def body(i):
                now, before, out, gates = spans(i)
                if before:
                    transpose_prob(i, 0)
                if now:
                    absorbed_keys(i, range(0, 2))
                if gates:
                    transpose_x2(i)
                if before:
                    values(i, 0)
                if now:
                    absorbed_keys(i, range(2, 4))
                if out:
                    transpose_out(i)
                if before:
                    transpose_prob(i, 1)
                if now:
                    absorbed_keys(i, range(4, 8))
                if gates:
                    gate_logits(i)
                if isinstance(i, int) and i == STEPS:
                    first_x2()
                if isinstance(i, int) and i == STEPS + 1:
                    early_weights()
                if before:
                    values(i, 1)
                if now:
                    scores(i, 0)
                if before:
                    output(i, 0)
                if now:
                    scores(i, 1)
                if has_next(i):
                    transpose_in(i + 1)
                if before:
                    output(i, 1)

            def first_x2():
                pe.wait_ge(s["xa"], TILES // 2)
                pe.wait_ge(s["shift"], STEPS * 2)
                for t in range(TILES):
                    ins = nc.tensor.transpose(ps_s[1][:, P * t:P * t + P], act[:, t, :], ident[:, :])
                ins.then_inc(s["x0_ps"], 1)

            def early_weights():
                pe.wait_ge(s["gates"], GATE_STEPS)
                for n in range(2):
                    rows = sel_rows[n]
                    ins = nc.tensor.transpose(ps_s[0][0:rows.stop - rows.start, P * n:P * n + P],
                                              flat(g["sel"][:, :, :])[:, rows], ident[:, :])
                ins.then_inc(s["wt_ps"], 1)

            transpose_in(0)
            pipeline(pe, body)

        @block.vector
        def _(dve):
            def normalise(i):
                if past(i, 0):
                    dve.wait_ge(s["t_ps"], i)
                for p in range(2):
                    nc.vector.tensor_scalar(xs[:, p, :].unsqueeze(1), act[:, ds(i * 2 + p, 1), :],
                                            mean[:, ds(i * 2 + p, 1)], rstd[:, ds(i * 2 + p, 1)],
                                            ALU.subtract, ALU.mult).then_inc(s["xs"], 1)
                dve.wait_ge(s["xs"], i * 2 + 2)
                nc.vector.tensor_scalar(act[:, ds(i * 2, 2), :], xs[:, :, :], 1.0, None, ALU.mult).then_inc(s["xn"], 1)

            def x2(i):
                dve.wait_ge(s["rstd"], i + 1)
                for p in range(2):
                    nc.vector.tensor_scalar(y[:, p, :], y[:, p, :], moments[:, p, 0:1], y_rstd[:, p:p + 1],
                                            ALU.subtract, ALU.mult).then_inc(s["x2"], 1)

            def softmax_in(i, p):
                for half in range(2):
                    dve.wait_ge(s["score"], i * 4 + 2 * p + half + 1)
                    nc.vector.tensor_reduce(top[:, p, 8 * half:8 * half + 8], heads(ps_s[half][:, :]), AX.X,
                                            ALU.max).then_inc(s["top"], 1)
                for half in range(2):
                    dve.wait_ge(s["top"], i * 4 + 2 * p + half + 1)
                    ins = nc.vector.tensor_tensor(heads(prob[p][:, 512 * half:512 * half + 512]),
                                                  heads(ps_s[half][:, :]),
                                                  over_keys(top[:, p, 8 * half:8 * half + 8]), ALU.subtract)
                ins.then_inc(s["shift"], 1)

            def softmax_sum(i, p):
                dve.wait_ge(s["exp"], i * 2 + p + 1)
                nc.vector.tensor_reduce(rsum[:, p, :], heads(prob[p][:, :]), AX.X, ALU.add).then_inc(s["sum"], 1)
                dve.wait_ge(s["sum"], i * 2 + p + 1)
                nc.vector.reciprocal(rsum[:, p, :], rsum[:, p, :]).then_inc(s["rsum"], 1)

            def transposed_prob(i, p):
                for which in range(2):
                    js = slice(4 * which, 4 * which + 4)
                    dve.wait_ge(s["pt_hi"], i * 4 - 4 + 2 * p + which + 1)
                    nc.vector.tensor_tensor(pt_lo[p][:, js, :].rearrange("p j q -> p (j q)"),
                                            ring[which][position("pt", p) % 2][:, :],
                                            pt_hi[p][:, js, :].rearrange("p j q -> p (j q)").bitcast(F32),
                                            ALU.subtract).then_inc(s["pt_lo"], 1)

            def values_low(i, p, ns):
                for n in ns:
                    b, half = n // 2, n % 2
                    bank = ring[half][position("r", 4 * p + n - half) % 2]
                    c = P * p + T * b
                    part = [r[:, :, c:c + T].rearrange("p (j h) q -> p j h q", h=2)[:, :, half, :] for r in (r_hi, r_lo)]
                    dve.wait_ge(s["r_hi"], i * 8 - 8 + 4 * p + n + 1)
                    nc.vector.tensor_tensor(part[1], bank[:, :].rearrange("p (j q) -> p j q", q=T),
                                            part[0].bitcast(F32), ALU.subtract).then_inc(s["r_lo"], 1)

            def keys_in(i, ns):
                for n in ns:
                    dve.wait_ge(s["g_ps"], i * 8 + 2 * n + 2)
                    if n == 0 and past(i, 0):
                        dve.wait_ge(s["score"], i * 4)
                    h = 4 * n + 2
                    nc.vector.tensor_tensor(keys[:, h:h + 2, :],
                                            ring[1][position("g", n) % 2][:, :].rearrange("p (h k) -> p h k", h=2),
                                            over_keys(b_vec[:, h:h + 2], 2 * P), ALU.add).then_inc(s["g_dve"], 1)

            def context_low(i):
                dve.wait_ge(s["ct_hi"], i + 1)
                nc.vector.tensor_tensor(ct_lo[:, :], ps_t[:, 2 * P:4 * P], ct_hi[:, :].bitcast(F32),
                                        ALU.subtract).then_inc(s["ct_lo"], 1)

            done = [0]

            def then(ins):
                done[0] += 1
                ins.then_inc(s["gates"], 1)
                dve.wait_ge(s["gates"], done[0])

            normalise(0)
            context_low(0)

            def body(i):
                now, before, out, gates = spans(i)
                if before:
                    transposed_prob(i, 0)
                if now:
                    keys_in(i, (0,))
                if before:
                    softmax_sum(i - 1, 1)
                    values_low(i, 0, range(4))
                if now:
                    keys_in(i, (1,))
                if out:
                    dve.wait_ge(s["yt_ps"], i - 1)
                    if past(i, 2):
                        dve.wait_ge(s["x2_ps"], i - 2)
                        dve.wait_ge(s["xa"], i - 2)
                    nc.vector.tensor_tensor(y[:, :, :], act[:, ds(i * 2 - 4, 2), :],
                                            ps_t[:, 0:2 * P].rearrange("p (i d) -> p i d", i=2),
                                            ALU.add).then_inc(s["y"], 1)
                if before:
                    transposed_prob(i, 1)
                if out:
                    dve.wait_ge(s["y"], i - 1)
                    for p in range(2):
                        nc.vector.bn_stats(y_stats[:, p, :], y[:, p, :]).then_inc(s["st"], 1)
                if now:
                    keys_in(i, (2, 3))
                if out:
                    dve.wait_ge(s["st"], i * 2 - 2)
                if before:
                    values_low(i, 1, (0,))
                if out:
                    for p in range(2):
                        nc.vector.bn_aggr(moments[:, p, :], y_stats[:, p, :]).then_inc(s["var"], 1)
                if isinstance(i, int) and i == STEPS + 2:
                    dve.wait_ge(s["wt_ps"], 1)
                    for n in range(2):
                        rows = slice(0, sel_rows[n].stop - sel_rows[n].start)
                        nc.vector.tensor_copy(g["wt"][rows, n, :], ps_s[0][rows, P * n:P * n + P]).then_inc(s["wt"], 1)
                if gates:
                    dve.wait_ge(s["l_ps"], i - 2)
                    nc.vector.tensor_scalar(g["gate"][:, ds(i * 2 - 6, 2), :],
                                            ps_y[:, 2 * P:2 * P + 2 * E].rearrange("p (t e) -> p t e", e=E), 1.0, None,
                                            ALU.mult).then_inc(s["logits"], 1)
                if isinstance(i, int) and i == STEPS + 1:
                    gate_weights(nc, then, g, early)
                if before:
                    values_low(i, 1, (1, 2, 3))
                if now:
                    softmax_in(i, 0)
                    if has_next(i):
                        normalise(i + 1)
                    softmax_sum(i, 0)
                    softmax_in(i, 1)
                if has_next(i):
                    context_low(i + 1)
                if out:
                    x2(i - 2)
                if isinstance(i, int) and i == STEPS:
                    dve.wait_ge(s["x0_hi"], 1)
                    nc.vector.tensor_tensor(x0_lo[:, :], ps_s[1][:, :], x0_hi[:, :].bitcast(F32),
                                            ALU.subtract).then_inc(s["x0_lo"], 1)
                    then(nc.vector.memset(g["keep"], 1.0))
                    then(nc.vector.memset(g["keep"][:, :, 0], 0.0))
                    dve.wait_ge(s["l_exp"], 1)
                    first_gates(nc, then, g, early)
                    second_gates(nc, then, g, early)

            pipeline(dve, body)

        @block.scalar
        def _(actv):
            def context_high(i):
                actv.wait_ge(s["t_ps"], i + 1)
                if past(i, 0):
                    actv.wait_ge(s["g_ps"], i * 8)
                nc.scalar.activation(ct_hi[:, :], ps_t[:, 2 * P:4 * P], ACT.Copy).then_inc(s["ct_hi"], 1)

            def exps(i, p):
                actv.wait_ge(s["shift"], i * 2 + p + 1)
                nc.scalar.activation(prob[p][:, :], prob[p][:, :], ACT.Exp).then_inc(s["exp"], 1)

            def transposed_prob(i, p):
                if past(i, 1):
                    actv.wait_ge(s["r_ps"], i * 8 - 16 + 4 * p + 4)
                for which in range(2):
                    actv.wait_ge(s["pt_ps"], i * 4 - 4 + 2 * p + which + 1)
                    nc.scalar.activation(pt_hi[p][:, 4 * which:4 * which + 4, :].rearrange("p j q -> p (j q)"),
                                         ring[which][position("pt", p) % 2][:, :], ACT.Copy).then_inc(s["pt_hi"], 1)

            def c_high(i):
                actv.wait_ge(cpad_in, i * 32 + 32)
                if past(i, 0):
                    actv.wait_ge(s["r_ps"], i * 8)
                nc.scalar.activation(c_hi[:, :, :, :], cpad[:, :, :, :], ACT.Copy).then_inc(s["c_hi"], 1)

            def values_high(i, p):
                for n in range(4):
                    b, half = n // 2, n % 2
                    bank = ring[half][position("r", 4 * p + n - half) % 2]
                    c = P * p + T * b
                    actv.wait_ge(s["r_ps"], i * 8 - 8 + 4 * p + n + 1)
                    nc.scalar.activation(r_hi[:, :, c:c + T].rearrange("p (j h) q -> p j h q", h=2)[:, :, half, :],
                                         bank[:, :].rearrange("p (j q) -> p j q", q=T), ACT.Copy).then_inc(s["r_hi"], 1)

            def keys_in(i, ns):
                for n in ns:
                    actv.wait_ge(s["g_ps"], i * 8 + 2 * n + 1)
                    for h in (4 * n, 4 * n + 1):
                        ins = nc.scalar.activation(keys[:, h, :],
                                                   ring[0][position("g", n) % 2][:, 256 * (h % 2):256 * (h % 2) + 256],
                                                   ACT.Identity, bias=b_vec[:, h:h + 1])
                    ins.then_inc(s["g_act"], 1)

            def body(i):
                now, before, out, gates = spans(i)
                if before:
                    transposed_prob(i, 0)
                if out:
                    actv.wait_ge(s["y_ps"], i - 1)
                    if past(i, 2):
                        actv.wait_ge(s["yt_ps"], i - 2)
                    nc.scalar.activation(yt[:, :], ps_y[:, 0:2 * P], ACT.Identity,
                                         bias=y_bias[:, 0:1]).then_inc(s["yt"], 1)
                if before:
                    exps(i - 1, 1)
                if now:
                    keys_in(i, (0,))
                    if past(i, 0):
                        actv.wait_ge(s["score"], i * 4)
                    actv.wait_ge(s["ct_lo"], i + 1)
                    nc.scalar.activation(xt[:, :, :], ps_t[:, 0:2 * P].rearrange("p (i d) -> p i d", i=2),
                                         ACT.Copy, bias=1.0).then_inc(s["xt"], 1)
                if before:
                    values_high(i, 0)
                if now:
                    keys_in(i, (1,))
                if gates:
                    actv.wait_ge(s["x2_ps"], i - 2)
                    nc.scalar.activation(x2t[:, :], ps_y[:, 2 * P:4 * P], ACT.Copy).then_inc(s["x2t"], 1)
                if before:
                    transposed_prob(i, 1)
                if now:
                    keys_in(i, (2, 3))
                if before:
                    values_high(i, 1)
                if isinstance(i, int) and i == STEPS:
                    actv.wait_ge(s["x0_ps"], 1)
                    nc.scalar.activation(x0_hi[:, :], ps_s[1][:, :], ACT.Copy).then_inc(s["x0_hi"], 1)
                    exp_logits(early)
                if now:
                    c_high(i)
                    exps(i, 0)
                if has_next(i):
                    context_high(i + 1)

            def exp_logits(tiles):
                actv.wait_ge(s["logits"], tiles.stop // 2)
                nc.scalar.activation(g["gate"][:, tiles, :], g["gate"][:, tiles, :], ACT.Exp,
                                     scale=-1.0).then_inc(s["l_exp"], 1)

            context_high(0)
            pipeline(actv, body)
            exp_logits(slice(EARLY, PAIRS))

        @block.gpsimd
        def _(pool):
            def norm(i, p):
                pool.wait_ge(s["rsum"], i * 2 + p + 1)
                nc.gpsimd.tensor_tensor(heads(prob[p][:, :]), heads(prob[p][:, :]), over_keys(rsum[:, p, :]),
                                        ALU.mult).then_inc(s["norm"], 1)

            def keep_x2(i):
                pool.wait_ge(s["x2"], i * 2 + 2)
                nc.gpsimd.tensor_tensor(act[:, ds(i * 2, 2), :], y[:, :, :],
                                        one[:, 0:2].unsqueeze(2).broadcast_to((P, 2, D)), ALU.mult).then_inc(s["xa"], 1)

            def c_low(i):
                pool.wait_ge(s["c_hi"], i + 1)
                nc.gpsimd.tensor_tensor(c_lo[:, :, :, :], cpad[:, :, :, :], c_hi[:, :, :, :].bitcast(F32),
                                        ALU.subtract).then_inc(s["c_lo"], 1)

            def y_scale(i):
                pool.wait_ge(s["var"], i * 2 + 2)
                nc.gpsimd.tensor_tensor(y_rstd[:, :], moments[:, :, 1], eps[:, 0:y_rstd.shape[1]],
                                        ALU.add).then_inc(s["eps"], 1)
                pool.wait_ge(s["eps"], i + 1)
                nc.gpsimd.tensor_tensor(y_rstd[:, :], y_rstd[:, :], power[:, 0:y_rstd.shape[1]],
                                        ALU.pow).then_inc(s["rstd"], 1)

            def cut(e):
                raw, hi, lo = w_raw[:, :, :].unsqueeze(2), w_hi[:, :, ds(e, 1), :], w_lo[:, :, ds(e, 1), :]
                pool.wait_ge(s["w_in"], e * 48 + 48)
                nc.gpsimd.tensor_tensor(hi, raw, one[:, 0:3].unsqueeze(2).unsqueeze(3).broadcast_to((P, 3, 1, FF)),
                                        ALU.mult).then_inc(s["w_hi"], 1)
                pool.wait_ge(s["w_hi"], e + 1)
                nc.gpsimd.tensor_tensor(lo, raw, hi.bitcast(F32), ALU.subtract).then_inc(s["w_lo"], 1)

            cut(0)

            def body(i, cutting=False):
                if not isinstance(i, int) or i >= 2:
                    y_scale(i - 2)
                if not isinstance(i, int) or i < STEPS:
                    c_low(i)
                    norm(i, 0)
                if not isinstance(i, int) or i >= 2:
                    keep_x2(i - 2)
                if not isinstance(i, int) or i < STEPS:
                    norm(i, 1)
                if cutting:
                    cut(i + 1)

            for i in range(2):
                body(i, True)
            with pool.Fori(2, E) as i:
                body(i, True)
            with pool.Fori(E, STEPS) as i:
                body(i)
            for i in range(STEPS, STEPS + 2):
                body(i)


def flat(ap):
    return ap.rearrange("p t e -> p (t e)")


def gate_tensors(sb):
    g = {n: sb("gate_" + n, [P, PAIRS, E]) for n in ("gate", "sel")}
    g.update({n: sb("gate_" + n, [P, PAIRS]) for n in ("best", "total")})
    g["wt"] = sb("gate_wt", [P, 3, P])
    return g


SCRATCH = ("pick", "count", "rest", "keep")


def choose_largest(nc, then, g, r, source, chosen):
    best = over_keys(g["best"][:, r], E)
    then(nc.vector.tensor_reduce(g["best"][:, r], source[:, r, :], AX.X, ALU.max))
    then(nc.vector.tensor_tensor(chosen[:, r, :], source[:, r, :], best, ALU.is_equal))
    then(nc.vector.tensor_tensor_scan(flat(g["count"][:, r, :]), flat(g["keep"][:, r, :]), flat(chosen[:, r, :]), 0.0,
                                      ALU.mult, ALU.add))
    then(nc.vector.scalar_tensor_tensor(out=flat(chosen[:, r, :]), in0=flat(g["count"][:, r, :]), scalar=1.0,
                                        in1=flat(chosen[:, r, :]), op0=ALU.is_equal, op1=ALU.mult))


def store_weights(sp, wt_dram, g, n, rows, wt_stored):
    sp.dma_start(wt_dram.rearrange("t e k -> (t e) k")[rows, :], g["wt"][0:rows.stop - rows.start, n, :])\
      .then_inc(wt_stored, 16)


def first_gates(nc, then, g, r):
    gate, sel, rest = (flat(g[n][:, r, :]) for n in ("gate", "sel", "rest"))
    then(nc.vector.tensor_scalar(gate, gate, 1.0, None, ALU.add))
    then(nc.vector.reciprocal(gate, gate))
    choose_largest(nc, then, g, r, g["gate"], g["sel"])
    then(nc.vector.scalar_tensor_tensor(out=rest, in0=sel, scalar=-4.0, in1=gate,
                                        op0=ALU.mult, op1=ALU.add))


def second_gates(nc, then, g, r):
    choose_largest(nc, then, g, r, g["rest"], g["pick"])


def gate_weights(nc, then, g, r):
    gate, sel, pick = (flat(g[n][:, r, :]) for n in ("gate", "sel", "pick"))
    total = g["total"][:, r]
    then(nc.vector.tensor_tensor(sel, sel, pick, ALU.add))
    then(nc.vector.tensor_tensor(sel, sel, gate, ALU.mult))
    then(nc.vector.tensor_reduce(total, g["sel"][:, r, :], AX.X, ALU.add))
    then(nc.vector.reciprocal(total, total))
    then(nc.vector.tensor_tensor(g["sel"][:, r, :], g["sel"][:, r, :], over_keys(total, E), ALU.mult))


def experts(nc, sem, sb, ps, act, ident, power, eps, w1, w3, w2, g, x0_hi, x0_lo, wt_dram, wt_stored, out):
    LAG, KEEP = 3, 6
    late, late_rows = slice(EARLY, PAIRS), slice(EARLY * E, PAIRS * E)
    g = {**g, **{n: sb("ff_" + n, [P, PAIRS, E]) for n in SCRATCH}}
    xs = sb("ff_xs", [P, TILES, D])
    x_hi, x_lo = (sb(n, [P, GROUPS - 1, TILES * P], F32R) for n in ("ff_x_hi", "ff_x_lo"))
    gated = sb("ff_gated", [P, 2, TILES * P])
    hidden = sb("ff_hidden", [P, 3, TILES * P])
    h_hi, h_lo = sb("ff_h_hi", [P, KEEP, TILES * P], F32R), sb("ff_h_lo", [P, KEEP, TILES * P], F32R)
    gates = sb("ff_gates", [P, E, TILES * P])
    yt = sb("ff_yt", [P, TILES * P])
    y = sb("ff_y", [P, TILES, D])
    y_stats, moments = sb("ff_y_stats", [P, TILES, 6]), sb("ff_moments", [P, TILES, 2])
    y_rstd = sb("ff_y_rstd", [P, TILES])
    ps_1, ps_3, ps_y, ps_t, ps_x, ps_w = ps[0:2], ps[2:4], ps[4], ps[5], ps[6], ps[7]
    s = {n: sem("ff_" + n) for n in ("u1", "u3", "silu", "mul", "gate", "hi", "lo", "down", "y_ps", "yt", "yt_ps",
                                     "y", "st", "var", "eps", "rstd", "x3", "stored", "xs",
                                     "xt_ps", "x_hi", "x_lo", "gates", "wt_ps", "wt")}
    gate_in = [sem(f"ff_gate_in{e}") for e in range(E)]
    OUT_AT = 5
    IN_AT = 13
    LATE_AT = 9

    def whole(pe_like, body, tail):
        body(0, True)
        with pe_like.Fori(1, GROUPS - 1) as i:
            body(i, False)
        body(GROUPS - 1, False)
        tail()

    def has_next(i):
        return not isinstance(i, int) or i + 1 < GROUPS

    with nc.Block() as block:

        @block.sync
        def _(sp):
            def load(i, e):
                src = wt_dram[ds(i * TILES, TILES), e, :].unsqueeze(0).broadcast_to((P, TILES, P))
                sp.dma_start(gates[:, e, :].rearrange("p (t k) -> p t k", t=TILES), src).then_inc(gate_in[e], 16)

            def store(i):
                sp.wait_ge(s["x3"], i * TILES + TILES)
                sp.dma_start(out[:, ds(i * TILES, TILES), :], y[:, :, :]).then_inc(s["stored"], 16)

            sp.wait_ge(wt_stored, 32)
            for e in range(E):
                load(0, e)
            sp.wait_ge(s["wt"], 1)
            store_weights(sp, wt_dram, g, 2, late_rows, wt_stored)
            sp.wait_ge(wt_stored, 48)
            with sp.Fori(1, GROUPS) as i:
                for e in range(E):
                    sp.wait_ge(s["gate"], i * 2 * E - 2 * E + 2 * e + 2)
                    load(i, e)
                store(i - 1)
            store(GROUPS - 1)
            sp.wait_ge(s["stored"], 16 * GROUPS)

        @block.tensor
        def _(pe):
            def up(i, u):
                e, c = u // 2, u % 2
                cols = slice(FF * e + P * c, FF * e + P * c + P)
                n = i * UNITS + u
                for which, (w, bank, mark) in enumerate(((w1, ps_1[u % 2], "u1"), (w3, ps_3[u % 2], "u3"))):
                    if u >= 2 or not isinstance(i, int) or i:
                        pe.wait_ge(s[("silu", "mul")[which]], n - 1)
                    if isinstance(i, int) and i == 0:
                        x_h, x_l = x0_hi[:, :].unsqueeze(1), x0_lo[:, :].unsqueeze(1)
                    else:
                        x_h, x_l = x_hi[:, ds(i - 1, 1), :], x_lo[:, ds(i - 1, 1), :]
                    out = bank[:, :].unsqueeze(1)
                    nc.tensor.matmul(out, w[0][:, cols], x_h, start=True, stop=False)
                    nc.tensor.matmul(out, w[1][:, cols], x_h, start=False, stop=False)
                    nc.tensor.matmul(out, w[0][:, cols], x_l, start=False, stop=True).then_inc(s[mark], 1)

            def transpose_in(i):
                pe.wait_ge(s["xs"], i)
                if not isinstance(i, int) or i > 1:
                    pe.wait_ge(s["x_lo"], i - 1)
                for t in range(TILES):
                    ins = nc.tensor.transpose(ps_x[:, P * t:P * t + P], xs[:, t, :], ident[:, :])
                ins.then_inc(s["xt_ps"], 1)

            def late_weights():
                pe.wait_ge(s["gates"], GATE_STEPS)
                nc.tensor.transpose(ps_w[0:TILES * E, 0:P], flat(g["sel"][:, late, :]),
                                    ident[:, :]).then_inc(s["wt_ps"], 1)

            def down(i, u, first):
                n = i * UNITS + u
                pe.wait_ge(s["lo"], n + 1)
                if u == 0 and not first:
                    pe.wait_ge(s["yt"], i)
                c = slice(D * u, D * u + D)
                k = u % KEEP
                nc.tensor.matmul(ps_y[:, :], w2[0][:, c], h_hi[:, k, :], start=(u == 0), stop=False)
                nc.tensor.matmul(ps_y[:, :], w2[1][:, c], h_hi[:, k, :], start=False, stop=False)
                ins = nc.tensor.matmul(ps_y[:, :], w2[0][:, c], h_lo[:, k, :], start=False, stop=(u == UNITS - 1))
                ins.then_inc(s["down"], 1)

            def out(count):
                pe.wait_ge(s["yt"], count)
                for t in range(TILES):
                    ins = nc.tensor.transpose(ps_t[:, P * t:P * t + P], yt[:, P * t:P * t + P], ident[:, :])
                ins.then_inc(s["yt_ps"], 1)

            def body(i, first):
                if not first:
                    pe.wait_ge(s["x_lo"], i)
                for u in range(UNITS):
                    up(i, u)
                    if u == IN_AT and has_next(i):
                        transpose_in(i + 1)
                    if u == LATE_AT and first:
                        late_weights()
                    if u >= LAG:
                        down(i, u - LAG, first)
                    elif not first:
                        down(i - 1, u - LAG + UNITS, True)
                    if u == OUT_AT and not first:
                        out(i)

            def tail():
                for u in range(UNITS - LAG, UNITS):
                    down(GROUPS - 1, u, True)
                out(GROUPS)

            whole(pe, body, tail)

        @block.scalar
        def _(actv):
            def high(i, u):
                n = i * UNITS + u
                actv.wait_ge(s["mul"], n + 1)
                if u >= 2:
                    actv.wait_ge(s["gate"], i * 2 * E + u - 1)
                if u >= KEEP or not isinstance(i, int) or i:
                    actv.wait_ge(s["down"], n - KEEP + 1)
                nc.scalar.activation(h_hi[:, u % KEEP, :], hidden[:, u % 3, :], ACT.Copy).then_inc(s["hi"], 1)

            def x_high(i):
                actv.wait_ge(s["xt_ps"], i)
                nc.scalar.activation(x_hi[:, ds(i - 1, 1), :], ps_x[:, :].unsqueeze(1), ACT.Copy).then_inc(s["x_hi"], 1)

            def output(count):
                actv.wait_ge(s["down"], count * UNITS)
                nc.scalar.activation(yt[:, :], ps_y[:, :], ACT.Copy, scale=1.0 / 3.0).then_inc(s["yt"], 1)

            def body(i, first):
                for u in range(UNITS):
                    n = i * UNITS + u
                    actv.wait_ge(s["u1"], n + 1)
                    if u >= 2 or not first:
                        actv.wait_ge(s["mul"], n - 1)
                    nc.scalar.activation(gated[:, u % 2, :], ps_1[u % 2][:, :], ACT.Silu).then_inc(s["silu"], 1)
                    if u >= 2:
                        high(i, u - 2)
                    elif not first:
                        high(i - 1, u - 2 + UNITS)
                    if u == LAG - 1 and not first:
                        output(i)
                    if u == IN_AT + 1 and has_next(i):
                        x_high(i + 1)

            def tail():
                for u in range(UNITS - 2, UNITS):
                    high(GROUPS - 1, u)
                output(GROUPS)

            actv.preload_act_table(ACT.Silu)
            whole(actv, body, tail)

        @block.vector
        def _(dve):
            def low(i, u):
                n = i * UNITS + u
                dve.wait_ge(s["hi"], n + 1)
                nc.vector.tensor_tensor(h_lo[:, u % KEEP, :], hidden[:, u % 3, :], h_hi[:, u % KEEP, :].bitcast(F32),
                                        ALU.subtract).then_inc(s["lo"], 1)

            def add_out(i):
                dve.wait_ge(s["yt_ps"], i + 1)
                nc.vector.tensor_tensor(y[:, :, :], act[:, ds(i * TILES, TILES), :],
                                        ps_t[:, :].rearrange("p (t d) -> p t d", t=TILES), ALU.add).then_inc(s["y"], 1)

            def statistics(i):
                dve.wait_ge(s["y"], i + 1)
                for t in range(TILES):
                    nc.vector.bn_stats(y_stats[:, t, :], y[:, t, :]).then_inc(s["st"], 1)

            def variance(i):
                for t in range(TILES):
                    nc.vector.bn_aggr(moments[:, t, :], y_stats[:, t, :]).then_inc(s["var"], 1)

            def x3(i):
                dve.wait_ge(s["rstd"], i + 1)
                for t in range(TILES):
                    nc.vector.tensor_scalar(y[:, t, :], y[:, t, :], moments[:, t, 0:1], y_rstd[:, t:t + 1],
                                            ALU.subtract, ALU.mult).then_inc(s["x3"], 1)

            def fixed(i):
                if not isinstance(i, int) or i > 1:
                    dve.wait_ge(s["xt_ps"], i - 1)
                nc.vector.tensor_scalar(xs[:, :, :], act[:, ds(i * TILES, TILES), :], 1.0, None,
                                        ALU.mult).then_inc(s["xs"], 1)

            def x_low(i):
                dve.wait_ge(s["x_hi"], i)
                nc.vector.tensor_tensor(x_lo[:, ds(i - 1, 1), :], ps_x[:, :].unsqueeze(1),
                                        x_hi[:, ds(i - 1, 1), :].bitcast(F32), ALU.subtract).then_inc(s["x_lo"], 1)

            done = [0]

            def then(ins):
                done[0] += 1
                ins.then_inc(s["gates"], 1)
                dve.wait_ge(s["gates"], done[0])

            late_gates = {3: first_gates, 5: second_gates, 7: gate_weights}
            after_up = {OUT_AT + 1: add_out, OUT_AT + 2: statistics, OUT_AT + 3: variance, OUT_AT + 6: x3}

            def body(i, first):
                for u in range(UNITS):
                    n = i * UNITS + u
                    dve.wait_ge(s["silu"], n + 1)
                    dve.wait_ge(s["u3"], n + 1)
                    if u >= 3 or not first:
                        dve.wait_ge(s["lo"], n - 2)
                    if u == OUT_AT + 3 and not first:
                        dve.wait_ge(s["st"], i * TILES)
                    nc.vector.tensor_tensor(hidden[:, u % 3, :], gated[:, u % 2, :], ps_3[u % 2][:, :],
                                            ALU.mult).then_inc(s["mul"], 1)
                    if u >= 2:
                        low(i, u - 2)
                    elif not first:
                        low(i - 1, u - 2 + UNITS)
                    if u == UNITS - 1 and not first:
                        dve.wait_ge(s["stored"], i * 16)
                    if u in after_up and not first:
                        after_up[u](i - 1)
                    if u == IN_AT - 1 and has_next(i):
                        fixed(i + 1)
                    if u == IN_AT + 1 and has_next(i):
                        x_low(i + 1)
                    if first and u in late_gates:
                        late_gates[u](nc, then, g, late)
                    if first and u == LATE_AT + 1:
                        dve.wait_ge(s["wt_ps"], 1)
                        nc.vector.tensor_copy(g["wt"][0:TILES * E, 2, :], ps_w[0:TILES * E, 0:P]).then_inc(s["wt"], 1)

            def tail():
                for u in range(UNITS - 2, UNITS):
                    low(GROUPS - 1, u)
                add_out(GROUPS - 1)
                statistics(GROUPS - 1)
                dve.wait_ge(s["st"], GROUPS * TILES)
                variance(GROUPS - 1)
                x3(GROUPS - 1)

            then(nc.vector.memset(g["keep"][:, :, :], 1.0))
            then(nc.vector.memset(g["keep"][:, :, 0], 0.0))
            whole(dve, body, tail)

        @block.gpsimd
        def _(pool):
            def y_scale(i):
                pool.wait_ge(s["var"], i * TILES + TILES)
                nc.gpsimd.tensor_tensor(y_rstd[:, :], moments[:, :, 1], eps[:, 0:y_rstd.shape[1]],
                                        ALU.add).then_inc(s["eps"], 1)
                pool.wait_ge(s["eps"], i + 1)
                nc.gpsimd.tensor_tensor(y_rstd[:, :], y_rstd[:, :], power[:, 0:y_rstd.shape[1]],
                                        ALU.pow).then_inc(s["rstd"], 1)

            def body(i, first):
                for u in range(2, UNITS):
                    e = u // 2 - 1
                    if u == OUT_AT + 5 and not first:
                        y_scale(i - 1)
                    if u % 2 == 0:
                        pool.wait_ge(gate_in[e], i * 16 + 16)
                    pool.wait_ge(s["mul"], i * UNITS + u + 1)
                    nc.gpsimd.tensor_tensor(hidden[:, u % 3, :], hidden[:, u % 3, :], gates[:, e, :],
                                            ALU.mult).then_inc(s["gate"], 1)

            whole(pool, body, lambda: y_scale(GROUPS - 1))


def decoder_layer(nc, i, out, wt_dram):
    with ExitStack() as whole:
        def allocator(ctx):
            return lambda name, shape, dt=F32: ctx.enter_context(nc.sbuf_tensor(name, shape, dt))

        def sem(name):
            return whole.enter_context(nc.semaphore(name))

        sb = allocator(whole)
        g = gate_tensors(sb)
        x0_hi, x0_lo = (sb(n, [P, TILES * P], F32R) for n in ("x0_hi", "x0_lo"))
        ps = [whole.enter_context(nc.psum_tensor(f"bank{n}", [P, 512], F32)) for n in range(8)]
        act = sb("act", [P, PAIRS, D])
        stats = sb("stats", [P, PAIRS, 6])
        mean, var, rstd, power = (sb(n, [P, PAIRS]) for n in ("mean", "var", "rstd", "power"))
        eps, one = sb("eps", [P, TILES]), sb("one", [P, TILES])
        ident = sb("ident", [P, P])
        wg = sb("wg", [P, E])
        ff_hi, ff_lo = (sb(n, [P, 3, (E + 1) * FF], F32R) for n in ("ff_hi", "ff_lo"))
        x, out = (a.rearrange("(i b) t d -> (b t) i d", b=2) for a in (i["x"], out))
        sa_w_in, x_in, x_rest, ab_b_in, wt_stored, cn_in, cpad_in, cpad_zero = (
            sem(n) for n in ("sa_w_in", "x_in", "x_rest", "ab_b_in", "wt_stored", "cn_in", "cpad_in", "cpad_zero"))
        ab_w_in = [sem(f"ab_w_in{n}") for n in range(4)]

        with ExitStack() as before_experts:
            sb2 = allocator(before_experts)
            a_hi, a_lo, n_hi, n_lo = (sb2(n, [P, H, P], F32R) for n in ("a_hi", "a_lo", "n_hi", "n_lo"))
            b_vec, y_bias = sb2("b_vec", [P, H]), sb2("y_bias", [P, 1])
            cn = sb2("ca_cn", [P, 2, D])
            cpad = sb2("ca_cpad", [P, 4, 2, D])

            with ExitStack() as before_cross:
                sb0 = allocator(before_cross)
                raw = [sb0("raw_" + n, [P, H * HK]) for n in ("Wq", "Wk", "Wv")]
                wu = sb0("Wu", [P, H // 2, D])
                bq, bk, bv = (sb0(n, [P, H // 2]) for n in ("bq", "bk", "bv"))
                bu = sb0("bu", [P, 1])

                with ExitStack() as phase:
                    sb1 = allocator(phase)
                    wqkv, wout = sb1("sa_wqkv", [P, 3 * D]), sb1("sa_wout", [P, D])
                    table = sb1("table", [P, H, T])
                    quad_scale, head_mask = sb1("quad_scale", [P, 4]), sb1("head_mask", [P, 4])
                    parity = sb1("parity", [P, 2])
                    rel_i, rel, mask16 = sb1("rel_i", [P, T], I32), sb1("rel", [P, T]), sb1("mask16", [P, H])

                    def load_first(sp):
                        sp.dma_start(act[:, 0:FIRST_PAIRS, :], x[:, 0:FIRST_PAIRS, :]).then_inc(x_in, 16)
                        sp.dma_start(wqkv[:, :], i["L0_attn_Wqkv"]).then_inc(sa_w_in, 16)
                        sp.dma_start(wout[:, :], i["L0_attn_Wout"]).then_inc(sa_w_in, 16)
                        sp.dma_start(act[:, FIRST_PAIRS:, :], x[:, FIRST_PAIRS:, :]).then_inc(x_rest, 16)

                    def load_rest(sp):
                        for n, name in enumerate(("Wq", "Wk", "Wv")):
                            sp.dma_start(raw[n][:, :], i["L0_xattn_" + name]).then_inc(ab_w_in[n], 16)
                        sp.dma_start(wu[:, :, :], i["L0_xattn_Wu"].rearrange("(j p) n -> p j n", p=P))\
                          .then_inc(ab_w_in[3], 16)
                        for t, name in ((bq, "bq"), (bk, "bk"), (bv, "bv")):
                            sp.dma_start(t[:, :], i["L0_xattn_" + name]).then_inc(ab_b_in, 16)
                        sp.dma_start(bu[:, :], i["L0_xattn_bu"].rearrange("(p a) -> p a", a=1)).then_inc(ab_b_in, 16)
                        sp.dma_start(wg[:, :], i["L0_ffn_Wg"]).then_inc(ab_b_in, 16)

                    constants(nc, sem, load_first, ident, table, quad_scale, head_mask, parity, rel_i, rel, mask16, power, eps,
                              one)
                    self_attention(nc, sem, sb1, ps, load_rest, wqkv, wout, sa_w_in, x_in, x_rest, act, stats, ident, table,
                                   quad_scale, head_mask, parity)

                def zero_cpad():
                    nc.gpsimd.memset(cpad[:, :, :, :], 0.0).then_inc(cpad_zero, 1)

                def first_context(sp):
                    load_cn(nc, sp, i["ctx_1024"], cn, cn_in, 0)
                    sp.wait_ge(cpad_zero, 1)
                    load_cpad(nc, sp, i["ctx_1024"], cpad, cpad_in, 0)

                with ExitStack() as inner:
                    absorb_weights(nc, sem, allocator(inner), ps, raw, wu, bq, bk, bv, bu, ab_w_in, ab_b_in, ident,
                                   a_hi, a_lo, b_vec, n_hi, n_lo, y_bias, stats, mean, var, rstd, power,
                                   zero_cpad, first_context)
            cross_attention(nc, sem, sb2, ps, i["ctx_1024"], cn, cpad, cn_in, cpad_in, act, mean, rstd, ident,
                            a_hi, a_lo, b_vec, n_hi, n_lo, y_bias, power, eps, one, {n: i["L0_ffn_" + n] for n in (
                                "Ws1", "Ws3", "Ws2", "We1", "We3", "We2")}, ff_hi, ff_lo,
                            wg, g, x0_hi, x0_lo, wt_dram, wt_stored)

        with ExitStack() as phase:
            sb3 = allocator(phase)
            w1, w3, w2 = ((ff_hi[:, n, :], ff_lo[:, n, :]) for n in range(3))
            experts(nc, sem, sb3, ps, act, ident, power, eps, w1, w3, w2, g, x0_hi, x0_lo, wt_dram, wt_stored, out)


_INS = ["x", "ctx_1024", "L0_attn_Wqkv", "L0_attn_Wout", "L0_xattn_Wq", "L0_xattn_bq", "L0_xattn_Wk", "L0_xattn_bk",
        "L0_xattn_Wv", "L0_xattn_bv", "L0_xattn_Wu", "L0_xattn_bu", "L0_ffn_Wg", "L0_ffn_Ws1", "L0_ffn_Ws3",
        "L0_ffn_Ws2", "L0_ffn_We1", "L0_ffn_We3", "L0_ffn_We2"]


def kernel(**inputs):
    import concourse.bacc as bacc
    from concourse.bass_utils import run_bass_kernel_spmd

    nc = bacc.Bacc("TRN2", target_bir_lowering=False, num_devices=1)
    arrays, aps = {}, {}
    for name in _INS:
        a = np.asarray(inputs[name])
        if name.endswith(("bq", "bk", "bv")):
            a = a.reshape(-1, P).T
        a = np.ascontiguousarray(a)
        arrays[f"in_{name}"] = a
        aps[name] = nc.dram_tensor(f"in_{name}", a.shape, mybir.dt.from_np(a.dtype), kind="ExternalInput").ap()
    out = nc.dram_tensor("out", (B, T, D), F32, kind="ExternalOutput").ap()
    wt_dram = nc.dram_tensor("gate_weights", (PAIRS, E, P), F32, kind="Internal").ap()
    decoder_layer(nc, aps, out, wt_dram)
    result = run_bass_kernel_spmd(nc, [arrays], core_ids=[0])
    return result.results[0]["out"]
```
